# Optimizing a Trainium2 kernel written in Bass

```python
import numpy as np
import jax
import jax.numpy as jnp

def _softmax(x, axis=-1):
    return jax.nn.softmax(x, axis=axis)

def _gelu(x):
    return jax.nn.gelu(x, approximate=True)

def _silu(x):
    return jax.nn.silu(x)

def _sigmoid(x):
    return jax.nn.sigmoid(x)

def _layernorm(x, axis=-1, eps=1e-05):
    m = jnp.mean(x, axis=axis, keepdims=True)
    v = jnp.var(x, axis=axis, keepdims=True)
    return (x - m) / jnp.sqrt(v + eps)

def _scatter_add(tgt, idx, src, axis=0):
    return tgt.at[idx].add(src)

def _segment_sum(src, seg, n):
    return jax.ops.segment_sum(src, seg, n)
kernel_name = 'mk_xattn_seq_d4_seqx_r4_e0c585'

def setup_inputs(seed: int=0):
    np.random.seed(seed)
    _w = jnp.asarray

    def _rec_inputs():
        import jax
        import jax.numpy as jnp
        _rk = jax.random.key(seed)
        x = 7.22e-05 + 1 * jax.random.normal(jax.random.fold_in(_rk, 1), (8, 256, 256), jnp.float32)
        _lenS = 256 - jax.random.randint(jax.random.fold_in(_rk, 7), (8,), 0, max(1, 256 // 4) + 1, jnp.int32)
        _lenS2 = 256 - jax.random.randint(jax.random.fold_in(_rk, 8), (8,), 0, max(1, 256 // 4) + 1, jnp.int32)
        _ctx_1024P = jax.random.normal(jax.random.fold_in(_rk, 11), (8, 16, 256), jnp.float32)
        _ctx_1024c = jax.random.dirichlet(jax.random.fold_in(_rk, 511), 0.3 * jnp.ones((16,), jnp.float32), (8, 256))
        _ctx_1024t = jnp.einsum('bsk,bkd->bsd', _ctx_1024c, _ctx_1024P)
        _ctx_1024t = _ctx_1024t * jax.lax.rsqrt(jnp.mean(jnp.square(_ctx_1024t)) + 1e-12) * 0.953939
        ctx_1024 = 4.13588e-05 + 0.999923 * (_ctx_1024t + 0.3 * jax.random.normal(jax.random.fold_in(_rk, 611), (8, 256, 256), jnp.float32))
        _validS = jnp.arange(256)[None, :] < _lenS[:, None]
        _validS2 = jnp.arange(256)[None, :] < _lenS2[:, None]
        _causal = jnp.tril(jnp.ones((256, 256), dtype=bool))
        mask_Bx1x1xS2_if1 = jnp.where(jnp.ones((8, 1, 1, 256), dtype=bool), 1, 0).astype(jnp.int32)
        mask_Bx1xSxS2_if1 = jnp.where(jnp.ones((8, 1, 256, 256), dtype=bool), 1, 0).astype(jnp.int32)
        return (x, ctx_1024, mask_Bx1x1xS2_if1, mask_Bx1xSxS2_if1)
    x, ctx_1024, mask_Bx1x1xS2_if1, mask_Bx1xSxS2_if1 = _rec_inputs()

    def _L0_xattn_setup():
        import jax, jax.numpy as jnp
        import numpy as np
        D_MODEL = 256
        NUM_HEADS = 16
        D_FF = 1024
        D_K = D_MODEL // NUM_HEADS
        LN_EPS = 1e-05

        def _linear(x, w, b):
            return jnp.einsum('bsd,od->bso', x, w) + b

        def _layernorm(x, g, b):
            mu = jnp.mean(x, axis=-1, keepdims=True)
            var = jnp.mean(jnp.square(x - mu), axis=-1, keepdims=True)
            return (x - mu) * jax.lax.rsqrt(var + LN_EPS) * g + b

        def _mha(q_in, kv_in, mask, wq, bq, wk, bk, wv, bv, wo, bo):
            B, Sq, _ = q_in.shape
            Sk = kv_in.shape[1]
            q = _linear(q_in, wq, bq).reshape(B, Sq, NUM_HEADS, D_K).transpose(0, 2, 1, 3)
            k = _linear(kv_in, wk, bk).reshape(B, Sk, NUM_HEADS, D_K).transpose(0, 2, 1, 3)
            v = _linear(kv_in, wv, bv).reshape(B, Sk, NUM_HEADS, D_K).transpose(0, 2, 1, 3)
            scores = jnp.einsum('bhqd,bhkd->bhqk', q, k) / jnp.sqrt(jnp.asarray(D_K, q.dtype))
            scores = jnp.where(mask == 0, jnp.asarray(-1000000000.0, scores.dtype), scores)
            attn = jax.nn.softmax(scores, axis=-1)
            out = jnp.einsum('bhqk,bhkd->bhqd', attn, v)
            out = out.transpose(0, 2, 1, 3).reshape(B, Sq, D_MODEL)
            return _linear(out, wo, bo)
        key = jax.random.key(seed)
        ks = jax.random.split(key, 24)
        B, S = (4, 512)
        s = 0.02
        d = {'tgt': jax.random.normal(ks[0], (B, S, D_MODEL), jnp.float32), 'enc_output': jax.random.normal(ks[1], (B, S, D_MODEL), jnp.float32), 'src_mask': jnp.ones((B, 1, 1, S), jnp.int32), 'tgt_mask': jnp.ones((B, 1, S, S), jnp.int32)}
        names = ['sa_wq', 'sa_wk', 'sa_wv', 'sa_wo', 'ca_wq', 'ca_wk', 'ca_wv', 'ca_wo']
        for i, n in enumerate(names):
            d[n] = jax.random.normal(ks[2 + i], (D_MODEL, D_MODEL), jnp.float32) * s
            d[n.replace('w', 'b')] = jnp.zeros((D_MODEL,), jnp.float32)
        d['ffn_w1'] = jax.random.normal(ks[10], (D_FF, D_MODEL), jnp.float32) * s
        d['ffn_b1'] = jnp.zeros((D_FF,), jnp.float32)
        d['ffn_w2'] = jax.random.normal(ks[11], (D_MODEL, D_FF), jnp.float32) * s
        d['ffn_b2'] = jnp.zeros((D_MODEL,), jnp.float32)
        for i in (1, 2, 3):
            d[f'ln{i}_g'] = jnp.ones((D_MODEL,), jnp.float32)
            d[f'ln{i}_b'] = jnp.zeros((D_MODEL,), jnp.float32)
        return d
    _L0_xattn_all = _L0_xattn_setup()
    _L0_xattn_in = {k: v for k, v in _L0_xattn_all.items() if k in ('sa_wq', 'sa_bq', 'sa_wk', 'sa_bk', 'sa_wv', 'sa_bv', 'sa_wo', 'sa_bo', 'ca_wq', 'ca_bq', 'ca_wk', 'ca_bk', 'ca_wv', 'ca_bv', 'ca_wo', 'ca_bo', 'ffn_w1', 'ffn_b1', 'ffn_w2', 'ffn_b2', 'ln1_g', 'ln1_b', 'ln2_g', 'ln2_b', 'ln3_g', 'ln3_b')}
    del _L0_xattn_all

    def _L1_xattn_setup():
        import jax, jax.numpy as jnp
        import numpy as np
        N, L, C, NHEAD = (4, 512, 256, 8)
        D = C // NHEAD
        EPS_ATTN = 1e-06
        EPS_LN = 1e-05

        def _w(key, shape, scale=0.02):
            return jax.random.normal(key, shape, dtype=jnp.float32) * scale

        def layernorm(x, g, b):
            m = jnp.mean(x, axis=-1, keepdims=True)
            v = jnp.mean(jnp.square(x - m), axis=-1, keepdims=True)
            return (x - m) * jax.lax.rsqrt(v + EPS_LN) * g + b

        def linear_attention(q, k, v):
            Q = jax.nn.elu(q) + 1.0
            K = jax.nn.elu(k) + 1.0
            vlen = v.shape[1]
            v = v / vlen
            KV = jnp.einsum('nshd,nshv->nhdv', K, v)
            Z = 1.0 / (jnp.einsum('nlhd,nhd->nlh', Q, K.sum(axis=1)) + EPS_ATTN)
            out = jnp.einsum('nlhd,nhdv,nlh->nlhv', Q, KV, Z) * vlen
            return out

        def heads(x):
            n, l, c = x.shape
            return x.reshape(n, l, NHEAD, D)

        def encoder_layer(x, wq, wk, wv, wm, w1, w2, g1, b1, g2, b2):
            n, l, c = x.shape
            msg = linear_attention(heads(x @ wq), heads(x @ wk), heads(x @ wv))
            msg = msg.reshape(n, l, c) @ wm
            x = x + layernorm(msg, g1, b1)
            x = x + layernorm(jax.nn.relu(x @ w1) @ w2, g2, b2)
            return x

        def decoder_layer(x, src, wq0, wk0, wv0, wm0, wq1, wk1, wv1, wm1, w1, w2, g0, b0, g1, b1, g2, b2):
            n, l, c = x.shape
            msg = linear_attention(heads(x @ wq0), heads(x @ wk0), heads(x @ wv0))
            msg = msg.reshape(n, l, c) @ wm0
            x = x + layernorm(msg, g0, b0)
            msg = linear_attention(heads(x @ wq1), heads(src @ wk1), heads(src @ wv1))
            msg = msg.reshape(n, l, c) @ wm1
            x = x + layernorm(msg, g1, b1)
            x = x + layernorm(jax.nn.relu(x @ w1) @ w2, g2, b2)
            return x
        key = jax.random.key(seed)
        ks = jax.random.split(key, 32)
        inp = {'depth_feat': jax.random.normal(ks[0], (N, L, C), dtype=jnp.float32), 'context_feat': jax.random.normal(ks[1], (N, L, C), dtype=jnp.float32), 'depth_pos': jax.random.normal(ks[2], (N, L, C), dtype=jnp.float32), 'e_wq': _w(ks[3], (C, C)), 'e_wk': _w(ks[4], (C, C)), 'e_wv': _w(ks[5], (C, C)), 'e_wm': _w(ks[6], (C, C)), 'e_w1': _w(ks[7], (C, 2 * C)), 'e_w2': _w(ks[8], (2 * C, C)), 'e_g1': jnp.ones((C,), jnp.float32), 'e_b1': jnp.zeros((C,), jnp.float32), 'e_g2': jnp.ones((C,), jnp.float32), 'e_b2': jnp.zeros((C,), jnp.float32), 'd_wq0': _w(ks[9], (C, C)), 'd_wk0': _w(ks[10], (C, C)), 'd_wv0': _w(ks[11], (C, C)), 'd_wm0': _w(ks[12], (C, C)), 'd_wq1': _w(ks[13], (C, C)), 'd_wk1': _w(ks[14], (C, C)), 'd_wv1': _w(ks[15], (C, C)), 'd_wm1': _w(ks[16], (C, C)), 'd_w1': _w(ks[17], (C, 2 * C)), 'd_w2': _w(ks[18], (2 * C, C)), 'd_g0': jnp.ones((C,), jnp.float32), 'd_b0': jnp.zeros((C,), jnp.float32), 'd_g1': jnp.ones((C,), jnp.float32), 'd_b1': jnp.zeros((C,), jnp.float32), 'd_g2': jnp.ones((C,), jnp.float32), 'd_b2': jnp.zeros((C,), jnp.float32)}
        return inp
    _L1_xattn_all = _L1_xattn_setup()
    _L1_xattn_in = {k: v for k, v in _L1_xattn_all.items() if k in ('e_wq', 'e_wk', 'e_wv', 'e_wm', 'e_w1', 'e_w2', 'e_g1', 'e_b1', 'e_g2', 'e_b2', 'd_wq0', 'd_wk0', 'd_wv0', 'd_wm0', 'd_wq1', 'd_wk1', 'd_wv1', 'd_wm1', 'd_w1', 'd_w2', 'd_g0', 'd_b0', 'd_g1', 'd_b1', 'd_g2', 'd_b2')}
    del _L1_xattn_all

    def _L2_xattn_setup():
        import jax, jax.numpy as jnp
        import numpy as np
        D, H, E, K, DFF = (256, 16, 8, 2, 1024)
        B, L, T = (4, 128, 512)
        EPS = 1e-05

        def _xavier(key, shape):
            fan_in, fan_out = (shape[-1], shape[-2])
            a = jnp.sqrt(6.0 / (fan_in + fan_out))
            return jax.random.uniform(key, shape, jnp.float32, -a, a)

        def _ln(x, g, b):
            m = x.mean(-1, keepdims=True)
            v = ((x - m) ** 2).mean(-1, keepdims=True)
            return (x - m) / jnp.sqrt(v + EPS) * g + b

        def _mha(q_in, kv_in, in_w, in_b, out_w, out_b):
            wq, wk, wv = jnp.split(in_w, 3, axis=0)
            bq, bk, bv = jnp.split(in_b, 3, axis=0)
            dh = D // H

            def heads(x, w, b):
                y = x @ w.T + b
                return y.reshape(x.shape[0], x.shape[1], H, dh).transpose(0, 2, 1, 3)
            q = heads(q_in, wq, bq)
            k = heads(kv_in, wk, bk)
            v = heads(kv_in, wv, bv)
            scores = jnp.einsum('bhqd,bhkd->bhqk', q, k) / jnp.sqrt(jnp.float32(dh))
            attn = jax.nn.softmax(scores, axis=-1)
            out = jnp.einsum('bhqk,bhkd->bhqd', attn, v)
            out = out.transpose(0, 2, 1, 3).reshape(q_in.shape[0], q_in.shape[1], D)
            return out @ out_w.T + out_b

        def _fuse_moe(x, ln_g, ln_b, rw, rb, fc1_w, fc1_b, fc2_w, fc2_b):
            h = _ln(x, ln_g, ln_b)
            logits = h @ rw.T + rb
            vals, idx = jax.lax.top_k(logits, K)
            gates = jax.nn.softmax(vals, axis=-1)
            N = x.shape[0] * x.shape[1]
            hf = h.reshape(N, D)
            h1 = jax.nn.gelu(jnp.einsum('nd,efd->enf', hf, fc1_w) + fc1_b[:, None, :], approximate=False)
            eo = jnp.einsum('enf,edf->end', h1, fc2_w) + fc2_b[:, None, :]
            idx_f = idx.reshape(N, K)
            gates_f = gates.reshape(N, K)
            gathered = eo[idx_f, jnp.arange(N)[:, None], :]
            mixed = (gathered * gates_f[..., None]).sum(axis=1).reshape(x.shape)
            return x + mixed
        key = jax.random.key(seed)
        ks = jax.random.split(key, 16)
        inp = {'latents': jax.random.normal(ks[0], (B, L, D), jnp.float32), 'tokens': jax.random.normal(ks[1], (B, T, D), jnp.float32), 'sa_ln_g': jnp.ones((D,)), 'sa_ln_b': jnp.zeros((D,)), 'sa_in_w': _xavier(ks[2], (3 * D, D)), 'sa_in_b': jnp.zeros((3 * D,)), 'sa_out_w': _xavier(ks[3], (D, D)), 'sa_out_b': jnp.zeros((D,)), 'ca_q_ln_g': jnp.ones((D,)), 'ca_q_ln_b': jnp.zeros((D,)), 'ca_kv_ln_g': jnp.ones((D,)), 'ca_kv_ln_b': jnp.zeros((D,)), 'ca_in_w': _xavier(ks[4], (3 * D, D)), 'ca_in_b': jnp.zeros((3 * D,)), 'ca_out_w': _xavier(ks[5], (D, D)), 'ca_out_b': jnp.zeros((D,)), 'moe_ln_g': jnp.ones((D,)), 'moe_ln_b': jnp.zeros((D,)), 'router_w': _xavier(ks[6], (E, D)), 'router_b': jnp.zeros((E,)), 'e_fc1_w': jax.vmap(lambda k: _xavier(k, (DFF, D)))(jax.random.split(ks[7], E)), 'e_fc1_b': jnp.zeros((E, DFF)), 'e_fc2_w': jax.vmap(lambda k: _xavier(k, (D, DFF)))(jax.random.split(ks[8], E)), 'e_fc2_b': jnp.zeros((E, D))}
        return inp
    _L2_xattn_all = _L2_xattn_setup()
    _L2_xattn_in = {k: v for k, v in _L2_xattn_all.items() if k in ('sa_ln_g', 'sa_ln_b', 'sa_in_w', 'sa_in_b', 'sa_out_w', 'sa_out_b', 'ca_q_ln_g', 'ca_q_ln_b', 'ca_kv_ln_g', 'ca_kv_ln_b', 'ca_in_w', 'ca_in_b', 'ca_out_w', 'ca_out_b', 'moe_ln_g', 'moe_ln_b', 'router_w', 'router_b', 'e_fc1_w', 'e_fc1_b', 'e_fc2_w', 'e_fc2_b')}
    del _L2_xattn_all

    def _L3_xattn_setup():
        import jax, jax.numpy as jnp
        import numpy as np
        D_MODEL = 256
        N_HEAD = 16
        DK = D_MODEL // N_HEAD
        LN_EPS = 1e-05

        def _layernorm(x, g, b):
            mu = jnp.mean(x, axis=-1, keepdims=True)
            var = jnp.mean(jnp.square(x - mu), axis=-1, keepdims=True)
            return (x - mu) * jax.lax.rsqrt(var + LN_EPS) * g + b

        def _attn(x_q, x_kv, wq, bq, wk, bk, wv, bv, wo, bo, causal):
            B, Tq, D = x_q.shape
            Tk = x_kv.shape[1]
            Q = (x_q @ wq + bq).reshape(B, Tq, N_HEAD, DK)
            K = (x_kv @ wk + bk).reshape(B, Tk, N_HEAD, DK)
            V = (x_kv @ wv + bv).reshape(B, Tk, N_HEAD, DK)
            scores = jnp.einsum('bqhd,bkhd->bhqk', Q, K) / jnp.sqrt(jnp.float32(DK)).astype(x_q.dtype)
            if causal:
                mask = jnp.tril(jnp.ones((Tq, Tk), dtype=bool))
                scores = jnp.where(mask, scores, jnp.finfo(scores.dtype).min)
            a = jax.nn.softmax(scores, axis=-1)
            out = jnp.einsum('bhqk,bkhd->bqhd', a, V).reshape(B, Tq, D)
            return out @ wo + bo
        key = jax.random.key(seed)
        ks = iter(jax.random.split(key, 32))
        s = 1.0 / np.sqrt(D_MODEL)

        def lin(k, din, dout):
            return jax.random.uniform(k, (din, dout), jnp.float32, -1, 1) / np.sqrt(din)
        inp = {'x': jax.random.normal(next(ks), (2, 512, D_MODEL), jnp.float32), 'x_en': jax.random.normal(next(ks), (2, 512, D_MODEL), jnp.float32)}
        for pre in ('mmha', 'mha'):
            for nm in ('wq', 'wk', 'wv', 'wo'):
                inp[f'{pre}_{nm}'] = lin(next(ks), D_MODEL, D_MODEL)
                inp[f'{pre}_{nm}_b'] = jnp.zeros((D_MODEL,), jnp.float32)
        for i in (1, 2, 3):
            inp[f'ln{i}_g'] = jnp.ones((D_MODEL,), jnp.float32)
            inp[f'ln{i}_b'] = jnp.zeros((D_MODEL,), jnp.float32)
        inp['ffn_w1'] = lin(next(ks), D_MODEL, 4 * D_MODEL)
        inp['ffn_b1'] = jnp.zeros((4 * D_MODEL,), jnp.float32)
        inp['ffn_w2'] = lin(next(ks), 4 * D_MODEL, D_MODEL)
        inp['ffn_b2'] = jnp.zeros((D_MODEL,), jnp.float32)
        return inp
    _L3_xattn_all = _L3_xattn_setup()
    _L3_xattn_in = {k: v for k, v in _L3_xattn_all.items() if k in ('mmha_wq', 'mmha_wq_b', 'mmha_wk', 'mmha_wk_b', 'mmha_wv', 'mmha_wv_b', 'mmha_wo', 'mmha_wo_b', 'mha_wq', 'mha_wq_b', 'mha_wk', 'mha_wk_b', 'mha_wv', 'mha_wv_b', 'mha_wo', 'mha_wo_b', 'ln1_g', 'ln1_b', 'ln2_g', 'ln2_b', 'ln3_g', 'ln3_b', 'ffn_w1', 'ffn_b1', 'ffn_w2', 'ffn_b2')}
    del _L3_xattn_all
    return {'x': x, 'ctx_1024': ctx_1024, 'mask_Bx1x1xS2_if1': mask_Bx1x1xS2_if1, 'mask_Bx1xSxS2_if1': mask_Bx1xSxS2_if1, 'L0_xattn_sa_wq': _L0_xattn_in['sa_wq'], 'L0_xattn_sa_bq': _L0_xattn_in['sa_bq'], 'L0_xattn_sa_wk': _L0_xattn_in['sa_wk'], 'L0_xattn_sa_bk': _L0_xattn_in['sa_bk'], 'L0_xattn_sa_wv': _L0_xattn_in['sa_wv'], 'L0_xattn_sa_bv': _L0_xattn_in['sa_bv'], 'L0_xattn_sa_wo': _L0_xattn_in['sa_wo'], 'L0_xattn_sa_bo': _L0_xattn_in['sa_bo'], 'L0_xattn_ca_wq': _L0_xattn_in['ca_wq'], 'L0_xattn_ca_bq': _L0_xattn_in['ca_bq'], 'L0_xattn_ca_wk': _L0_xattn_in['ca_wk'], 'L0_xattn_ca_bk': _L0_xattn_in['ca_bk'], 'L0_xattn_ca_wv': _L0_xattn_in['ca_wv'], 'L0_xattn_ca_bv': _L0_xattn_in['ca_bv'], 'L0_xattn_ca_wo': _L0_xattn_in['ca_wo'], 'L0_xattn_ca_bo': _L0_xattn_in['ca_bo'], 'L0_xattn_ffn_w1': _L0_xattn_in['ffn_w1'], 'L0_xattn_ffn_b1': _L0_xattn_in['ffn_b1'], 'L0_xattn_ffn_w2': _L0_xattn_in['ffn_w2'], 'L0_xattn_ffn_b2': _L0_xattn_in['ffn_b2'], 'L0_xattn_ln1_g': _L0_xattn_in['ln1_g'], 'L0_xattn_ln1_b': _L0_xattn_in['ln1_b'], 'L0_xattn_ln2_g': _L0_xattn_in['ln2_g'], 'L0_xattn_ln2_b': _L0_xattn_in['ln2_b'], 'L0_xattn_ln3_g': _L0_xattn_in['ln3_g'], 'L0_xattn_ln3_b': _L0_xattn_in['ln3_b'], 'L1_xattn_e_wq': _L1_xattn_in['e_wq'], 'L1_xattn_e_wk': _L1_xattn_in['e_wk'], 'L1_xattn_e_wv': _L1_xattn_in['e_wv'], 'L1_xattn_e_wm': _L1_xattn_in['e_wm'], 'L1_xattn_e_w1': _L1_xattn_in['e_w1'], 'L1_xattn_e_w2': _L1_xattn_in['e_w2'], 'L1_xattn_e_g1': _L1_xattn_in['e_g1'], 'L1_xattn_e_b1': _L1_xattn_in['e_b1'], 'L1_xattn_e_g2': _L1_xattn_in['e_g2'], 'L1_xattn_e_b2': _L1_xattn_in['e_b2'], 'L1_xattn_d_wq0': _L1_xattn_in['d_wq0'], 'L1_xattn_d_wk0': _L1_xattn_in['d_wk0'], 'L1_xattn_d_wv0': _L1_xattn_in['d_wv0'], 'L1_xattn_d_wm0': _L1_xattn_in['d_wm0'], 'L1_xattn_d_wq1': _L1_xattn_in['d_wq1'], 'L1_xattn_d_wk1': _L1_xattn_in['d_wk1'], 'L1_xattn_d_wv1': _L1_xattn_in['d_wv1'], 'L1_xattn_d_wm1': _L1_xattn_in['d_wm1'], 'L1_xattn_d_w1': _L1_xattn_in['d_w1'], 'L1_xattn_d_w2': _L1_xattn_in['d_w2'], 'L1_xattn_d_g0': _L1_xattn_in['d_g0'], 'L1_xattn_d_b0': _L1_xattn_in['d_b0'], 'L1_xattn_d_g1': _L1_xattn_in['d_g1'], 'L1_xattn_d_b1': _L1_xattn_in['d_b1'], 'L1_xattn_d_g2': _L1_xattn_in['d_g2'], 'L1_xattn_d_b2': _L1_xattn_in['d_b2'], 'L2_xattn_sa_ln_g': _L2_xattn_in['sa_ln_g'], 'L2_xattn_sa_ln_b': _L2_xattn_in['sa_ln_b'], 'L2_xattn_sa_in_w': _L2_xattn_in['sa_in_w'], 'L2_xattn_sa_in_b': _L2_xattn_in['sa_in_b'], 'L2_xattn_sa_out_w': _L2_xattn_in['sa_out_w'], 'L2_xattn_sa_out_b': _L2_xattn_in['sa_out_b'], 'L2_xattn_ca_q_ln_g': _L2_xattn_in['ca_q_ln_g'], 'L2_xattn_ca_q_ln_b': _L2_xattn_in['ca_q_ln_b'], 'L2_xattn_ca_kv_ln_g': _L2_xattn_in['ca_kv_ln_g'], 'L2_xattn_ca_kv_ln_b': _L2_xattn_in['ca_kv_ln_b'], 'L2_xattn_ca_in_w': _L2_xattn_in['ca_in_w'], 'L2_xattn_ca_in_b': _L2_xattn_in['ca_in_b'], 'L2_xattn_ca_out_w': _L2_xattn_in['ca_out_w'], 'L2_xattn_ca_out_b': _L2_xattn_in['ca_out_b'], 'L2_xattn_moe_ln_g': _L2_xattn_in['moe_ln_g'], 'L2_xattn_moe_ln_b': _L2_xattn_in['moe_ln_b'], 'L2_xattn_router_w': _L2_xattn_in['router_w'], 'L2_xattn_router_b': _L2_xattn_in['router_b'], 'L2_xattn_e_fc1_w': _L2_xattn_in['e_fc1_w'], 'L2_xattn_e_fc1_b': _L2_xattn_in['e_fc1_b'], 'L2_xattn_e_fc2_w': _L2_xattn_in['e_fc2_w'], 'L2_xattn_e_fc2_b': _L2_xattn_in['e_fc2_b'], 'L3_xattn_mmha_wq': _L3_xattn_in['mmha_wq'], 'L3_xattn_mmha_wq_b': _L3_xattn_in['mmha_wq_b'], 'L3_xattn_mmha_wk': _L3_xattn_in['mmha_wk'], 'L3_xattn_mmha_wk_b': _L3_xattn_in['mmha_wk_b'], 'L3_xattn_mmha_wv': _L3_xattn_in['mmha_wv'], 'L3_xattn_mmha_wv_b': _L3_xattn_in['mmha_wv_b'], 'L3_xattn_mmha_wo': _L3_xattn_in['mmha_wo'], 'L3_xattn_mmha_wo_b': _L3_xattn_in['mmha_wo_b'], 'L3_xattn_mha_wq': _L3_xattn_in['mha_wq'], 'L3_xattn_mha_wq_b': _L3_xattn_in['mha_wq_b'], 'L3_xattn_mha_wk': _L3_xattn_in['mha_wk'], 'L3_xattn_mha_wk_b': _L3_xattn_in['mha_wk_b'], 'L3_xattn_mha_wv': _L3_xattn_in['mha_wv'], 'L3_xattn_mha_wv_b': _L3_xattn_in['mha_wv_b'], 'L3_xattn_mha_wo': _L3_xattn_in['mha_wo'], 'L3_xattn_mha_wo_b': _L3_xattn_in['mha_wo_b'], 'L3_xattn_ln1_g': _L3_xattn_in['ln1_g'], 'L3_xattn_ln1_b': _L3_xattn_in['ln1_b'], 'L3_xattn_ln2_g': _L3_xattn_in['ln2_g'], 'L3_xattn_ln2_b': _L3_xattn_in['ln2_b'], 'L3_xattn_ln3_g': _L3_xattn_in['ln3_g'], 'L3_xattn_ln3_b': _L3_xattn_in['ln3_b'], 'L3_xattn_ffn_w1': _L3_xattn_in['ffn_w1'], 'L3_xattn_ffn_b1': _L3_xattn_in['ffn_b1'], 'L3_xattn_ffn_w2': _L3_xattn_in['ffn_w2'], 'L3_xattn_ffn_b2': _L3_xattn_in['ffn_b2']}

def reference(x, ctx_1024, mask_Bx1x1xS2_if1, mask_Bx1xSxS2_if1, L0_xattn_sa_wq, L0_xattn_sa_bq, L0_xattn_sa_wk, L0_xattn_sa_bk, L0_xattn_sa_wv, L0_xattn_sa_bv, L0_xattn_sa_wo, L0_xattn_sa_bo, L0_xattn_ca_wq, L0_xattn_ca_bq, L0_xattn_ca_wk, L0_xattn_ca_bk, L0_xattn_ca_wv, L0_xattn_ca_bv, L0_xattn_ca_wo, L0_xattn_ca_bo, L0_xattn_ffn_w1, L0_xattn_ffn_b1, L0_xattn_ffn_w2, L0_xattn_ffn_b2, L0_xattn_ln1_g, L0_xattn_ln1_b, L0_xattn_ln2_g, L0_xattn_ln2_b, L0_xattn_ln3_g, L0_xattn_ln3_b, L1_xattn_e_wq, L1_xattn_e_wk, L1_xattn_e_wv, L1_xattn_e_wm, L1_xattn_e_w1, L1_xattn_e_w2, L1_xattn_e_g1, L1_xattn_e_b1, L1_xattn_e_g2, L1_xattn_e_b2, L1_xattn_d_wq0, L1_xattn_d_wk0, L1_xattn_d_wv0, L1_xattn_d_wm0, L1_xattn_d_wq1, L1_xattn_d_wk1, L1_xattn_d_wv1, L1_xattn_d_wm1, L1_xattn_d_w1, L1_xattn_d_w2, L1_xattn_d_g0, L1_xattn_d_b0, L1_xattn_d_g1, L1_xattn_d_b1, L1_xattn_d_g2, L1_xattn_d_b2, L2_xattn_sa_ln_g, L2_xattn_sa_ln_b, L2_xattn_sa_in_w, L2_xattn_sa_in_b, L2_xattn_sa_out_w, L2_xattn_sa_out_b, L2_xattn_ca_q_ln_g, L2_xattn_ca_q_ln_b, L2_xattn_ca_kv_ln_g, L2_xattn_ca_kv_ln_b, L2_xattn_ca_in_w, L2_xattn_ca_in_b, L2_xattn_ca_out_w, L2_xattn_ca_out_b, L2_xattn_moe_ln_g, L2_xattn_moe_ln_b, L2_xattn_router_w, L2_xattn_router_b, L2_xattn_e_fc1_w, L2_xattn_e_fc1_b, L2_xattn_e_fc2_w, L2_xattn_e_fc2_b, L3_xattn_mmha_wq, L3_xattn_mmha_wq_b, L3_xattn_mmha_wk, L3_xattn_mmha_wk_b, L3_xattn_mmha_wv, L3_xattn_mmha_wv_b, L3_xattn_mmha_wo, L3_xattn_mmha_wo_b, L3_xattn_mha_wq, L3_xattn_mha_wq_b, L3_xattn_mha_wk, L3_xattn_mha_wk_b, L3_xattn_mha_wv, L3_xattn_mha_wv_b, L3_xattn_mha_wo, L3_xattn_mha_wo_b, L3_xattn_ln1_g, L3_xattn_ln1_b, L3_xattn_ln2_g, L3_xattn_ln2_b, L3_xattn_ln3_g, L3_xattn_ln3_b, L3_xattn_ffn_w1, L3_xattn_ffn_b1, L3_xattn_ffn_w2, L3_xattn_ffn_b2):
    import jax
    import jax.numpy as jnp

    def _L0_xattn_ref(tgt, enc_output, src_mask, tgt_mask, sa_wq, sa_bq, sa_wk, sa_bk, sa_wv, sa_bv, sa_wo, sa_bo, ca_wq, ca_bq, ca_wk, ca_bk, ca_wv, ca_bv, ca_wo, ca_bo, ffn_w1, ffn_b1, ffn_w2, ffn_b2, ln1_g, ln1_b, ln2_g, ln2_b, ln3_g, ln3_b):
        import jax, jax.numpy as jnp
        import numpy as np
        D_MODEL = 256
        NUM_HEADS = 16
        D_FF = 1024
        D_K = D_MODEL // NUM_HEADS
        LN_EPS = 1e-05

        def _linear(x, w, b):
            return jnp.einsum('bsd,od->bso', x, w) + b

        def _layernorm(x, g, b):
            mu = jnp.mean(x, axis=-1, keepdims=True)
            var = jnp.mean(jnp.square(x - mu), axis=-1, keepdims=True)
            return (x - mu) * jax.lax.rsqrt(var + LN_EPS) * g + b

        def _mha(q_in, kv_in, mask, wq, bq, wk, bk, wv, bv, wo, bo):
            B, Sq, _ = q_in.shape
            Sk = kv_in.shape[1]
            q = _linear(q_in, wq, bq).reshape(B, Sq, NUM_HEADS, D_K).transpose(0, 2, 1, 3)
            k = _linear(kv_in, wk, bk).reshape(B, Sk, NUM_HEADS, D_K).transpose(0, 2, 1, 3)
            v = _linear(kv_in, wv, bv).reshape(B, Sk, NUM_HEADS, D_K).transpose(0, 2, 1, 3)
            scores = jnp.einsum('bhqd,bhkd->bhqk', q, k) / jnp.sqrt(jnp.asarray(D_K, q.dtype))
            scores = jnp.where(mask == 0, jnp.asarray(-1000000000.0, scores.dtype), scores)
            attn = jax.nn.softmax(scores, axis=-1)
            out = jnp.einsum('bhqk,bhkd->bhqd', attn, v)
            out = out.transpose(0, 2, 1, 3).reshape(B, Sq, D_MODEL)
            return _linear(out, wo, bo)
        t2 = _mha(tgt, tgt, tgt_mask, sa_wq, sa_bq, sa_wk, sa_bk, sa_wv, sa_bv, sa_wo, sa_bo)
        x = _layernorm(tgt + t2, ln1_g, ln1_b)
        t2 = _mha(x, enc_output, src_mask, ca_wq, ca_bq, ca_wk, ca_bk, ca_wv, ca_bv, ca_wo, ca_bo)
        x = _layernorm(x + t2, ln2_g, ln2_b)
        t2 = _linear(jax.nn.relu(_linear(x, ffn_w1, ffn_b1)), ffn_w2, ffn_b2)
        return _layernorm(x + t2, ln3_g, ln3_b)

    def _L1_xattn_ref(depth_feat, context_feat, depth_pos, e_wq, e_wk, e_wv, e_wm, e_w1, e_w2, e_g1, e_b1, e_g2, e_b2, d_wq0, d_wk0, d_wv0, d_wm0, d_wq1, d_wk1, d_wv1, d_wm1, d_w1, d_w2, d_g0, d_b0, d_g1, d_b1, d_g2, d_b2):
        import jax, jax.numpy as jnp
        import numpy as np
        N, L, C, NHEAD = (4, 512, 256, 8)
        D = C // NHEAD
        EPS_ATTN = 1e-06
        EPS_LN = 1e-05

        def _w(key, shape, scale=0.02):
            return jax.random.normal(key, shape, dtype=jnp.float32) * scale

        def layernorm(x, g, b):
            m = jnp.mean(x, axis=-1, keepdims=True)
            v = jnp.mean(jnp.square(x - m), axis=-1, keepdims=True)
            return (x - m) * jax.lax.rsqrt(v + EPS_LN) * g + b

        def linear_attention(q, k, v):
            Q = jax.nn.elu(q) + 1.0
            K = jax.nn.elu(k) + 1.0
            vlen = v.shape[1]
            v = v / vlen
            KV = jnp.einsum('nshd,nshv->nhdv', K, v)
            Z = 1.0 / (jnp.einsum('nlhd,nhd->nlh', Q, K.sum(axis=1)) + EPS_ATTN)
            out = jnp.einsum('nlhd,nhdv,nlh->nlhv', Q, KV, Z) * vlen
            return out

        def heads(x):
            n, l, c = x.shape
            return x.reshape(n, l, NHEAD, D)

        def encoder_layer(x, wq, wk, wv, wm, w1, w2, g1, b1, g2, b2):
            n, l, c = x.shape
            msg = linear_attention(heads(x @ wq), heads(x @ wk), heads(x @ wv))
            msg = msg.reshape(n, l, c) @ wm
            x = x + layernorm(msg, g1, b1)
            x = x + layernorm(jax.nn.relu(x @ w1) @ w2, g2, b2)
            return x

        def decoder_layer(x, src, wq0, wk0, wv0, wm0, wq1, wk1, wv1, wm1, w1, w2, g0, b0, g1, b1, g2, b2):
            n, l, c = x.shape
            msg = linear_attention(heads(x @ wq0), heads(x @ wk0), heads(x @ wv0))
            msg = msg.reshape(n, l, c) @ wm0
            x = x + layernorm(msg, g0, b0)
            msg = linear_attention(heads(x @ wq1), heads(src @ wk1), heads(src @ wv1))
            msg = msg.reshape(n, l, c) @ wm1
            x = x + layernorm(msg, g1, b1)
            x = x + layernorm(jax.nn.relu(x @ w1) @ w2, g2, b2)
            return x
        ctx = context_feat + depth_pos
        ctx = encoder_layer(ctx, e_wq, e_wk, e_wv, e_wm, e_w1, e_w2, e_g1, e_b1, e_g2, e_b2)
        out = decoder_layer(depth_feat, ctx, d_wq0, d_wk0, d_wv0, d_wm0, d_wq1, d_wk1, d_wv1, d_wm1, d_w1, d_w2, d_g0, d_b0, d_g1, d_b1, d_g2, d_b2)
        return out

    def _L2_xattn_ref(latents, tokens, sa_ln_g, sa_ln_b, sa_in_w, sa_in_b, sa_out_w, sa_out_b, ca_q_ln_g, ca_q_ln_b, ca_kv_ln_g, ca_kv_ln_b, ca_in_w, ca_in_b, ca_out_w, ca_out_b, moe_ln_g, moe_ln_b, router_w, router_b, e_fc1_w, e_fc1_b, e_fc2_w, e_fc2_b):
        import jax, jax.numpy as jnp
        import numpy as np
        D, H, E, K, DFF = (256, 16, 8, 2, 1024)
        B, L, T = (4, 128, 512)
        EPS = 1e-05

        def _xavier(key, shape):
            fan_in, fan_out = (shape[-1], shape[-2])
            a = jnp.sqrt(6.0 / (fan_in + fan_out))
            return jax.random.uniform(key, shape, jnp.float32, -a, a)

        def _ln(x, g, b):
            m = x.mean(-1, keepdims=True)
            v = ((x - m) ** 2).mean(-1, keepdims=True)
            return (x - m) / jnp.sqrt(v + EPS) * g + b

        def _mha(q_in, kv_in, in_w, in_b, out_w, out_b):
            wq, wk, wv = jnp.split(in_w, 3, axis=0)
            bq, bk, bv = jnp.split(in_b, 3, axis=0)
            dh = D // H

            def heads(x, w, b):
                y = x @ w.T + b
                return y.reshape(x.shape[0], x.shape[1], H, dh).transpose(0, 2, 1, 3)
            q = heads(q_in, wq, bq)
            k = heads(kv_in, wk, bk)
            v = heads(kv_in, wv, bv)
            scores = jnp.einsum('bhqd,bhkd->bhqk', q, k) / jnp.sqrt(jnp.float32(dh))
            attn = jax.nn.softmax(scores, axis=-1)
            out = jnp.einsum('bhqk,bhkd->bhqd', attn, v)
            out = out.transpose(0, 2, 1, 3).reshape(q_in.shape[0], q_in.shape[1], D)
            return out @ out_w.T + out_b

        def _fuse_moe(x, ln_g, ln_b, rw, rb, fc1_w, fc1_b, fc2_w, fc2_b):
            h = _ln(x, ln_g, ln_b)
            logits = h @ rw.T + rb
            vals, idx = jax.lax.top_k(logits, K)
            gates = jax.nn.softmax(vals, axis=-1)
            N = x.shape[0] * x.shape[1]
            hf = h.reshape(N, D)
            h1 = jax.nn.gelu(jnp.einsum('nd,efd->enf', hf, fc1_w) + fc1_b[:, None, :], approximate=False)
            eo = jnp.einsum('enf,edf->end', h1, fc2_w) + fc2_b[:, None, :]
            idx_f = idx.reshape(N, K)
            gates_f = gates.reshape(N, K)
            gathered = eo[idx_f, jnp.arange(N)[:, None], :]
            mixed = (gathered * gates_f[..., None]).sum(axis=1).reshape(x.shape)
            return x + mixed
        q = _ln(latents, sa_ln_g, sa_ln_b)
        x = latents + _mha(q, q, sa_in_w, sa_in_b, sa_out_w, sa_out_b)
        qc = _ln(x, ca_q_ln_g, ca_q_ln_b)
        kv = _ln(tokens, ca_kv_ln_g, ca_kv_ln_b)
        x = x + _mha(qc, kv, ca_in_w, ca_in_b, ca_out_w, ca_out_b)
        return _fuse_moe(x, moe_ln_g, moe_ln_b, router_w, router_b, e_fc1_w, e_fc1_b, e_fc2_w, e_fc2_b)

    def _L3_xattn_ref(x, x_en, mmha_wq, mmha_wq_b, mmha_wk, mmha_wk_b, mmha_wv, mmha_wv_b, mmha_wo, mmha_wo_b, mha_wq, mha_wq_b, mha_wk, mha_wk_b, mha_wv, mha_wv_b, mha_wo, mha_wo_b, ln1_g, ln1_b, ln2_g, ln2_b, ln3_g, ln3_b, ffn_w1, ffn_b1, ffn_w2, ffn_b2):
        import jax, jax.numpy as jnp
        import numpy as np
        D_MODEL = 256
        N_HEAD = 16
        DK = D_MODEL // N_HEAD
        LN_EPS = 1e-05

        def _layernorm(x, g, b):
            mu = jnp.mean(x, axis=-1, keepdims=True)
            var = jnp.mean(jnp.square(x - mu), axis=-1, keepdims=True)
            return (x - mu) * jax.lax.rsqrt(var + LN_EPS) * g + b

        def _attn(x_q, x_kv, wq, bq, wk, bk, wv, bv, wo, bo, causal):
            B, Tq, D = x_q.shape
            Tk = x_kv.shape[1]
            Q = (x_q @ wq + bq).reshape(B, Tq, N_HEAD, DK)
            K = (x_kv @ wk + bk).reshape(B, Tk, N_HEAD, DK)
            V = (x_kv @ wv + bv).reshape(B, Tk, N_HEAD, DK)
            scores = jnp.einsum('bqhd,bkhd->bhqk', Q, K) / jnp.sqrt(jnp.float32(DK)).astype(x_q.dtype)
            if causal:
                mask = jnp.tril(jnp.ones((Tq, Tk), dtype=bool))
                scores = jnp.where(mask, scores, jnp.finfo(scores.dtype).min)
            a = jax.nn.softmax(scores, axis=-1)
            out = jnp.einsum('bhqk,bkhd->bqhd', a, V).reshape(B, Tq, D)
            return out @ wo + bo
        h = _layernorm(x, ln1_g, ln1_b)
        x = x + _attn(h, h, mmha_wq, mmha_wq_b, mmha_wk, mmha_wk_b, mmha_wv, mmha_wv_b, mmha_wo, mmha_wo_b, causal=True)
        h = _layernorm(x, ln2_g, ln2_b)
        x = x + _attn(h, x_en, mha_wq, mha_wq_b, mha_wk, mha_wk_b, mha_wv, mha_wv_b, mha_wo, mha_wo_b, causal=False)
        h = _layernorm(x, ln3_g, ln3_b)
        x = x + (jax.nn.relu(h @ ffn_w1 + ffn_b1) @ ffn_w2 + ffn_b2)
        return x
    x = _L0_xattn_ref(x, ctx_1024, mask_Bx1x1xS2_if1, mask_Bx1xSxS2_if1, L0_xattn_sa_wq, L0_xattn_sa_bq, L0_xattn_sa_wk, L0_xattn_sa_bk, L0_xattn_sa_wv, L0_xattn_sa_bv, L0_xattn_sa_wo, L0_xattn_sa_bo, L0_xattn_ca_wq, L0_xattn_ca_bq, L0_xattn_ca_wk, L0_xattn_ca_bk, L0_xattn_ca_wv, L0_xattn_ca_bv, L0_xattn_ca_wo, L0_xattn_ca_bo, L0_xattn_ffn_w1, L0_xattn_ffn_b1, L0_xattn_ffn_w2, L0_xattn_ffn_b2, L0_xattn_ln1_g, L0_xattn_ln1_b, L0_xattn_ln2_g, L0_xattn_ln2_b, L0_xattn_ln3_g, L0_xattn_ln3_b)
    x = _L1_xattn_ref(x, ctx_1024, ctx_1024, L1_xattn_e_wq, L1_xattn_e_wk, L1_xattn_e_wv, L1_xattn_e_wm, L1_xattn_e_w1, L1_xattn_e_w2, L1_xattn_e_g1, L1_xattn_e_b1, L1_xattn_e_g2, L1_xattn_e_b2, L1_xattn_d_wq0, L1_xattn_d_wk0, L1_xattn_d_wv0, L1_xattn_d_wm0, L1_xattn_d_wq1, L1_xattn_d_wk1, L1_xattn_d_wv1, L1_xattn_d_wm1, L1_xattn_d_w1, L1_xattn_d_w2, L1_xattn_d_g0, L1_xattn_d_b0, L1_xattn_d_g1, L1_xattn_d_b1, L1_xattn_d_g2, L1_xattn_d_b2)
    x = _L2_xattn_ref(x, ctx_1024, L2_xattn_sa_ln_g, L2_xattn_sa_ln_b, L2_xattn_sa_in_w, L2_xattn_sa_in_b, L2_xattn_sa_out_w, L2_xattn_sa_out_b, L2_xattn_ca_q_ln_g, L2_xattn_ca_q_ln_b, L2_xattn_ca_kv_ln_g, L2_xattn_ca_kv_ln_b, L2_xattn_ca_in_w, L2_xattn_ca_in_b, L2_xattn_ca_out_w, L2_xattn_ca_out_b, L2_xattn_moe_ln_g, L2_xattn_moe_ln_b, L2_xattn_router_w, L2_xattn_router_b, L2_xattn_e_fc1_w, L2_xattn_e_fc1_b, L2_xattn_e_fc2_w, L2_xattn_e_fc2_b)
    x = _L3_xattn_ref(x, ctx_1024, L3_xattn_mmha_wq, L3_xattn_mmha_wq_b, L3_xattn_mmha_wk, L3_xattn_mmha_wk_b, L3_xattn_mmha_wv, L3_xattn_mmha_wv_b, L3_xattn_mmha_wo, L3_xattn_mmha_wo_b, L3_xattn_mha_wq, L3_xattn_mha_wq_b, L3_xattn_mha_wk, L3_xattn_mha_wk_b, L3_xattn_mha_wv, L3_xattn_mha_wv_b, L3_xattn_mha_wo, L3_xattn_mha_wo_b, L3_xattn_ln1_g, L3_xattn_ln1_b, L3_xattn_ln2_g, L3_xattn_ln2_b, L3_xattn_ln3_g, L3_xattn_ln3_b, L3_xattn_ffn_w1, L3_xattn_ffn_b1, L3_xattn_ffn_w2, L3_xattn_ffn_b2)
    return x

_drawn_inputs = setup_inputs


def setup_inputs(seed=0):
    import zlib

    import numpy as np

    out = dict(_drawn_inputs(seed))
    spreads = {'L0_xattn_sa_bq': (0.0, 0.8),
     'L0_xattn_sa_bk': (0.0, 0.8),
     'L0_xattn_sa_bv': (0.0, 0.1),
     'L0_xattn_sa_bo': (0.0, 0.1),
     'L0_xattn_ca_bq': (0.0, 0.8),
     'L0_xattn_ca_bk': (0.0, 0.8),
     'L0_xattn_ca_bv': (0.0, 0.1),
     'L0_xattn_ca_bo': (0.0, 0.1),
     'L0_xattn_ffn_b1': (0.0, 0.1),
     'L0_xattn_ffn_b2': (0.0, 0.1),
     'L0_xattn_ln1_g': (1.0, 0.2),
     'L0_xattn_ln1_b': (0.0, 0.1),
     'L0_xattn_ln2_g': (1.0, 0.2),
     'L0_xattn_ln2_b': (0.0, 0.1),
     'L0_xattn_ln3_g': (1.0, 0.2),
     'L0_xattn_ln3_b': (0.0, 0.1),
     'L1_xattn_e_g1': (1.0, 0.2),
     'L1_xattn_e_b1': (0.0, 0.1),
     'L1_xattn_e_g2': (1.0, 0.2),
     'L1_xattn_e_b2': (0.0, 0.1),
     'L1_xattn_d_g0': (1.0, 0.2),
     'L1_xattn_d_b0': (0.0, 0.1),
     'L1_xattn_d_g1': (1.0, 0.2),
     'L1_xattn_d_b1': (0.0, 0.1),
     'L1_xattn_d_g2': (1.0, 0.2),
     'L1_xattn_d_b2': (0.0, 0.1),
     'L2_xattn_sa_ln_g': (1.0, 0.2),
     'L2_xattn_sa_ln_b': (0.0, 0.1),
     'L2_xattn_sa_in_b': (0.0, 0.1),
     'L2_xattn_sa_out_b': (0.0, 0.1),
     'L2_xattn_ca_q_ln_g': (1.0, 0.6),
     'L2_xattn_ca_q_ln_b': (0.0, 0.8),
     'L2_xattn_ca_kv_ln_g': (1.0, 0.2),
     'L2_xattn_ca_kv_ln_b': (0.0, 0.1),
     'L2_xattn_ca_in_b': (0.0, 0.1),
     'L2_xattn_ca_out_b': (0.0, 0.1),
     'L2_xattn_moe_ln_g': (1.0, 0.2),
     'L2_xattn_moe_ln_b': (0.0, 0.1),
     'L2_xattn_router_b': (0.0, 0.1),
     'L2_xattn_e_fc1_b': (0.0, 0.278),
     'L2_xattn_e_fc2_b': (0.0, 0.1),
     'L3_xattn_mmha_wq_b': (0.0, 0.8),
     'L3_xattn_mmha_wk_b': (0.0, 0.8),
     'L3_xattn_mmha_wv_b': (0.0, 0.302),
     'L3_xattn_mmha_wo_b': (0.0, 0.1),
     'L3_xattn_mha_wq_b': (0.0, 0.8),
     'L3_xattn_mha_wk_b': (0.0, 0.8),
     'L3_xattn_mha_wv_b': (0.0, 0.289),
     'L3_xattn_mha_wo_b': (0.0, 0.1),
     'L3_xattn_ln1_g': (1.0, 0.6),
     'L3_xattn_ln1_b': (0.0, 0.553),
     'L3_xattn_ln2_g': (1.0, 0.6),
     'L3_xattn_ln2_b': (0.0, 0.8),
     'L3_xattn_ln3_g': (1.0, 0.6),
     'L3_xattn_ln3_b': (0.0, 0.791),
     'L3_xattn_ffn_b1': (0.0, 0.482),
     'L3_xattn_ffn_b2': (0.0, 0.1)}
    factors = {'L0_xattn_sa_wq': 8.0,
     'L0_xattn_sa_wk': 8.0,
     'L0_xattn_sa_wv': 3.096,
     'L0_xattn_ca_wq': 8.0,
     'L0_xattn_ca_wk': 8.0,
     'L1_xattn_e_wq': 8.0,
     'L1_xattn_e_wk': 3.427,
     'L1_xattn_d_wq0': 8.0,
     'L1_xattn_d_wk0': 3.567,
     'L1_xattn_d_wq1': 6.619,
     'L1_xattn_d_wk1': 3.618,
     'L3_xattn_mmha_wq': 8.0,
     'L3_xattn_mmha_wk': 8.0,
     'L3_xattn_mha_wq': 5.608,
     'L3_xattn_mha_wk': 5.885}
    for name, (base, spread) in spreads.items():
        noise = np.random.default_rng([zlib.crc32(name.encode()), seed]).standard_normal(out[name].shape)
        drawn = base * np.exp(spread * noise) if base else spread * noise
        out[name] = jnp.asarray(drawn.astype(out[name].dtype))
    for name, factor in factors.items():
        out[name] = (out[name] * factor).astype(out[name].dtype)
    return out
```

```python
from contextlib import ExitStack

import numpy as np

import concourse.bass as bass
from concourse import mybir

F32 = mybir.dt.float32
F32R = mybir.dt.float32r
BF16 = mybir.dt.bfloat16
I32 = mybir.dt.int32
U32 = mybir.dt.uint32
ALU = mybir.AluOpType
ACT = mybir.ActivationFunctionType
AX = mybir.AxisListType

P = 128
B = 8
S = 256
D = 256
NT = S // P
NF = D // P
H = 16
DH = D // H
NE = 8
FE = 1024
EPS = 1e-5
EXP_LN = "natural_log_exp_and_others"
MASKED = -float(2 ** 100)
CHUNK = 512
STAGES = 4


class Signal:

    def __init__(self, nc, ctx, name):
        self.sem = ctx.enter_context(nc.semaphore(name))
        self.base = 0
        self.per = 0

    def begin(self, per):
        self.per = per

    def end(self, n=B):
        self.base += self.per * n
        self.per = 0

    def at(self, b, k):
        return self.sem, b * self.per + (self.base + k)


def for_sequences(eng, body):
    body(0, 0, True, False)
    with eng.Fori(0, (B - 2) // 2) as i:
        body(2 * i + 1, 1, False, False)
        body(2 * i + 2, 0, False, False)
    body(B - 1, 1, False, True)


ATT = ("att", 4 * NF * D)
GROUPS = [("L0s", 4 * NF * D), ("L0c", 4 * NF * D), ("L0f", 2 * 4 * NF * D),
          ("L1e", 4 * NF * D), ("L1ef", 2 * 2 * NF * D), ("L1s", 4 * NF * D), ("L1c", 4 * NF * D),
          ("L1df", 2 * 2 * NF * D), ("L2s", 4 * NF * D), ("L2c", 4 * NF * D)] + \
         [(f"E{e}", 2 * 4 * NF * D) for e in range(NE)] + \
         [("L3s", 4 * NF * D), ("L3c", 4 * NF * D), ("L3f", 2 * 4 * NF * D)]
GOFF = {}
_o = 0
for _n, _c in GROUPS:
    GOFF[_n] = _o
    _o += _c
WCOLS = _o
GSIZE = dict(GROUPS)
GINDEX = {n: i for i, (n, _) in enumerate(GROUPS)}

ROWS = {"L0s": ["L0_xattn_sa_bv", "L0_xattn_sa_bo", "L0_xattn_ln1_g", "L0_xattn_ln1_b"],
        "L0c": ["L0_xattn_ca_bv", "L0_xattn_ca_bo", "L0_xattn_ln2_g", "L0_xattn_ln2_b"],
        "L0f": ["L0_xattn_ffn_b2", "L0_xattn_ln3_g", "L0_xattn_ln3_b"],
        "L1e": ["L1_xattn_e_g1", "L1_xattn_e_b1"], "L1ef": ["L1_xattn_e_g2", "L1_xattn_e_b2"],
        "L1s": ["L1_xattn_d_g0", "L1_xattn_d_b0"], "L1c": ["L1_xattn_d_g1", "L1_xattn_d_b1"],
        "L1df": ["L1_xattn_d_g2", "L1_xattn_d_b2"],
        "L2s": ["@L2_xattn_sa_in_b:2", "L2_xattn_sa_out_b"],
        "L2c": ["@L2_xattn_ca_in_b:2", "L2_xattn_ca_out_b"],
        "E0": ["#L2_xattn_e_fc2_b:%d" % e for e in range(NE)],
        "L3s": ["L3_xattn_mmha_wv_b", "L3_xattn_mmha_wo_b"],
        "L3c": ["L3_xattn_mha_wv_b", "L3_xattn_mha_wo_b"],
        "L3f": ["L3_xattn_ffn_b2"]}
ROFF = {}
_o = 0
for _n, _r in ROWS.items():
    ROFF[_n] = _o
    _o += len(_r)
NROWS = _o
MAXROWS = 4

COLS = ["L0_xattn_sa_bq", "L0_xattn_sa_bk", "L0_xattn_ca_bq", "L0_xattn_ca_bk",
        "@L2_xattn_sa_in_b:0", "@L2_xattn_sa_in_b:1", "@L2_xattn_ca_in_b:0", "@L2_xattn_ca_in_b:1",
        "L3_xattn_mmha_wq_b", "L3_xattn_mmha_wk_b", "L3_xattn_mha_wq_b", "L3_xattn_mha_wk_b",
        "L2_xattn_sa_ln_g", "L2_xattn_sa_ln_b", "L2_xattn_ca_q_ln_g", "L2_xattn_ca_q_ln_b",
        "L2_xattn_ca_kv_ln_g", "L2_xattn_ca_kv_ln_b", "L2_xattn_moe_ln_g", "L2_xattn_moe_ln_b",
        "L3_xattn_ln1_g", "L3_xattn_ln1_b", "L3_xattn_ln2_g", "L3_xattn_ln2_b",
        "L3_xattn_ln3_g", "L3_xattn_ln3_b"]
COFF = {}
_o = 0
for _n in COLS:
    COFF[_n] = _o
    _o += NF
for _n in ("L0_xattn_ffn_b1", "L3_xattn_ffn_b1"):
    COFF[_n] = _o
    _o += 8
COFF["experts"] = _o
_o += NE * FE // P
NCOLS = _o
BQS = ["L0_xattn_sa_bq", "L0_xattn_ca_bq", "@L2_xattn_sa_in_b:0", "@L2_xattn_ca_in_b:0",
       "L3_xattn_mmha_wq_b", "L3_xattn_mha_wq_b"]


class Core:

    def __init__(self, nc, ctx, d):
        self.nc, self.d = nc, d
        sb = lambda n, s, t=F32: ctx.enter_context(nc.sbuf_tensor(n, s, t))
        self.X = sb("X", [P, B * NT, D])
        self.wh = [sb(f"w_hi{i}", [P, 4096], F32R) for i in range(2)]
        self.wl = [sb(f"w_lo{i}", [P, 4096], F32R) for i in range(2)]
        self.stage = sb("w_stage", [P, STAGES, CHUNK])
        self.rows = [sb(f"rows{i}", [P, MAXROWS, D]) for i in range(2)]
        self.cols = sb("cols", [P, NCOLS])
        self.bq4 = sb("bq4", [P, len(BQS), NF])
        self.ident = sb("ident", [P, P])
        self.ident_bf = sb("ident_bf", [P, P], BF16)
        self.tri = sb("tri", [P, P])
        self.tri_bf = sb("tri_bf", [P, P], BF16)
        self.psum = ctx.enter_context(nc.psum_tensor("psum", [P, 8, 512], F32))
        self.sig = {}
        self.ctx = ctx
        self.begun = []
        self.phase = ""

    def s(self, name):
        if name not in self.sig:
            self.sig[name] = Signal(self.nc, self.ctx, name)
        return self.sig[name]

    def begin(self, **per):
        for n, k in per.items():
            self.s(n).begin(k)
        self.begun = list(per)
        return [self.s(n) for n in per]

    def end(self):
        for n in self.begun:
            self.s(n).end()

    def col(self, name, j):
        c = COFF[name] + j
        return self.cols[:, c:c + 1]


def load_group(core, pool, name):
    nc, d = core.nc, core.d
    g = GINDEX[name]
    par = g % 2
    n = GSIZE[name] // CHUNK
    raw, hi_done, split = core.s("w_raw"), core.s("w_hi_done"), core.s("w_split")
    wh, wl = core.wh[par], core.wl[par]
    if name in ROWS and name != "E0":
        nr = len(ROWS[name])
        src = d["rows"][ROFF[name]:ROFF[name] + nr, :].partition_broadcast(P)
        pool.dma_start(core.rows[par][:, 0:nr, :], src).then_inc(core.s("rows_in").sem, 16)

    def bring(c):
        if split.base + c - STAGES + 1 > 0:
            pool.wait_ge(split.sem, split.base + c - STAGES + 1)
        pool.dma_start(core.stage[:, c % STAGES, :],
                       d["weights"][:, GOFF[name] + c * CHUNK:GOFF[name] + (c + 1) * CHUNK]
                       ).then_inc(core.raw_sems[c % STAGES].sem, 16)

    for c in range(min(STAGES - 1, n)):
        bring(c)
    for c in range(n):
        if c + STAGES - 1 < n:
            bring(c + STAGES - 1)
        slot = core.raw_sems[c % STAGES]
        slot.base += 16
        pool.wait_ge(slot.sem, slot.base)
        st = core.stage[:, c % STAGES, :]
        a, z = c * CHUNK, (c + 1) * CHUNK
        if name in ("L0s", "L0c", "L2s", "L2c", "L3s", "L3c") and c == 0:
            sc = core.s("w_scaled")
            pool.tensor_scalar(st, st, DH ** -0.5, None, ALU.mult).then_inc(sc.sem, 1)
            sc.base += 1
            pool.wait_ge(sc.sem, sc.base)
        pool.tensor_copy(wh[:, a:z], st).then_inc(hi_done.sem, 1)
        hi_done.base += 1
        pool.wait_ge(hi_done.sem, hi_done.base)
        pool.tensor_tensor(wl[:, a:z], st, wh[:, a:z].bitcast(F32), ALU.subtract).then_inc(split.sem, 1)
    split.base += n
    if name in ROWS and name != "E0":
        rin = core.s("rows_in")
        rin.base += 16
        pool.wait_ge(rin.sem, rin.base)


def weights_of(core, name):
    par = GINDEX[name] % 2
    return core.wh[par], core.wl[par], core.rows[par]


def three_pass(pe, out, lh, ll, rh, rl, first, last):
    pe.matmul(out, lh, rh, start=first, stop=False)
    pe.matmul(out, lh, rl, start=False, stop=False)
    return pe.matmul(out, ll, rh, start=False, stop=last)


def project_features(pe, out, wh, wl, off, width, xh, xl, tiles, n=S):
    for j, f in enumerate(tiles):
        for k in range(NF):
            a = off + k * width + f * P
            m = three_pass(pe, out[:, j, 0:n], wh[:, a:a + P], wl[:, a:a + P], xh[:, k, :], xl[:, k, :],
                           k == 0, k == NF - 1)
    return m


def project_tokens(pe, out, wh, wl, off, xh, xl, nk=NF):
    for t in range(NT):
        for k in range(nk):
            a = off + k * D
            m = three_pass(pe, out[:, t, :], xh[:, k, t * P:(t + 1) * P], xl[:, k, t * P:(t + 1) * P],
                           wh[:, a:a + D], wl[:, a:a + D], k == 0, k == nk - 1)
    return m


def turn(pe, core, out, x):
    for t in range(NT):
        for f in range(NF):
            m = pe.transpose(out[:, f, t * P:(t + 1) * P], x[:, t, f * P:(f + 1) * P], core.ident[:, :])
    return m


def bank(core, i):
    return core.psum[:, i, :].rearrange("p (a n) -> p a n", a=2)


class Source:

    def __init__(self, core, ctx, tag, kind, ln=None, state=None, dram=None):
        nc = core.nc
        sb = lambda n, s, t=F32: ctx.enter_context(nc.sbuf_tensor(f"{core.phase}_{tag}_{n}", s, t))
        self.core, self.tag, self.ln, self.state, self.dram = core, tag, ln, state, dram
        self.x_in = sb("in", [P, NT, D])
        self.raw = sb("raw", [P, NT, D]) if dram is not None and ln else None
        self.xh = sb("hi", [P, NF, S], F32R)
        self.xl = sb("lo", [P, NF, S], F32R)
        if ln:
            self.full = sb("full", [P, NF, S])
            self.stats = sb("stats", [P, NT, 6])
            self.mv = sb("mv", [P, NT, 2])
            self.lnv = sb("lnv", [P, NT])
            self.rstd = sb("rstd", [P, NT])
        per = {f"{tag}_in": NT if ln else 1, f"{tag}_turned": 1, f"{tag}_hi": NF if ln else 1, f"{tag}_lo": 1}
        if dram is not None:
            per[f"{tag}_load" if ln else f"{tag}_in"] = 16
        if ln:
            per.update({f"{tag}_stats": NT, f"{tag}_mv": NT, f"{tag}_aggr": 1, f"{tag}_lnv": 1, f"{tag}_rstd": 1, f"{tag}_full": NF})
            per[f"{tag}_hi"] = 1
        self.per = per

    def sg(self, n):
        return self.core.s(f"{self.tag}_{n}")

    def load(self, sp, b):
        if self.dram is None:
            return
        if self.ln:
            sp.wait_ge(*self.sg("in").at(b, 0))
            sp.dma_start(self.raw[:, :, :], self.dram[:, bass.ds(NT * b, NT), :]).then_inc(self.sg("load").sem, 16)
        else:
            sp.wait_ge(*self.sg("turned").at(b, 0))
            sp.dma_start(self.x_in[:, :, :], self.dram[:, bass.ds(NT * b, NT), :]).then_inc(self.sg("in").sem, 16)

    def src(self, b, t=None):
        if self.raw is not None:
            return self.raw[:, :, :] if t is None else self.raw[:, t, :]
        return self.state[:, bass.ds(NT * b, NT), :] if t is None else self.state[:, NT * b + t, :]

    def dve_stats(self, v, b):
        if self.ln is None:
            if self.dram is None:
                v.wait_ge(*self.sg("turned").at(b, 0))
                v.tensor_copy(self.x_in[:, :, :], self.src(b)).then_inc(self.sg("in").sem, 1)
            return
        if self.raw is not None:
            v.wait_ge(*self.sg("load").at(b, 16))
        for t in range(NT):
            v.bn_stats(self.stats[:, t, :], self.src(b, t)).then_inc(self.sg("stats").sem, 1)
        v.wait_ge(*self.sg("stats").at(b, NT))
        v.wait_ge(*self.sg("rstd").at(b, 0))
        v.sem_inc(self.sg("aggr").sem, 1)
        for t in range(NT):
            v.bn_aggr(self.mv[:, t, :], self.stats[:, t, :]).then_inc(self.sg("mv").sem, 1)

    def act_rstd(self, a, b):
        if self.ln is None:
            return
        a.wait_ge(*self.sg("mv").at(b, NT))
        a.activation(self.lnv[:, :], self.mv[:, :, 1], ACT.Ln, bias=self.core.eps[:, 0:1]).then_inc(self.sg("lnv").sem, 1)
        a.wait_ge(*self.sg("lnv").at(b, 1))
        a.wait_ge(*self.sg("in").at(b, 0))
        a.activation(self.rstd[:, :], self.lnv[:, :], ACT.Exp, scale=-0.5).then_inc(self.sg("rstd").sem, 1)

    def dve_norm(self, v, b):
        if self.ln is None:
            return
        v.wait_ge(*self.sg("rstd").at(b, 1))
        v.wait_ge(*self.sg("turned").at(b, 0))
        for t in range(NT):
            v.tensor_scalar(self.x_in[:, t, :], self.src(b, t), self.mv[:, t, 0:1], self.rstd[:, t:t + 1],
                            ALU.subtract, ALU.mult).then_inc(self.sg("in").sem, 1)

    def pe_turn(self, pe, b, out):
        pe.wait_ge(*self.sg("in").at(b, self.sg("in").per))
        turn(pe, self.core, out, self.x_in).then_inc(self.sg("turned").sem, 1)

    def act_hi(self, a, b, src, used):
        a.wait_ge(*self.sg("turned").at(b, 1))
        if self.ln is None:
            a.wait_ge(*used.at(b, 0))
            a.activation(self.xh[:, :, :], src, ACT.Copy).then_inc(self.sg("hi").sem, 1)
            return
        a.wait_ge(*self.sg("lo").at(b, 0))
        for f in range(NF):
            a.activation(self.full[:, f, :], src[:, f, :], ACT.Identity, bias=self.core.col(self.ln[1], f),
                         scale=self.core.col(self.ln[0], f)).then_inc(self.sg("full").sem, 1)

    def dve_lo(self, v, b, src, used):
        if self.ln is None:
            v.wait_ge(*self.sg("hi").at(b, 1))
            v.wait_ge(*used.at(b, 0))
            v.tensor_tensor(self.xl[:, :, :], src, self.xh[:, :, :].bitcast(F32), ALU.subtract
                            ).then_inc(self.sg("lo").sem, 1)
            return
        v.wait_ge(*self.sg("full").at(b, NF))
        v.wait_ge(*used.at(b, 0))
        v.tensor_copy(self.xh[:, :, :], self.full[:, :, :]).then_inc(self.sg("hi").sem, 1)
        v.wait_ge(*self.sg("hi").at(b, 1))
        v.tensor_tensor(self.xl[:, :, :], self.full[:, :, :], self.xh[:, :, :].bitcast(F32), ALU.subtract
                        ).then_inc(self.sg("lo").sem, 1)


class Finish:

    def __init__(self, core, ctx, kind, rows, bias, g, state):
        nc = core.nc
        sb = lambda n, s, t=F32: ctx.enter_context(nc.sbuf_tensor(f"{core.phase}_fin_{n}", s, t))
        self.core, self.kind, self.rows, self.bias, self.g, self.state = core, kind, rows, bias, g, state
        self.y = sb("y", [P, NT, D])
        self.z = sb("z", [P, NT, D]) if kind != "pre" else None
        if kind != "pre":
            self.stats = sb("stats", [P, NT, 6])
            self.mv = sb("mv", [P, NT, 2])
            self.lnv = sb("lnv", [P, NT])
            self.rstd = sb("rstd", [P, NT])
        self.per = {"fin_read": 1, "fin_done": 1}
        if kind == "inner":
            self.per["fin_norm2"] = 1
        if kind != "pre":
            self.per.update({"fin_y": 1, "fin_stats": NT, "fin_aggr": 1, "fin_mv": NT, "fin_lnv": 1, "fin_rstd": 1,
                             "fin_norm": NT, "fin_scaled": 1})

    def row(self, r):
        return self.rows[:, r:r + 1, :].broadcast_to([P, NT, D])

    def dve_read(self, v, b, out, out_sig, out_n):
        s = self.core.s
        v.wait_ge(*out_sig.at(b, out_n))
        v.wait_ge(*s("fin_done").at(b, 0))
        x = self.state[:, bass.ds(NT * b, NT), :]
        if self.bias is not None:
            v.tensor_tensor(self.y[:, :, :], out, self.row(self.bias), ALU.add).then_inc(s("fin_read").sem, 1)
        else:
            v.tensor_copy(self.y[:, :, :], out).then_inc(s("fin_read").sem, 1)
        v.wait_ge(*s("fin_read").at(b, 1))
        if self.kind == "pre":
            v.tensor_tensor(x, x, self.y[:, :, :], ALU.add).then_inc(s("fin_done").sem, 1)
            return
        if self.kind == "post":
            v.tensor_tensor(self.y[:, :, :], self.y[:, :, :], x, ALU.add).then_inc(s("fin_y").sem, 1)
            v.wait_ge(*s("fin_y").at(b, 1))
        for t in range(NT):
            v.bn_stats(self.stats[:, t, :], self.y[:, t, :]).then_inc(s("fin_stats").sem, 1)
        v.wait_ge(*s("fin_stats").at(b, NT))
        v.sem_inc(s("fin_aggr").sem, 1)
        for t in range(NT):
            v.bn_aggr(self.mv[:, t, :], self.stats[:, t, :]).then_inc(s("fin_mv").sem, 1)

    def act_rstd(self, a, b):
        s = self.core.s
        if self.kind == "pre":
            return
        a.wait_ge(*s("fin_mv").at(b, NT))
        a.activation(self.lnv[:, :], self.mv[:, :, 1], ACT.Ln, bias=self.core.eps[:, 0:1]).then_inc(s("fin_lnv").sem, 1)
        a.wait_ge(*s("fin_lnv").at(b, 1))
        a.activation(self.rstd[:, :], self.lnv[:, :], ACT.Exp, scale=-0.5).then_inc(s("fin_rstd").sem, 1)

    def dve_norm(self, v, b):
        s = self.core.s
        if self.kind == "pre":
            return
        x = self.state[:, bass.ds(NT * b, NT), :]
        v.wait_ge(*s("fin_rstd").at(b, 1))
        for t in range(NT):
            v.tensor_scalar(self.z[:, t, :], self.y[:, t, :], self.mv[:, t, 0:1], self.rstd[:, t:t + 1],
                            ALU.subtract, ALU.mult).then_inc(s("fin_norm").sem, 1)
        v.wait_ge(*s("fin_norm").at(b, NT))
        v.tensor_tensor(self.z[:, :, :], self.z[:, :, :], self.row(self.g), ALU.mult).then_inc(s("fin_scaled").sem, 1)
        v.wait_ge(*s("fin_scaled").at(b, 1))
        if self.kind == "inner":
            v.tensor_tensor(self.z[:, :, :], self.z[:, :, :], self.row(self.g + 1), ALU.add).then_inc(s("fin_norm2").sem, 1)
            v.wait_ge(*s("fin_norm2").at(b, 1))
            v.tensor_tensor(x, x, self.z[:, :, :], ALU.add).then_inc(s("fin_done").sem, 1)
        else:
            v.tensor_tensor(x, self.z[:, :, :], self.row(self.g + 1), ALU.add).then_inc(s("fin_done").sem, 1)


def attention(core, name, q_src, kv_src, bq, bk, kind, g, mask, nxt):
    nc = core.nc
    with ExitStack() as ctx:
        core.phase = name
        sb = lambda n, s, t=F32: ctx.enter_context(nc.sbuf_tensor(f"{name}_{n}", s, t))
        wh, wl, rows = weights_of(core, name)
        w_at = lambda m: m * NF * D
        q = Source(core, ctx, "q", kind, **q_src)
        kv = Source(core, ctx, "kv", kind, **kv_src) if kv_src else q
        cross = kv is not q
        G8 = H // NF
        qh = [sb(f"qh{i}", [P, NF, S], F32R) for i in range(2)]
        ql = [sb(f"ql{i}", [P, NF, S], F32R) for i in range(2)]
        k2 = sb("k2", [P, NF, 2, S], F32R)
        kh, kl = k2[:, :, 0, :], k2[:, :, 1, :]
        kx = sb("kx", [P, NF, 2, G8, S], F32R)
        vx = [sb(f"vx{i}", [P, NT, H // 2, 2, 2 * DH]) for i in range(2)]
        e = sb("e", [P, 2, NT, 2, S])
        et = sb("et", [P, G8, NT, S])
        neg = sb("neg", [P, 2, NT, 2])
        den = sb("den", [P, 2, NT, H])
        rcp = sb("rcp", [P, NT, H])
        rcpx = sb("rcpx", [P, NT, H, DH])
        rt = sb("rt", [P, NF, S])
        on = sb("on", [P, NF, S])
        oh = sb("oh", [P, NF, S], F32R)
        ol = sb("ol", [P, NF, S], F32R)
        fin = Finish(core, ctx, kind, rows, 1, g, core.X)
        if mask in ("self", "keys"):
            mt = NT if mask == "self" else 1
            mi = sb("mi", [P, mt, S], I32)
            mb = [sb(f"mb{i}", [P, mt, S], BF16) for i in range(2)]
        U = H // 2
        keys_of = [P, S] if mask == "causal" else [S, S]
        NE_ = 2 * NT
        core.begin(**q.per, **(kv.per if cross else {}), **fin.per,
                   q_psum=1, qh=NF, ql=NF, k_psum=1, kh=NF, kl=NF, kx0=G8 * 16, kx1=G8 * 16, v_psum=1, vx=2,
                   scores=U, neg=(2 if mask == "causal" else 1) * U, exps=NE_ * U, et_psum=U,
                   et=(2 * (1 + (mask == "causal"))) * U, pv=NF, rcp=1, rcpx=1, rt_psum=1, rt=1, on=1, oh=1, ol=1,
                   out_psum=1, mask_in=16 if mask in ("self", "keys") else 0, mask_b=1)
        s = core.s
        NEG = s("neg").per // U
        ETN = s("et").per // U
        M = bank(core, 7)
        O = bank(core, 6)
        SC = [core.psum[:, 2 * i:2 * i + 2, :].rearrange("p t (h k) -> p t h k", h=2) for i in range(2)]
        ET = core.psum[:, 4:6, :].rearrange("p h (t q) -> p h t q", t=NT)
        kx_zero, vx_zero = s("kx_zero"), s("vx_zero")
        ready = core.s("w_split")
        ready_at = ready.base
        rows_at = core.s("rows_in").base

        with nc.Block() as block:
            @block.sync
            def _(sp):
                def kx_dma(b, ft):
                    for i in range(G8):
                        r = slice(DH * i, DH * (i + 1))
                        sp.dma_start(kx[r, ft, :, i, :].bitcast(F32), k2[r, ft, :, :].bitcast(F32)).then_inc(s(f"kx{ft}").sem, 16)

                def inputs(b):
                    q.load(sp, b)
                    if cross:
                        kv.load(sp, b)
                    if mask == "self" or mask == "keys":
                        sp.wait_ge(*s("mask_b").at(b, 0))
                        src = (core.d["mask_self"][:, bass.ds(NT * b, NT), :] if mask == "self" else
                               core.d["mask_keys"][bass.ds(b, 1), :].partition_broadcast(P))
                        sp.dma_start(mi[:, :, :], src).then_inc(s("mask_in").sem, 16)

                def body(b, par, first, last):
                    if not last:
                        inputs(b + 1)
                        nb = b + 1
                        sp.wait_ge(*s("kh").at(nb, NF))
                        sp.wait_ge(*s("kl").at(nb, NF))
                        kx_dma(nb, 0)
                        sp.wait_ge(*s("scores").at(b, U))
                        kx_dma(nb, 1)
                inputs(0)
                sp.wait_ge(*s("kh").at(0, NF))
                sp.wait_ge(*s("kl").at(0, NF))
                sp.wait_ge(kx_zero.sem, kx_zero.base + 2)
                for ft in range(NF):
                    kx_dma(0, ft)
                for_sequences(sp, body)

            @block.gpsimd
            def _(pool):
                pool.memset(kx[:, 1, :, :, :].bitcast(F32), 0.0).then_inc(kx_zero.sem, 1)
                pool.memset(vx[0][:, :, :, :, :], 0.0).then_inc(vx_zero.sem, 1)
                pool.memset(vx[1][:, :, :, :, :], 0.0).then_inc(vx_zero.sem, 1)
                if nxt:
                    load_group(core, pool, nxt)

            @block.tensor
            def _(pe):
                def scores(b, par, u):
                    ft, pr = u // (U // NF), u % (U // NF)
                    if u == 0:
                        pe.wait_ge(*s("qh").at(b, NF))
                        pe.wait_ge(*s("ql").at(b, NF))
                        if mask in ("self", "keys"):
                            pe.wait_ge(*s("mask_b").at(b, 1))
                    if pr == 0:
                        pe.wait_ge(*s(f"kx{ft}").at(b, G8 * 16))
                    if u >= 2:
                        pe.wait_ge(*s("exps").at(b, NE_ * (u - 1)))
                    elif u == 1:
                        pe.wait_ge(*s("exps").at(b, 0))
                    elif not (isinstance(b, int) and b == 0):
                        pe.wait_ge(*s("exps").at(b - 1, NE_ * (U - 1)))
                    out = SC[u % 2]
                    for t in range(NT):
                        n = keys_of[t]
                        o = out[:, t, :, 0:n]
                        lh = qh[par][:, ft, t * P:(t + 1) * P]
                        ll = ql[par][:, ft, t * P:(t + 1) * P]
                        rh = kx[:, ft, 0, 2 * pr:2 * pr + 2, 0:n]
                        rl = kx[:, ft, 1, 2 * pr:2 * pr + 2, 0:n]
                        m = three_pass(pe, o, lh, ll, rh, rl, True, mask in (None, "causal"))
                        if mask == "causal":
                            tri = core.tri_bf[:, :].unsqueeze(1).broadcast_to([P, 2, P])
                            m = pe.matmul(out[:, t, :, n - P:n], core.ident_bf[:, :], tri, start=False, stop=True,
                                          skip_group_check=True)
                        elif mask:
                            mm = mb[par][:, t if mask == "self" else 0, :].unsqueeze(1).broadcast_to([P, 2, S])
                            m = pe.matmul(o, core.ident_bf[:, :], mm, start=False, stop=True)
                    m.then_inc(s("scores").sem, 1)

                def turn_e(b, u):
                    pe.wait_ge(*s("exps").at(b, NE_ * (u + 1)))
                    pe.wait_ge(*s("et").at(b, ETN * u))
                    for h in range(2):
                        for k in range(NT):
                            for t in range(NT):
                                if k * P < keys_of[t]:
                                    m = pe.transpose(ET[:, h, k, t * P:(t + 1) * P],
                                                     e[:, u % 2, t, h, k * P:(k + 1) * P], core.ident[:, :])
                    m.then_inc(s("et_psum").sem, 1)

                def pv(b, par, ft):
                    pe.wait_ge(*s("et").at(b, ETN * (U // NF) * (ft + 1)))
                    pe.wait_ge(*s("vx").at(b, 2))
                    if ft == 0:
                        pe.wait_ge(*s("on").at(b, 0))
                    for hp in range(2):
                        for k in range(NT):
                            for g_ in range(G8 // 2):
                                q0 = P if (mask == "causal" and k == 1) else 0
                                lhs = vx[par][:, k, ft * (G8 // 2) + g_, hp, :]
                                m = pe.matmul(O[32 * g_:32 * g_ + 32, ft, q0:S], lhs, et[:, 2 * g_ + hp, k, q0:S],
                                              start=(hp == 0 and k == 0), stop=(hp == 1 and k == NT - 1),
                                              tile_position=(0, 32 * g_), skip_group_check=True)
                    m.then_inc(s("pv").sem, 1)

                def turn_rcp(b):
                    pe.wait_ge(*s("rcpx").at(b, 1))
                    for t in range(NT):
                        for f in range(NF):
                            m = pe.transpose(M[:, f, t * P:(t + 1) * P],
                                             rcpx[:, t, f * G8:(f + 1) * G8, :].rearrange("p h d -> p (h d)"),
                                             core.ident[:, :])
                    m.then_inc(s("rt_psum").sem, 1)

                def out_proj(b):
                    pe.wait_ge(*s("oh").at(b, 1))
                    pe.wait_ge(*s("ol").at(b, 1))
                    pe.wait_ge(*s("rt").at(b, 1))
                    project_tokens(pe, M, wh, wl, w_at(3), oh, ol).then_inc(s("out_psum").sem, 1)

                def turn_q(b, free):
                    free()
                    q.pe_turn(pe, b, M)

                def src_free(src, b):
                    pe.wait_ge(*src.sg("lo").at(b, 1))
                    pe.wait_ge(*src.sg("hi").at(b, src.sg("hi").per))

                def turn_kv(b):
                    src_free(q, b)
                    kv.pe_turn(pe, b, M)

                def q_proj(b):
                    src_free(q, b)
                    src_free(kv, b)
                    project_features(pe, M, wh, wl, w_at(0), D, q.xh, q.xl, range(NF)).then_inc(s("q_psum").sem, 1)

                def k_proj(b):
                    pe.wait_ge(*s("qh").at(b, NF))
                    pe.wait_ge(*s("ql").at(b, NF))
                    project_features(pe, M, wh, wl, w_at(1), D, kv.xh, kv.xl, range(NF)).then_inc(s("k_psum").sem, 1)

                def v_proj(b):
                    pe.wait_ge(*s("kh").at(b, NF))
                    pe.wait_ge(*s("kl").at(b, NF))
                    project_tokens(pe, M, wh, wl, w_at(2), kv.xh, kv.xl).then_inc(s("v_psum").sem, 1)

                def m_free_after_v(b):
                    pe.wait_ge(*s("vx").at(b, 2))

                def body(b, par, first, last):
                    for u in range(U):
                        if u < U - 1:
                            scores(b, par, u + 1)
                        elif not last:
                            scores(b + 1, 1 - par, 0)
                        if u == 0:
                            m_free_after_v(b)
                            if not first:
                                pv(b - 1, 1 - par, 1)
                                turn_rcp(b - 1)
                        if u == 1 and not first:
                            out_proj(b - 1)
                        if u == U // NF:
                            pv(b, par, 0)
                        if not last:
                            if u == 2:
                                if not first:
                                    pe.wait_ge(*s("fin_read").at(b - 1, 1))
                                q.pe_turn(pe, b + 1, M)
                            if u == 3 and cross:
                                turn_kv(b + 1)
                            if u == 4:
                                q_proj(b + 1)
                            if u == 5:
                                k_proj(b + 1)
                            if u == 6:
                                v_proj(b + 1)
                        turn_e(b, u)

                if ready_at:
                    pe.wait_ge(ready.sem, ready_at)
                q.pe_turn(pe, 0, M)
                if cross:
                    turn_kv(0)
                q_proj(0)
                k_proj(0)
                v_proj(0)
                scores(0, 0, 0)
                for_sequences(pe, body)
                pv(B - 1, 1, 1)
                pe.wait_ge(*s("fin_read").at(B - 2, 1))
                turn_rcp(B - 1)
                out_proj(B - 1)

            @block.scalar
            def _(a):
                def exps(b, par, u):
                    a.wait_ge(*s("neg").at(b, NEG * (u + 1)))
                    if u >= 2:
                        a.wait_ge(*s("et_psum").at(b, u - 1))
                    elif u == 1:
                        a.wait_ge(*s("et_psum").at(b, 0))
                    elif not (isinstance(b, int) and b == 0):
                        a.wait_ge(*s("et_psum").at(b - 1, U - 1))
                    for t in range(NT):
                        n = keys_of[t]
                        for h in range(2):
                            hd = 2 * u + h
                            a.activation(e[:, u % 2, t, h, 0:n], SC[u % 2][:, t, h, 0:n], ACT.Exp,
                                         bias=neg[:, u % 2, t, h:h + 1],
                                         accum_out=den[:, par, t, hd:hd + 1]).then_inc(s("exps").sem, 1)

                def copy_rt(b):
                    a.wait_ge(*s("rt_psum").at(b, 1))
                    a.wait_ge(*s("on").at(b, 0))
                    a.activation(rt[:, :, :], M, ACT.Copy).then_inc(s("rt").sem, 1)

                def hi_q(b, par):
                    a.wait_ge(*s("q_psum").at(b, 1))
                    for f in range(NF):
                        dst = qh[par][:, f, :]
                        a.activation(dst, M[:, f, :], ACT.Identity, bias=bq(f)).then_inc(s("qh").sem, 1)

                def hi_k(b):
                    a.wait_ge(*s("k_psum").at(b, 1))
                    a.wait_ge(*s("kx0").at(b, 0))
                    a.wait_ge(*s("kx1").at(b, 0))
                    for f in range(NF):
                        a.activation(kh[:, f, :], M[:, f, :], ACT.Identity, bias=bk(f)).then_inc(s("kh").sem, 1)

                def body(b, par, first, last):
                    for u in range(U):
                        exps(b, par, u)
                        if u == 0:
                            if not first:
                                copy_rt(b - 1)
                            if not last:
                                q.act_rstd(a, b + 1)
                                if cross:
                                    kv.act_rstd(a, b + 1)
                        if u == 1 and not first:
                            fin.act_rstd(a, b - 1)
                        if not last:
                            if u == 2:
                                q.act_hi(a, b + 1, M, s("q_psum") if cross else s("v_psum"))
                            if u == 3 and cross:
                                kv.act_hi(a, b + 1, M, s("v_psum"))
                            if u == 4:
                                hi_q(b + 1, 1 - par)
                            if u == 5:
                                hi_k(b + 1)

                a.preload_act_table_set(EXP_LN)
                q.act_rstd(a, 0)
                if cross:
                    kv.act_rstd(a, 0)
                q.act_hi(a, 0, M, s("q_psum") if cross else s("v_psum"))
                if cross:
                    kv.act_hi(a, 0, M, s("v_psum"))
                hi_q(0, 0)
                hi_k(0)
                for_sequences(a, body)
                copy_rt(B - 1)
                fin.act_rstd(a, B - 1)

            @block.vector
            def _(v):
                def maxes(b, u):
                    v.wait_ge(*s("scores").at(b, u + 1))
                    if mask == "causal":
                        for t in range(NT):
                            v.tensor_reduce(neg[:, u % 2, t, :], SC[u % 2][:, t, :, 0:keys_of[t]], AX.X, ALU.max,
                                            negate=True).then_inc(s("neg").sem, 1)
                    else:
                        v.tensor_reduce(neg[:, u % 2, :, :], SC[u % 2], AX.X, ALU.max,
                                        negate=True).then_inc(s("neg").sem, 1)

                def copy_et(b, u):
                    v.wait_ge(*s("et_psum").at(b, u + 1))
                    if u == 0:
                        v.wait_ge(*s("pv").at(b, 0))
                    elif u == U // NF:
                        v.wait_ge(*s("pv").at(b, 1))
                    i = (2 * u) % G8
                    for h in range(2):
                        if mask == "causal":
                            v.tensor_copy(et[:, i + h, 0, :], ET[:, h, 0, :]).then_inc(s("et").sem, 1)
                            v.tensor_copy(et[:, i + h, 1, P:S], ET[:, h, 1, P:S]).then_inc(s("et").sem, 1)
                        else:
                            v.tensor_copy(et[:, i + h, :, :], ET[:, h, :, :]).then_inc(s("et").sem, 1)

                def recips(b, par):
                    v.wait_ge(*s("exps").at(b, NE_ * U))
                    v.wait_ge(*s("rcpx").at(b, 0))
                    v.reciprocal(rcp[:, :, :], den[:, par, :, :]).then_inc(s("rcp").sem, 1)
                    v.wait_ge(*s("rcp").at(b, 1))
                    v.wait_ge(*s("rt_psum").at(b, 0))
                    v.tensor_copy(rcpx[:, :, :, :].rearrange("p t h d -> p (t h) d"),
                                  rcp[:, :, :].rearrange("p t h -> p (t h)").unsqueeze(2).broadcast_to([P, NT * H, DH])
                                  ).then_inc(s("rcpx").sem, 1)

                def normalise(b):
                    v.wait_ge(*s("rt").at(b, 1))
                    v.wait_ge(*s("pv").at(b, NF))
                    v.wait_ge(*s("ol").at(b, 0))
                    v.tensor_tensor(on[:, :, :], O, rt[:, :, :], ALU.mult).then_inc(s("on").sem, 1)
                    v.wait_ge(*s("on").at(b, 1))
                    v.wait_ge(*s("out_psum").at(b, 0))
                    v.tensor_copy(oh[:, :, :], on[:, :, :]).then_inc(s("oh").sem, 1)
                    v.wait_ge(*s("oh").at(b, 1))
                    v.tensor_tensor(ol[:, :, :], on[:, :, :], oh[:, :, :].bitcast(F32), ALU.subtract).then_inc(s("ol").sem, 1)

                def lo_q(b, par):
                    v.wait_ge(*s("qh").at(b, NF))
                    for f in range(NF):
                        v.scalar_tensor_tensor(ql[par][:, f, :], M[:, f, :], bq(f), qh[par][:, f, :].bitcast(F32),
                                               ALU.add, ALU.subtract).then_inc(s("ql").sem, 1)

                def lo_k(b):
                    v.wait_ge(*s("kh").at(b, NF))
                    v.wait_ge(*s("kx0").at(b, 0))
                    v.wait_ge(*s("kx1").at(b, 0))
                    for f in range(NF):
                        v.scalar_tensor_tensor(kl[:, f, :], M[:, f, :], bk(f), kh[:, f, :].bitcast(F32),
                                               ALU.add, ALU.subtract).then_inc(s("kl").sem, 1)

                def spread_v(b, par):
                    v.wait_ge(*s("v_psum").at(b, 1))
                    src = M.rearrange("p t (g x d) -> p t g x d", x=2, d=DH)
                    bv = rows[:, 0, :].rearrange("p (g x d) -> p g x d", x=2, d=DH)
                    for x in range(2):
                        v.tensor_tensor(vx[par][:, :, :, x, x * DH:(x + 1) * DH], src[:, :, :, x, :],
                                        bv[:, :, x, :].unsqueeze(1).broadcast_to([P, NT, H // 2, DH]), ALU.add
                                        ).then_inc(s("vx").sem, 1)

                def convert_mask(b, par):
                    if mask in ("self", "keys"):
                        v.wait_ge(*s("mask_in").at(b, 16))
                        v.tensor_scalar(mb[par][:, :, :], mi[:, :, :], 0.0, MASKED, ALU.is_equal, ALU.mult
                                        ).then_inc(s("mask_b").sem, 1)

                def body(b, par, first, last):
                    for u in range(U):
                        if u == 0 and not first:
                            recips(b - 1, 1 - par)
                        if u < U - 1:
                            maxes(b, u + 1)
                        elif not last:
                            maxes(b + 1, 0)
                        if u == 0:
                            if not last:
                                q.dve_stats(v, b + 1)
                                if cross:
                                    kv.dve_stats(v, b + 1)
                            if not first:
                                normalise(b - 1)
                        if u == 1:
                            if not last:
                                q.dve_norm(v, b + 1)
                                if cross:
                                    kv.dve_norm(v, b + 1)
                            if not first:
                                fin.dve_read(v, b - 1, M, s("out_psum"), 1)
                        if u == 2:
                            if not last:
                                q.dve_lo(v, b + 1, M, s("q_psum") if cross else s("v_psum"))
                            if not first:
                                fin.dve_norm(v, b - 1)
                        if not last:
                            if u == 3:
                                if cross:
                                    kv.dve_lo(v, b + 1, M, s("v_psum"))
                                convert_mask(b + 1, 1 - par)
                            if u == 4:
                                lo_q(b + 1, 1 - par)
                            if u == 5:
                                lo_k(b + 1)
                            if u == 6:
                                spread_v(b + 1, 1 - par)
                        copy_et(b, u)

                v.memset(kx[:, 0, :, :, :].bitcast(F32), 0.0).then_inc(kx_zero.sem, 1)
                q.dve_stats(v, 0)
                q.dve_norm(v, 0)
                if cross:
                    kv.dve_stats(v, 0)
                    kv.dve_norm(v, 0)
                q.dve_lo(v, 0, M, s("q_psum") if cross else s("v_psum"))
                if cross:
                    kv.dve_lo(v, 0, M, s("v_psum"))
                convert_mask(0, 0)
                lo_q(0, 0)
                lo_k(0)
                v.wait_ge(vx_zero.sem, vx_zero.base + 2)
                if rows_at:
                    v.wait_ge(s("rows_in").sem, rows_at)
                spread_v(0, 0)
                maxes(0, 0)
                for_sequences(v, body)
                recips(B - 1, 1)
                normalise(B - 1)
                fin.dve_read(v, B - 1, M, s("out_psum"), 1)
                fin.dve_norm(v, B - 1)

        kx_zero.base += 2
        vx_zero.base += 2
        core.end()


def hidden_bank(core, j):
    return core.psum[:, j, :].rearrange("p (a n) -> p a n", a=2)


def feed_forward(core, name, src, hidden, b1, kind, bias, g, state, nxt):
    nc = core.nc
    with ExitStack() as ctx:
        core.phase = name
        sb = lambda n, s, t=F32: ctx.enter_context(nc.sbuf_tensor(f"{name}_{n}", s, t))
        wh, wl, rows = weights_of(core, name)
        q = Source(core, ctx, "q", kind, **src)
        fin = Finish(core, ctx, kind, rows, bias, g, state)
        HT = hidden // P
        NB = HT // 2
        relu = sb("relu", [P, HT, S])
        hh = [sb(f"hid_hi{i}", [P, HT, S], F32R) for i in range(2)]
        hl = [sb(f"hid_lo{i}", [P, HT, S], F32R) for i in range(2)]
        core.begin(**q.per, **fin.per, hid_psum=NB, relu=HT if b1 else NB, hid_hi=NB, hid_lo=NB, out_psum=1)
        s = core.s
        M, O = bank(core, 7), bank(core, 6)
        ready_at, rows_at = core.s("w_split").base, core.s("rows_in").base
        RN = s("relu").per // NB

        with nc.Block() as block:
            @block.sync
            def _(sp):
                sp.nop()

            @block.gpsimd
            def _(pool):
                if nxt:
                    load_group(core, pool, nxt)

            @block.tensor
            def _(pe):
                def turn_q(b):
                    pe.wait_ge(*q.sg("lo").at(b, 0))
                    q.pe_turn(pe, b, M)

                def hidden_of(b):
                    pe.wait_ge(*q.sg("lo").at(b, 1))
                    pe.wait_ge(*q.sg("hi").at(b, q.sg("hi").per))
                    for j in range(NB):
                        pe.wait_ge(*s("relu").at(b, 0))
                        project_features(pe, hidden_bank(core, j), wh, wl, 0, hidden, q.xh, q.xl,
                                         (2 * j, 2 * j + 1)).then_inc(s("hid_psum").sem, 1)

                def out_of(b, par):
                    pe.wait_ge(*s("hid_lo").at(b, NB))
                    pe.wait_ge(*s("fin_read").at(b, 0))
                    project_tokens(pe, O, wh, wl, NF * hidden, hh[par], hl[par], HT).then_inc(s("out_psum").sem, 1)

                def body(b, par, first, last):
                    if not last:
                        turn_q(b + 1)
                    out_of(b, par)
                    if not last:
                        hidden_of(b + 1)

                pe.wait_ge(s("w_split").sem, ready_at)
                turn_q(0)
                hidden_of(0)
                for_sequences(pe, body)

            @block.scalar
            def _(a):
                def relus(b):
                    a.wait_ge(*s("hid_lo").at(b, 0))
                    for j in range(NB):
                        a.wait_ge(*s("hid_psum").at(b, j + 1))
                        if b1:
                            for f in (2 * j, 2 * j + 1):
                                a.activation(relu[:, f, :], hidden_bank(core, j)[:, f % 2, :], ACT.Relu,
                                             bias=core.col(b1, f)).then_inc(s("relu").sem, 1)
                        else:
                            a.activation(relu[:, 2 * j:2 * j + 2, :], hidden_bank(core, j), ACT.Relu
                                         ).then_inc(s("relu").sem, 1)

                def body(b, par, first, last):
                    if not last:
                        q.act_rstd(a, b + 1)
                        q.act_hi(a, b + 1, M, s("hid_psum"))
                    fin.act_rstd(a, b)
                    if not last:
                        relus(b + 1)

                a.preload_act_table_set(EXP_LN)
                q.act_rstd(a, 0)
                q.act_hi(a, 0, M, s("hid_psum"))
                relus(0)
                for_sequences(a, body)

            @block.vector
            def _(v):
                def splits(b, par):
                    if not (isinstance(b, int) and b < 2):
                        v.wait_ge(*s("out_psum").at(b - 1, 0))
                    for j in range(NB):
                        t = slice(2 * j, 2 * j + 2)
                        v.wait_ge(*s("relu").at(b, RN * (j + 1)))
                        v.tensor_copy(hh[par][:, t, :], relu[:, t, :]).then_inc(s("hid_hi").sem, 1)
                        v.wait_ge(*s("hid_hi").at(b, j + 1))
                        v.tensor_tensor(hl[par][:, t, :], relu[:, t, :], hh[par][:, t, :].bitcast(F32), ALU.subtract
                                        ).then_inc(s("hid_lo").sem, 1)

                def body(b, par, first, last):
                    if not last:
                        q.dve_stats(v, b + 1)
                        q.dve_norm(v, b + 1)
                        q.dve_lo(v, b + 1, M, s("hid_psum"))
                    fin.dve_read(v, b, O, s("out_psum"), 1)
                    fin.dve_norm(v, b)
                    if not last:
                        splits(b + 1, 1 - par)

                q.dve_stats(v, 0)
                q.dve_norm(v, 0)
                q.dve_lo(v, 0, M, s("hid_psum"))
                if rows_at:
                    v.wait_ge(s("rows_in").sem, rows_at)
                splits(0, 0)
                for_sequences(v, body)
        core.end()


LH = 8
LD = D // LH
LB = P + P // LD


def linear_attention(core, name, q_src, kv_src, g, state, nxt):
    nc = core.nc
    with ExitStack() as ctx:
        core.phase = name
        sb = lambda n, s, t=F32: ctx.enter_context(nc.sbuf_tensor(f"{name}_{n}", s, t))
        wh, wl, rows = weights_of(core, name)
        w_at = lambda m: m * NF * D
        q = Source(core, ctx, "q", "inner", **q_src)
        kv = Source(core, ctx, "kv", "inner", **kv_src) if kv_src else q
        cross = kv is not q
        fin = Finish(core, ctx, "inner", rows, None, g, state)
        ex = sb("ex", [P, NF, S])
        rl = sb("rl", [P, NF, S])
        exk = sb("exk", [P, NT, D])
        rlk = sb("rlk", [P, NT, D])
        qe = [sb(f"qe{i}", [P, NF, S]) for i in range(2)]
        ke = sb("ke", [P, NT, D])
        vo = sb("vo", [P, NT, NF, LB])
        bd = sb("bd", [P, NF, LB])
        z = sb("z", [P, NT, NF, LB - P])
        zr = sb("zr", [P, NT, NF, LB - P])
        ms = sb("ms", [P, NT, D])
        mh = sb("mh", [P, NF, S], F32R)
        ml = sb("ml", [P, NF, S], F32R)
        core.begin(**q.per, **(kv.per if cross else {}), **fin.per, q_psum=1, q_ex=1, q_rl=1, qe=1,
                   k_psum=1, k_ex=1, k_rl=1, ke=1, v_psum=1, vo=1, kv_psum=1, bd=1, msg_psum=1, z=1, zr=1,
                   ms=NT, mt_psum=1, mh=1, ml=1, out_psum=1)
        s = core.s
        M, QB, KB, VB, TM = (bank(core, i) for i in (7, 0, 1, 2, 6))
        KV = core.psum[:, 3, 0:NF * LB].rearrange("p (f c) -> p f c", f=NF)
        MS = core.psum[:, 4:6, 0:NF * LB].rearrange("p t (f c) -> p t f c", f=NF)
        ready_at, rows_at = s("w_split").base, s("rows_in").base
        ones = s("ones")

        with nc.Block() as block:
            @block.sync
            def _(sp):
                sp.nop()

            @block.gpsimd
            def _(pool):
                if nxt:
                    load_group(core, pool, nxt)

            @block.tensor
            def _(pe):
                def free(src, b):
                    pe.wait_ge(*src.sg("lo").at(b, 1))
                    pe.wait_ge(*src.sg("hi").at(b, 1))

                def turn_q(b):
                    if not (isinstance(b, int) and b == 0):
                        free(kv, b - 1)
                    q.pe_turn(pe, b, M)

                def turn_kv(b):
                    free(q, b)
                    kv.pe_turn(pe, b, M)

                def q_proj(b):
                    free(q, b)
                    pe.wait_ge(*s("qe").at(b, 0))
                    project_features(pe, QB, wh, wl, w_at(0), D, q.xh, q.xl, range(NF)).then_inc(s("q_psum").sem, 1)

                def k_proj(b):
                    free(kv, b)
                    pe.wait_ge(*s("ke").at(b, 0))
                    project_tokens(pe, KB, wh, wl, w_at(1), kv.xh, kv.xl).then_inc(s("k_psum").sem, 1)

                def v_proj(b):
                    pe.wait_ge(*s("vo").at(b, 0))
                    project_tokens(pe, VB, wh, wl, w_at(2), kv.xh, kv.xl).then_inc(s("v_psum").sem, 1)

                def kv_product(b):
                    pe.wait_ge(*s("ke").at(b, 1))
                    pe.wait_ge(*s("vo").at(b, 1))
                    pe.wait_ge(*s("bd").at(b, 0))
                    for f in range(NF):
                        for t in range(NT):
                            m = pe.matmul(KV[:, f, :], ke[:, t, f * P:(f + 1) * P], vo[:, t, f, :],
                                          start=(t == 0), stop=(t == NT - 1))
                    m.then_inc(s("kv_psum").sem, 1)

                def message(b, par):
                    pe.wait_ge(*s("bd").at(b, 1))
                    pe.wait_ge(*s("qe").at(b, 1))
                    pe.wait_ge(*s("ms").at(b, 0))
                    for t in range(NT):
                        for f in range(NF):
                            m = pe.matmul(MS[:, t, f, :], qe[par][:, f, t * P:(t + 1) * P], bd[:, f, :],
                                          start=True, stop=True)
                    m.then_inc(s("msg_psum").sem, 1)

                def turn_message(b):
                    pe.wait_ge(*s("ms").at(b, NT))
                    pe.wait_ge(*s("fin_read").at(b, 0))
                    turn(pe, core, TM, ms).then_inc(s("mt_psum").sem, 1)

                def out_proj(b):
                    pe.wait_ge(*s("ml").at(b, 1))
                    project_tokens(pe, TM, wh, wl, w_at(3), mh, ml).then_inc(s("out_psum").sem, 1)

                def body(b, par, first, last):
                    kv_product(b)
                    if not last:
                        turn_q(b + 1)
                    message(b, par)
                    if not last:
                        if cross:
                            turn_kv(b + 1)
                        q_proj(b + 1)
                    turn_message(b)
                    if not last:
                        k_proj(b + 1)
                    out_proj(b)
                    if not last:
                        v_proj(b + 1)

                pe.wait_ge(s("w_split").sem, ready_at)
                turn_q(0)
                if cross:
                    turn_kv(0)
                q_proj(0)
                k_proj(0)
                v_proj(0)
                for_sequences(pe, body)

            @block.scalar
            def _(a):
                def used(src):
                    return s("v_psum") if src is kv else s("q_psum")

                def phi_parts(b, src, psum, ex_, rl_, n):
                    a.wait_ge(*s(f"{n}_psum").at(b, 1))
                    a.wait_ge(*s(f"{n}e").at(b, 0))
                    a.activation(ex_[:, :, :], psum, ACT.Exp).then_inc(s(f"{n}_ex").sem, 1)
                    a.activation(rl_[:, :, :], psum, ACT.Relu).then_inc(s(f"{n}_rl").sem, 1)

                def front(b):
                    q.act_hi(a, b, M, used(q))
                    if cross:
                        kv.act_hi(a, b, M, used(kv))
                    phi_parts(b, q, QB, ex, rl, "q")

                def message_hi(b):
                    a.wait_ge(*s("mt_psum").at(b, 1))
                    a.wait_ge(*s("out_psum").at(b, 0))
                    a.activation(mh[:, :, :], TM, ACT.Copy).then_inc(s("mh").sem, 1)

                def body(b, par, first, last):
                    if not last:
                        front(b + 1)
                    message_hi(b)
                    if not last:
                        phi_parts(b + 1, kv, KB, exk, rlk, "k")
                    fin.act_rstd(a, b)

                a.preload_act_table_set(EXP_LN)
                front(0)
                phi_parts(0, kv, KB, exk, rlk, "k")
                for_sequences(a, body)

            @block.vector
            def _(v):
                def used(src):
                    return s("v_psum") if src is kv else s("q_psum")

                def phi(b, out, ex_, rl_, n):
                    v.wait_ge(*s(f"{n}_rl").at(b, 1))
                    v.wait_ge(*s(f"{n}_ex").at(b, 1))
                    v.scalar_tensor_tensor(out[:, :, :], ex_[:, :, :], 1.0, rl_[:, :, :], ALU.min, ALU.add
                                           ).then_inc(s(f"{n}e").sem, 1)

                def phi_k(b):
                    v.wait_ge(*s("kv_psum").at(b, 0))
                    phi(b, ke, exk, rlk, "k")

                def values(b):
                    v.wait_ge(*s("v_psum").at(b, 1))
                    v.wait_ge(*s("kv_psum").at(b, 0))
                    v.tensor_copy(vo[:, :, :, 0:P], VB.rearrange("p t (f c) -> p t f c", f=NF)).then_inc(s("vo").sem, 1)

                def block_diagonal(b):
                    v.wait_ge(*s("kv_psum").at(b, 1))
                    v.wait_ge(*s("msg_psum").at(b, 0))
                    v.tensor_tensor(bd[:, :, :], KV, core.blocks[:, :].unsqueeze(1).broadcast_to([P, NF, LB]), ALU.mult
                                    ).then_inc(s("bd").sem, 1)

                def message(b):
                    v.wait_ge(*s("msg_psum").at(b, 1))
                    v.wait_ge(*s("zr").at(b, 0))
                    v.tensor_scalar(z[:, :, :, :], MS[:, :, :, P:LB], 1e-6, None, ALU.add).then_inc(s("z").sem, 1)
                    v.wait_ge(*s("z").at(b, 1))
                    v.wait_ge(*s("ms").at(b, 0))
                    v.reciprocal(zr[:, :, :, :], z[:, :, :, :]).then_inc(s("zr").sem, 1)
                    v.wait_ge(*s("zr").at(b, 1))
                    v.wait_ge(*s("mt_psum").at(b, 0))
                    for t in range(NT):
                        v.tensor_tensor(ms[:, t, :].rearrange("p (f j d) -> p f j d", f=NF, d=LD),
                                        MS[:, t, :, 0:P].rearrange("p f (j d) -> p f j d", d=LD),
                                        zr[:, t, :, :].unsqueeze(3).broadcast_to([P, NF, P // LD, LD]), ALU.mult
                                        ).then_inc(s("ms").sem, 1)

                def message_lo(b):
                    v.wait_ge(*s("mh").at(b, 1))
                    v.tensor_tensor(ml[:, :, :], TM, mh[:, :, :].bitcast(F32), ALU.subtract).then_inc(s("ml").sem, 1)

                def body(b, par, first, last):
                    if not last:
                        q.dve_stats(v, b + 1)
                        if cross:
                            kv.dve_stats(v, b + 1)
                    block_diagonal(b)
                    if not last:
                        q.dve_lo(v, b + 1, M, used(q))
                    message(b)
                    if not last:
                        if cross:
                            kv.dve_lo(v, b + 1, M, used(kv))
                        phi(b + 1, qe[1 - par], ex, rl, "q")
                    message_lo(b)
                    if not last:
                        phi_k(b + 1)
                    fin.dve_read(v, b, TM, s("out_psum"), 1)
                    if not last:
                        values(b + 1)
                    fin.dve_norm(v, b)

                v.memset(vo[:, :, :, P:LB], 1.0).then_inc(ones.sem, 1)
                if rows_at:
                    v.wait_ge(s("rows_in").sem, rows_at)
                q.dve_stats(v, 0)
                if cross:
                    kv.dve_stats(v, 0)
                q.dve_lo(v, 0, M, used(q))
                if cross:
                    kv.dve_lo(v, 0, M, used(kv))
                phi(0, qe[0], ex, rl, "q")
                phi_k(0)
                values(0)
                for_sequences(v, body)
        ones.base += 1
        core.end()


def load_expert(core, pool, e, par):
    s, d = core.s, core.d
    n = GSIZE["E0"] // CHUNK
    col0 = GOFF["E0"] + e * GSIZE["E0"]
    wh, wl = core.wh[par], core.wl[par]

    def bring(c):
        pool.wait_ge(*s("xw_split").at(e, max(0, c - STAGES + 1)))
        pool.dma_start(core.stage[:, c % STAGES, :], d["weights"][:, bass.ds(col0 + c * CHUNK, CHUNK)]
                       ).then_inc(s(f"xw_raw{c % STAGES}").sem, 16)

    pool.dma_start(core.rows[par][:, 0:1, :],
                   d["rows"][bass.ds(ROFF["E0"] + e, 1), :].partition_broadcast(P)).then_inc(s("xw_row").sem, 16)
    for c in range(STAGES - 1):
        bring(c)
    for c in range(n):
        if c + STAGES - 1 < n:
            bring(c + STAGES - 1)
        pool.wait_ge(*s(f"xw_raw{c % STAGES}").at(e, 16 * (c // STAGES + 1)))
        st = core.stage[:, c % STAGES, :]
        a, z = c * CHUNK, (c + 1) * CHUNK
        pool.sem_inc(s("xw_seen").sem, 1)
        pool.tensor_copy(wh[:, a:z], st).then_inc(s("xw_hi").sem, 1)
        pool.wait_ge(*s("xw_hi").at(e, c + 1))
        pool.tensor_tensor(wl[:, a:z], st, wh[:, a:z].bitcast(F32), ALU.subtract).then_inc(s("xw_split").sem, 1)
    pool.wait_ge(*s("xw_row").at(e, 16))


def gates(core, ctx, nxt_unused=None):
    nc = core.nc
    sb = lambda n, s, t=F32: ctx.enter_context(nc.sbuf_tensor(f"moe_{n}", s, t))
    xah = sb("xa_hi", [P, NF, B * S], F32R)
    xal = sb("xa_lo", [P, NF, B * S], F32R)
    gate = sb("gate", [P, B * NT, NE])
    with ExitStack() as inner:
        sb = lambda n, s, t=F32: inner.enter_context(nc.sbuf_tensor(f"moe_{n}", s, t))
        q = Source(core, inner, "q", "pre", ln=("L2_xattn_moe_ln_g", "L2_xattn_moe_ln_b"), state=core.X)
        rh = sb("router_hi", [P, NF, NE], F32R)
        rl = sb("router_lo", [P, NF, NE], F32R)
        T = B * NT
        lg = sb("lg", [P, T, NE])
        top = sb("top", [P, T, 8])
        idx = sb("idx", [P, T, 8], U32)
        idf = sb("idf", [P, T, 8])
        dif = sb("dif", [P, T, 1])
        e2 = sb("e2", [P, T, 1])
        dn = sb("dn", [P, T, 1])
        g1 = sb("g1", [P, T, 1])
        g2 = sb("g2", [P, T, 1])
        o1 = sb("o1", [P, T, NE])
        o2 = sb("o2", [P, T, NE])
        core.begin(**q.per, lg_psum=1, lg=1, xa_h=1, xa_l=1)
        s = core.s
        M, L = bank(core, 7), bank(core, 6)
        one = s("gate_step")
        base = one.base

        with nc.Block() as block:
            @block.gpsimd
            def _(pool):
                load_expert(core, pool, 0, 0)

            @block.tensor
            def _(pe):
                def body(b, par, first, last):
                    if not first:
                        pe.wait_ge(*q.sg("lo").at(b, 0))
                    q.pe_turn(pe, b, M)
                    pe.wait_ge(*q.sg("lo").at(b, 1))
                    pe.wait_ge(*s("lg").at(b, 0))
                    for t in range(NT):
                        for k in range(NF):
                            m = three_pass(pe, L[:, t, 0:NE], q.xh[:, k, t * P:(t + 1) * P],
                                           q.xl[:, k, t * P:(t + 1) * P], rh[:, k, :], rl[:, k, :],
                                           k == 0, k == NF - 1)
                    m.then_inc(s("lg_psum").sem, 1)
                pe.wait_ge(one.sem, base + 2)
                for_sequences(pe, body)

            @block.scalar
            def _(a):
                def body(b, par, first, last):
                    q.act_rstd(a, b)
                    q.act_hi(a, b, M, None)
                    cols = bass.ds(b * S, S)
                    a.wait_ge(*q.sg("hi").at(b, 1))
                    a.wait_ge(*q.sg("lo").at(b, 1))
                    a.sem_inc(s("split_seen").sem, 1)
                    a.activation(xah[:, :, cols], q.xh[:, :, :].bitcast(F32), ACT.Copy).then_inc(s("xa_h").sem, 1)
                    a.activation(xal[:, :, cols], q.xl[:, :, :].bitcast(F32), ACT.Copy).then_inc(s("xa_l").sem, 1)
                a.preload_act_table_set(EXP_LN)
                for_sequences(a, body)
                a.wait_ge(one.sem, base + 3)
                a.activation(e2[:, :, :], dif[:, :, :], ACT.Exp).then_inc(s("gate_exp").sem, 1)

            @block.vector
            def _(v):
                def body(b, par, first, last):
                    q.dve_stats(v, b)
                    q.dve_norm(v, b)
                    v.wait_ge(*s("xa_h").at(b, 0))
                    v.wait_ge(*s("xa_l").at(b, 0))
                    q.dve_lo(v, b, M, s("lg_psum"))
                    v.wait_ge(*s("lg_psum").at(b, 1))
                    v.tensor_tensor(lg[:, bass.ds(NT * b, NT), :], L[:, :, 0:NE],
                                    core.router_b[:, :].unsqueeze(1).broadcast_to([P, NT, NE]), ALU.add
                                    ).then_inc(s("lg").sem, 1)
                n = [base]

                def step(ins):
                    n[0] += 1
                    ins.then_inc(one.sem, 1)
                    v.wait_ge(one.sem, n[0])

                step(v.tensor_copy(rh[:, :, :], core.router_w[:, :, :]))
                step(v.tensor_tensor(rl[:, :, :], core.router_w[:, :, :], rh[:, :, :].bitcast(F32), ALU.subtract))
                for_sequences(v, body)
                v.wait_ge(*s("lg").at(B - 1, 1))
                for t in range(T):
                    v.max(top[:, t, :], lg[:, t, :]).then_inc(s("top").sem, 1)
                v.wait_ge(s("top").sem, s("top").base + T)
                for t in range(T):
                    v.max_index(idx[:, t, :], top[:, t, :], lg[:, t, :]).then_inc(s("top").sem, 1)
                step(v.tensor_tensor(dif[:, :, :], top[:, :, 1:2], top[:, :, 0:1], ALU.subtract))
                v.wait_ge(s("top").sem, s("top").base + 2 * T)
                step(v.tensor_copy(idf[:, :, :], idx[:, :, :]))
                v.wait_ge(s("gate_exp").sem, s("gate_exp").base + 1)
                step(v.tensor_scalar(dn[:, :, :], e2[:, :, :], 1.0, None, ALU.add))
                step(v.reciprocal(g1[:, :, :], dn[:, :, :]))
                step(v.tensor_tensor(g2[:, :, :], e2[:, :, :], g1[:, :, :], ALU.mult))
                ids = core.iota[:, :].unsqueeze(1).broadcast_to([P, T, NE])
                for o, g, j in ((o1, g1, 0), (o2, g2, 1)):
                    step(v.tensor_tensor(o[:, :, :], ids, idf[:, :, j:j + 1].broadcast_to([P, T, NE]), ALU.is_equal))
                    step(v.tensor_tensor(o[:, :, :], o[:, :, :], g[:, :, :].broadcast_to([P, T, NE]), ALU.mult))
                step(v.tensor_tensor(gate[:, :, :], o1[:, :, :], o2[:, :, :], ALU.add))
        one.base += 11
        s("top").base += 2 * T
        s("gate_exp").base += 1
        core.end()
    return xah, xal, gate


def experts(core, nxt):
    nc = core.nc
    s = core.s
    core.phase = "moe"
    with ExitStack() as ctx:
        for n, k in dict(xw_split=GSIZE["E0"] // CHUNK, xw_hi=GSIZE["E0"] // CHUNK, xw_row=16, b1e=1).items():
            s(n).begin(k)
        for i in range(STAGES):
            s(f"xw_raw{i}").begin(16 * GSIZE["E0"] // CHUNK // STAGES)
        xah, xal, gate = gates(core, ctx)
        sb = lambda n, s, t=F32: ctx.enter_context(nc.sbuf_tensor(f"moe_{n}", s, t))
        HT = FE // P
        NB = HT // 2
        act = sb("gelu", [P, HT, S])
        hh = [sb(f"hid_hi{i}", [P, HT, S], F32R) for i in range(2)]
        hl = [sb(f"hid_lo{i}", [P, HT, S], F32R) for i in range(2)]
        y = sb("y", [P, NT, D])
        b1e = sb("b1e", [P, HT])
        core.begin(hid_psum=NB, gelu=HT, hid_hi=NB, hid_lo=NB, out_psum=1, y=1, mixed=NT)
        O = bank(core, 6)

        with nc.Block() as block:
            @block.gpsimd
            def _(pool):
                def body(e, par, first, last):
                    if last:
                        pool.wait_ge(*s("mixed").at(B * (NE - 1), 0))
                        pool.wait_ge(*s("xw_split").at(NE - 1, GSIZE["E0"] // CHUNK))
                        load_group(core, pool, nxt)
                    else:
                        if not first:
                            pool.wait_ge(*s("mixed").at(B * e, 0))
                        load_expert(core, pool, e + 1, 1 - par)
                for_sequences(pool, body)

            @block.tensor
            def _(pe):
                def expert(e, ep, first_e, last_e):
                    wh, wl = core.wh[ep], core.wl[ep]

                    def hidden_of(b):
                        n = B * e + b
                        pe.wait_ge(*s("gelu").at(n, 0))
                        for j in range(NB):
                            cols = bass.ds(b * S, S)
                            o = hidden_bank(core, j)
                            for i, f in enumerate((2 * j, 2 * j + 1)):
                                for k in range(NF):
                                    a = k * FE + f * P
                                    m = three_pass(pe, o[:, i, :], wh[:, a:a + P], wl[:, a:a + P],
                                                   xah[:, k, cols], xal[:, k, cols], k == 0, k == NF - 1)
                            m.then_inc(s("hid_psum").sem, 1)

                    def body(b, par, first, last):
                        if not last:
                            hidden_of(b + 1)
                        n = B * e + b
                        pe.wait_ge(*s("hid_lo").at(n, NB))
                        pe.wait_ge(*s("y").at(n, 0))
                        project_tokens(pe, O, wh, wl, NF * FE, hh[par], hl[par], HT).then_inc(s("out_psum").sem, 1)

                    pe.wait_ge(*s("xw_split").at(e, GSIZE["E0"] // CHUNK))
                    hidden_of(0)
                    for_sequences(pe, body)
                for_sequences(pe, expert)

            @block.scalar
            def _(a):
                def expert(e, ep, first_e, last_e):
                    a.wait_ge(*s("gelu").at(B * e, 0))
                    a.sem_inc(s("bias_free").sem, 1)
                    a.activation(b1e[:, :], core.cols[:, bass.ds(COFF["experts"] + HT * e, HT)], ACT.Copy
                                 ).then_inc(s("b1e").sem, 1)
                    a.wait_ge(*s("b1e").at(e, 1))

                    def body(b, par, first, last):
                        n = B * e + b
                        a.wait_ge(*s("hid_lo").at(n, 0))
                        for j in range(NB):
                            a.wait_ge(*s("hid_psum").at(n, j + 1))
                            for f in (2 * j, 2 * j + 1):
                                a.activation(act[:, f, :], hidden_bank(core, j)[:, f % 2, :], ACT.Gelu,
                                             bias=b1e[:, f:f + 1]
                                             ).then_inc(s("gelu").sem, 1)
                    for_sequences(a, body)
                a.preload_act_table_set("gelu_and_others")
                for_sequences(a, expert)

            @block.vector
            def _(v):
                def expert(e, ep, first_e, last_e):
                    def splits(b, par):
                        n = B * e + b
                        for j in range(NB):
                            t = slice(2 * j, 2 * j + 2)
                            v.wait_ge(*s("gelu").at(n, 2 * (j + 1)))
                            v.tensor_copy(hh[par][:, t, :], act[:, t, :]).then_inc(s("hid_hi").sem, 1)
                            v.wait_ge(*s("hid_hi").at(n, j + 1))
                            v.tensor_tensor(hl[par][:, t, :], act[:, t, :], hh[par][:, t, :].bitcast(F32),
                                            ALU.subtract).then_inc(s("hid_lo").sem, 1)

                    def body(b, par, first, last):
                        n = B * e + b
                        if not last:
                            splits(b + 1, 1 - par)
                        v.wait_ge(*s("out_psum").at(n, 1))
                        v.wait_ge(*s("mixed").at(n, 0))
                        v.tensor_tensor(y[:, :, :], O, core.rows[ep][:, 0:1, :].broadcast_to([P, NT, D]), ALU.add
                                        ).then_inc(s("y").sem, 1)
                        v.wait_ge(*s("y").at(n, 1))
                        for t in range(NT):
                            x = core.X[:, NT * b + t, :]
                            v.scalar_tensor_tensor(x, y[:, t, :], gate[:, NT * b + t, bass.ds(e, 1)], x,
                                                   ALU.mult, ALU.add).then_inc(s("mixed").sem, 1)

                    v.wait_ge(*s("xw_split").at(e, GSIZE["E0"] // CHUNK))
                    v.wait_ge(*s("xw_row").at(e, 16))
                    splits(0, 0)
                    for_sequences(v, body)
                for_sequences(v, expert)
        for n in core.begun:
            s(n).end(B * NE)
        for n in ["xw_split", "xw_hi", "xw_row", "b1e"] + [f"xw_raw{i}" for i in range(STAGES)]:
            s(n).end(NE)


def program(nc, d):
    with ExitStack() as ctx:
        core = Core(nc, ctx, d)
        s = core.s
        sb = lambda n, sh, t=F32: ctx.enter_context(nc.sbuf_tensor(n, sh, t))
        core.eps = sb("eps", [P, 1])
        core.blocks = sb("blocks", [P, LB])
        core.router_w = sb("router_w", [P, NF, NE])
        core.router_b = sb("router_b", [P, NE])
        core.iota = sb("iota", [P, NE])
        core.raw_sems = [s(f"w_raw{i}") for i in range(STAGES)]

        with nc.Block() as block:
            @block.sync
            def _(sp):
                for dst, src in ((core.X[:, :, :], d["x"]), (core.cols[:, :], d["cols"]), (core.ident[:, :], d["ident"]),
                                 (core.tri[:, :], d["tri"]), (core.blocks[:, :], d["blocks"]),
                                 (core.router_w[:, :, :], d["router_w"]),
                                 (core.router_b[:, :], d["router_b"].partition_broadcast(P)),
                                 (core.iota[:, :], d["iota"].partition_broadcast(P))):
                    sp.dma_start(dst, src).then_inc(s("first_loads").sem, 16)
                sp.wait_ge(s("first_loads").sem, 8 * 16)

            @block.gpsimd
            def _(pool):
                load_group(core, pool, "L0s")

            @block.vector
            def _(v):
                v.memset(core.eps[:, :], EPS).then_inc(s("set_up").sem, 1)
                v.wait_ge(s("first_loads").sem, 8 * 16)
                v.tensor_copy(core.ident_bf[:, :], core.ident[:, :]).then_inc(s("set_up").sem, 1)
                v.tensor_copy(core.tri_bf[:, :], core.tri[:, :]).then_inc(s("set_up").sem, 1)
                for i, n in enumerate(BQS):
                    v.tensor_scalar(core.bq4[:, i, :], core.cols[:, COFF[n]:COFF[n] + NF], DH ** -0.5, None, ALU.mult
                                    ).then_inc(s("set_up").sem, 1)

        bq = lambda i: (lambda f: core.bq4[:, i, f:f + 1])
        bk = lambda n: (lambda f: core.col(n, f))
        X = core.X
        attention(core, "L0s", dict(state=X), None, bq(0), bk("L0_xattn_sa_bk"), "post", 2, "self", "L0c")
        attention(core, "L0c", dict(state=X), dict(dram=d["ctx"]), bq(1), bk("L0_xattn_ca_bk"), "post", 2, "keys", "L0f")
        feed_forward(core, "L0f", dict(state=X), 1024, "L0_xattn_ffn_b1", "post", 0, 1, X, "L1e")
        with ExitStack() as l1:
            C = l1.enter_context(nc.sbuf_tensor("C", [P, B * NT, D], F32))
            with nc.Block() as block:
                @block.sync
                def _(sp):
                    sp.dma_start(C[:, :, :], d["ctx"]).then_inc(s("ctx_in").sem, 16)

                @block.vector
                def _(v):
                    v.wait_ge(s("ctx_in").sem, 16)
                    v.tensor_tensor(C[:, :, :], C[:, :, :], C[:, :, :], ALU.add).then_inc(s("set_up").sem, 1)
            linear_attention(core, "L1e", dict(state=C), None, 0, C, "L1ef")
            feed_forward(core, "L1ef", dict(state=C), 512, None, "inner", None, 0, C, "L1s")
            linear_attention(core, "L1s", dict(state=X), None, 0, X, "L1c")
            linear_attention(core, "L1c", dict(state=X), dict(state=C), 0, X, "L1df")
            feed_forward(core, "L1df", dict(state=X), 512, None, "inner", None, 0, X, "L2s")
        ln = lambda n: (n + "_g", n + "_b")
        attention(core, "L2s", dict(state=X, ln=ln("L2_xattn_sa_ln")), None, bq(2), bk("@L2_xattn_sa_in_b:1"),
                  "pre", 0, None, "L2c")
        attention(core, "L2c", dict(state=X, ln=ln("L2_xattn_ca_q_ln")),
                  dict(dram=d["ctx"], ln=ln("L2_xattn_ca_kv_ln")), bq(3), bk("@L2_xattn_ca_in_b:1"),
                  "pre", 0, None, None)
        experts(core, "L3s")
        attention(core, "L3s", dict(state=X, ln=ln("L3_xattn_ln1")), None, bq(4), bk("L3_xattn_mmha_wk_b"),
                  "pre", 0, "causal", "L3c")
        attention(core, "L3c", dict(state=X, ln=ln("L3_xattn_ln2")), dict(dram=d["ctx"]), bq(5),
                  bk("L3_xattn_mha_wk_b"), "pre", 0, None, "L3f")
        feed_forward(core, "L3f", dict(state=X, ln=ln("L3_xattn_ln3")), 1024, "L3_xattn_ffn_b1", "pre", 0, 0, X, None)
        with nc.Block() as block:
            @block.sync
            def _(sp):
                sp.dma_start(d["out"], X[:, :, :]).then_inc(s("stored").sem, 16)
                sp.wait_ge(s("stored").sem, 16)


def token_tiles(a):
    return np.ascontiguousarray(a.reshape(B * NT, P, a.shape[-1]).transpose(1, 0, 2))


def operand(w):
    i, o = w.shape
    return w.reshape(i // P, P, o).transpose(1, 0, 2).reshape(P, -1)


def kernel(**inputs):
    import concourse.bacc as bacc
    from concourse.bass_utils import run_bass_kernel_spmd as launch

    a = {n: np.asarray(v) for n, v in inputs.items()}

    def vec(n):
        if n[0] == "@":
            n, j = n[1:].split(":")
            return a[n][int(j) * D:(int(j) + 1) * D]
        if n[0] == "#":
            n, j = n[1:].split(":")
            return a[n][int(j)]
        return a[n]

    w = []
    for x in ("sa", "ca"):
        w += [operand(a[f"L0_xattn_{x}_w{m}"].T) for m in "qkvo"]
    w += [operand(a["L0_xattn_ffn_w1"].T), operand(a["L0_xattn_ffn_w2"].T)]
    w += [operand(a[f"L1_xattn_e_w{m}"]) for m in "qkvm12"]
    for j in "01":
        w += [operand(a[f"L1_xattn_d_w{m}{j}"]) for m in "qkvm"]
    w += [operand(a["L1_xattn_d_w1"]), operand(a["L1_xattn_d_w2"])]
    for x in ("sa", "ca"):
        w += [operand(a[f"L2_xattn_{x}_in_w"][m * D:(m + 1) * D].T) for m in range(3)]
        w += [operand(a[f"L2_xattn_{x}_out_w"].T)]
    for e in range(NE):
        w += [operand(a["L2_xattn_e_fc1_w"][e].T), operand(a["L2_xattn_e_fc2_w"][e].T)]
    for x in ("mmha", "mha"):
        w += [operand(a[f"L3_xattn_{x}_w{m}"]) for m in "qkvo"]
    w += [operand(a["L3_xattn_ffn_w1"]), operand(a["L3_xattn_ffn_w2"])]

    cols = [vec(n).reshape(NF, P).T for n in COLS]
    cols += [a["L0_xattn_ffn_b1"].reshape(-1, P).T, a["L3_xattn_ffn_b1"].reshape(-1, P).T]
    cols += [a["L2_xattn_e_fc1_b"].reshape(-1, P).T]
    data = {
        "x": token_tiles(a["x"]), "ctx": token_tiles(a["ctx_1024"]),
        "mask_self": token_tiles(a["mask_Bx1xSxS2_if1"][:, 0]),
        "mask_keys": np.ascontiguousarray(a["mask_Bx1x1xS2_if1"].reshape(B, S)),
        "weights": np.ascontiguousarray(np.concatenate(w, axis=1)),
        "rows": np.stack([vec(n) for r in ROWS.values() for n in r]),
        "cols": np.ascontiguousarray(np.concatenate(cols, axis=1)),
        "router_w": np.ascontiguousarray(a["L2_xattn_router_w"].T.reshape(NF, P, NE).transpose(1, 0, 2)),
        "router_b": a["L2_xattn_router_b"],
        "ident": np.eye(P, dtype=np.float32),
        "tri": np.triu(np.full((P, P), MASKED, np.float32), 1),
        "blocks": np.ascontiguousarray(np.concatenate(
            [np.kron(np.eye(P // LD), np.ones((LD, LD))), np.kron(np.eye(P // LD), np.ones((LD, 1)))], axis=1
        ).astype(np.float32)),
        "iota": np.arange(NE, dtype=np.float32),
    }
    nc = bacc.Bacc("TRN2", target_bir_lowering=False, num_devices=1)
    d = {n: nc.dram_tensor(f"in_{n}", v.shape, mybir.dt.from_np(v.dtype), kind="ExternalInput").ap()
         for n, v in data.items()}
    d["out"] = nc.dram_tensor("out_0", (P, B * NT, D), F32, kind="ExternalOutput").ap()
    program(nc, d)
    r = launch(nc, [{f"in_{n}": v for n, v in data.items()}], core_ids=[0])
    got = r.results[0]["out_0"]
    return np.ascontiguousarray(got.transpose(1, 0, 2)).reshape(B, S, D)
```

```python
from contextlib import ExitStack

import numpy as np

import concourse.bass as bass
from concourse import mybir

F32 = mybir.dt.float32
F32R = mybir.dt.float32r
BF16 = mybir.dt.bfloat16
I32 = mybir.dt.int32
U32 = mybir.dt.uint32
ALU = mybir.AluOpType
ACT = mybir.ActivationFunctionType
AX = mybir.AxisListType

P = 128
B = 8
S = 256
D = 256
NT = S // P
NF = D // P
H = 16
DH = D // H
NE = 8
FE = 1024
EPS = 1e-5
EXP_LN = "natural_log_exp_and_others"
MASKED = -float(2 ** 100)
CHUNK = 512
STAGES = 4


class Signal:

    def __init__(self, nc, ctx, name):
        self.sem = ctx.enter_context(nc.semaphore(name))
        self.base = 0
        self.per = 0

    def begin(self, per):
        self.per = per

    def end(self, n=B):
        self.base += self.per * n
        self.per = 0

    def at(self, b, k):
        return self.sem, b * self.per + (self.base + k)


def for_sequences(eng, body):
    body(0, 0, True, False)
    with eng.Fori(0, (B - 2) // 2) as i:
        body(2 * i + 1, 1, False, False)
        body(2 * i + 2, 0, False, False)
    body(B - 1, 1, False, True)


def for_sequences_ahead(eng, body):
    body(0, 0, True, 2)
    with eng.Fori(0, (B - 4) // 2) as i:
        body(2 * i + 1, 1, False, 2)
        body(2 * i + 2, 0, False, 2)
    for b in range(B - 3, B):
        body(b, b % 2, False, min(2, B - 1 - b))


ATT = ("att", 4 * NF * D)
GROUPS = [("L0s", 4 * NF * D), ("L0c", 4 * NF * D), ("L0f", 2 * 4 * NF * D),
          ("L1e", 4 * NF * D), ("L1ef", 2 * 2 * NF * D), ("L1s", 4 * NF * D), ("L1c", 4 * NF * D),
          ("L1df", 2 * 2 * NF * D), ("L2s", 4 * NF * D), ("L2c", 4 * NF * D)] + \
         [(f"E{e}", 2 * 4 * NF * D) for e in range(NE)] + \
         [("L3s", 4 * NF * D), ("L3c", 4 * NF * D), ("L3f", 2 * 4 * NF * D)]
GOFF = {}
_o = 0
for _n, _c in GROUPS:
    GOFF[_n] = _o
    _o += _c
WCOLS = _o
GSIZE = dict(GROUPS)
GINDEX = {n: i for i, (n, _) in enumerate(GROUPS)}

ROWS = {"L0s": ["L0_xattn_sa_bv", "L0_xattn_sa_bo", "L0_xattn_ln1_g", "L0_xattn_ln1_b"],
        "L0c": ["L0_xattn_ca_bv", "L0_xattn_ca_bo", "L0_xattn_ln2_g", "L0_xattn_ln2_b"],
        "L0f": ["L0_xattn_ffn_b2", "L0_xattn_ln3_g", "L0_xattn_ln3_b"],
        "L1e": ["L1_xattn_e_g1", "L1_xattn_e_b1"], "L1ef": ["L1_xattn_e_g2", "L1_xattn_e_b2"],
        "L1s": ["L1_xattn_d_g0", "L1_xattn_d_b0"], "L1c": ["L1_xattn_d_g1", "L1_xattn_d_b1"],
        "L1df": ["L1_xattn_d_g2", "L1_xattn_d_b2"],
        "L2s": ["@L2_xattn_sa_in_b:2", "L2_xattn_sa_out_b"],
        "L2c": ["@L2_xattn_ca_in_b:2", "L2_xattn_ca_out_b"],
        "E0": ["#L2_xattn_e_fc2_b:%d" % e for e in range(NE)],
        "L3s": ["L3_xattn_mmha_wv_b", "L3_xattn_mmha_wo_b"],
        "L3c": ["L3_xattn_mha_wv_b", "L3_xattn_mha_wo_b"],
        "L3f": ["L3_xattn_ffn_b2"]}
ROFF = {}
_o = 0
for _n, _r in ROWS.items():
    ROFF[_n] = _o
    _o += len(_r)
NROWS = _o
MAXROWS = 4

COLS = ["L0_xattn_sa_bq", "L0_xattn_sa_bk", "L0_xattn_ca_bq", "L0_xattn_ca_bk",
        "@L2_xattn_sa_in_b:0", "@L2_xattn_sa_in_b:1", "@L2_xattn_ca_in_b:0", "@L2_xattn_ca_in_b:1",
        "L3_xattn_mmha_wq_b", "L3_xattn_mmha_wk_b", "L3_xattn_mha_wq_b", "L3_xattn_mha_wk_b",
        "L2_xattn_sa_ln_g", "L2_xattn_sa_ln_b", "L2_xattn_ca_q_ln_g", "L2_xattn_ca_q_ln_b",
        "L2_xattn_ca_kv_ln_g", "L2_xattn_ca_kv_ln_b", "L2_xattn_moe_ln_g", "L2_xattn_moe_ln_b",
        "L3_xattn_ln1_g", "L3_xattn_ln1_b", "L3_xattn_ln2_g", "L3_xattn_ln2_b",
        "L3_xattn_ln3_g", "L3_xattn_ln3_b"]
COFF = {}
_o = 0
for _n in COLS:
    COFF[_n] = _o
    _o += NF
for _n in ("L0_xattn_ffn_b1", "L3_xattn_ffn_b1"):
    COFF[_n] = _o
    _o += 8
COFF["experts"] = _o
_o += NE * FE // P
NCOLS = _o
BQS = ["L0_xattn_sa_bq", "L0_xattn_ca_bq", "@L2_xattn_sa_in_b:0", "@L2_xattn_ca_in_b:0",
       "L3_xattn_mmha_wq_b", "L3_xattn_mha_wq_b"]


class Core:

    def __init__(self, nc, ctx, d):
        self.nc, self.d = nc, d
        sb = lambda n, s, t=F32: ctx.enter_context(nc.sbuf_tensor(n, s, t))
        self.X = sb("X", [P, B * NT, D])
        self.wh = [sb(f"w_hi{i}", [P, 4096], F32R) for i in range(2)]
        self.wl = [sb(f"w_lo{i}", [P, 4096], F32R) for i in range(2)]
        self.stage = sb("w_stage", [P, STAGES, CHUNK])
        self.rows = [sb(f"rows{i}", [P, MAXROWS, D]) for i in range(2)]
        self.cols = sb("cols", [P, NCOLS])
        self.bq4 = sb("bq4", [P, len(BQS), NF])
        self.ident = sb("ident", [P, P])
        self.ident_bf = sb("ident_bf", [P, P], BF16)
        self.tri = sb("tri", [P, P])
        self.tri_bf = sb("tri_bf", [P, P], BF16)
        self.psum = ctx.enter_context(nc.psum_tensor("psum", [P, 8, 512], F32))
        self.sig = {}
        self.ctx = ctx
        self.begun = []
        self.phase = ""

    def s(self, name):
        if name not in self.sig:
            self.sig[name] = Signal(self.nc, self.ctx, name)
        return self.sig[name]

    def begin(self, **per):
        for n, k in per.items():
            self.s(n).begin(k)
        self.begun = list(per)
        return [self.s(n) for n in per]

    def end(self):
        for n in self.begun:
            self.s(n).end()

    def col(self, name, j):
        c = COFF[name] + j
        return self.cols[:, c:c + 1]


def load_group(core, pool, name):
    nc, d = core.nc, core.d
    g = GINDEX[name]
    par = g % 2
    n = GSIZE[name] // CHUNK
    raw, hi_done, split = core.s("w_raw"), core.s("w_hi_done"), core.s("w_split")
    wh, wl = core.wh[par], core.wl[par]
    if name in ROWS and name != "E0":
        nr = len(ROWS[name])
        src = d["rows"][ROFF[name]:ROFF[name] + nr, :].partition_broadcast(P)
        pool.dma_start(core.rows[par][:, 0:nr, :], src).then_inc(core.s("rows_in").sem, 16)

    def bring(c):
        if split.base + c - STAGES + 1 > 0:
            pool.wait_ge(split.sem, split.base + c - STAGES + 1)
        pool.dma_start(core.stage[:, c % STAGES, :],
                       d["weights"][:, GOFF[name] + c * CHUNK:GOFF[name] + (c + 1) * CHUNK]
                       ).then_inc(core.raw_sems[c % STAGES].sem, 16)

    for c in range(min(STAGES - 1, n)):
        bring(c)
    for c in range(n):
        if c + STAGES - 1 < n:
            bring(c + STAGES - 1)
        slot = core.raw_sems[c % STAGES]
        slot.base += 16
        pool.wait_ge(slot.sem, slot.base)
        st = core.stage[:, c % STAGES, :]
        a, z = c * CHUNK, (c + 1) * CHUNK
        if name in ("L0s", "L0c", "L2s", "L2c", "L3s", "L3c") and c == 0:
            sc = core.s("w_scaled")
            pool.tensor_scalar(st, st, DH ** -0.5, None, ALU.mult).then_inc(sc.sem, 1)
            sc.base += 1
            pool.wait_ge(sc.sem, sc.base)
        pool.tensor_copy(wh[:, a:z], st).then_inc(hi_done.sem, 1)
        hi_done.base += 1
        pool.wait_ge(hi_done.sem, hi_done.base)
        pool.tensor_tensor(wl[:, a:z], st, wh[:, a:z].bitcast(F32), ALU.subtract).then_inc(split.sem, 1)
    split.base += n
    if name in ROWS and name != "E0":
        rin = core.s("rows_in")
        rin.base += 16
        pool.wait_ge(rin.sem, rin.base)


def weights_of(core, name):
    par = GINDEX[name] % 2
    return core.wh[par], core.wl[par], core.rows[par]


def three_pass(pe, out, lh, ll, rh, rl, first, last):
    pe.matmul(out, lh, rh, start=first, stop=False)
    pe.matmul(out, lh, rl, start=False, stop=False)
    return pe.matmul(out, ll, rh, start=False, stop=last)


def project_features(pe, out, wh, wl, off, width, xh, xl, tiles, n=S):
    for j, f in enumerate(tiles):
        for k in range(NF):
            a = off + k * width + f * P
            m = three_pass(pe, out[:, j, 0:n], wh[:, a:a + P], wl[:, a:a + P], xh[:, k, :], xl[:, k, :],
                           k == 0, k == NF - 1)
    return m


def project_tokens(pe, out, wh, wl, off, xh, xl, nk=NF):
    for t in range(NT):
        for k in range(nk):
            a = off + k * D
            m = three_pass(pe, out[:, t, :], xh[:, k, t * P:(t + 1) * P], xl[:, k, t * P:(t + 1) * P],
                           wh[:, a:a + D], wl[:, a:a + D], k == 0, k == nk - 1)
    return m


def turn(pe, core, out, x):
    for t in range(NT):
        for f in range(NF):
            m = pe.transpose(out[:, f, t * P:(t + 1) * P], x[:, t, f * P:(f + 1) * P], core.ident[:, :])
    return m


def bank(core, i):
    return core.psum[:, i, :].rearrange("p (a n) -> p a n", a=2)


class Source:

    def __init__(self, core, ctx, tag, kind, ln=None, state=None, dram=None):
        nc = core.nc
        sb = lambda n, s, t=F32: ctx.enter_context(nc.sbuf_tensor(f"{core.phase}_{tag}_{n}", s, t))
        self.core, self.tag, self.ln, self.state, self.dram = core, tag, ln, state, dram
        self.x_in = sb("in", [P, NT, D])
        self.raw = sb("raw", [P, NT, D]) if dram is not None and ln else None
        self.xh = sb("hi", [P, NF, S], F32R)
        self.xl = sb("lo", [P, NF, S], F32R)
        if ln:
            self.full = sb("full", [P, NF, S])
            self.stats = sb("stats", [P, NT, 6])
            self.mv = sb("mv", [P, NT, 2])
            self.lnv = sb("lnv", [P, NT])
            self.rstd = sb("rstd", [P, NT])
        per = {f"{tag}_in": NT if ln else 1, f"{tag}_turned": 1, f"{tag}_hi": NF if ln else 1, f"{tag}_lo": 1}
        if dram is not None:
            per[f"{tag}_load" if ln else f"{tag}_in"] = 16
        if ln:
            per.update({f"{tag}_stats": NT, f"{tag}_mv": NT, f"{tag}_aggr": 1, f"{tag}_lnv": 1, f"{tag}_rstd": 1, f"{tag}_full": NF})
            per[f"{tag}_hi"] = 1
        self.per = per

    def sg(self, n):
        return self.core.s(f"{self.tag}_{n}")

    def load(self, sp, b):
        if self.dram is None:
            return
        if self.ln:
            sp.wait_ge(*self.sg("in").at(b, 0))
            sp.dma_start(self.raw[:, :, :], self.dram[:, bass.ds(NT * b, NT), :]).then_inc(self.sg("load").sem, 16)
        else:
            sp.wait_ge(*self.sg("turned").at(b, 0))
            sp.dma_start(self.x_in[:, :, :], self.dram[:, bass.ds(NT * b, NT), :]).then_inc(self.sg("in").sem, 16)

    def src(self, b, t=None):
        if self.raw is not None:
            return self.raw[:, :, :] if t is None else self.raw[:, t, :]
        return self.state[:, bass.ds(NT * b, NT), :] if t is None else self.state[:, NT * b + t, :]

    def dve_stats(self, v, b):
        if self.ln is None:
            if self.dram is None:
                v.wait_ge(*self.sg("turned").at(b, 0))
                v.tensor_copy(self.x_in[:, :, :], self.src(b)).then_inc(self.sg("in").sem, 1)
            return
        if self.raw is not None:
            v.wait_ge(*self.sg("load").at(b, 16))
        for t in range(NT):
            v.bn_stats(self.stats[:, t, :], self.src(b, t)).then_inc(self.sg("stats").sem, 1)
        v.wait_ge(*self.sg("stats").at(b, NT))
        v.wait_ge(*self.sg("rstd").at(b, 0))
        v.sem_inc(self.sg("aggr").sem, 1)
        for t in range(NT):
            v.bn_aggr(self.mv[:, t, :], self.stats[:, t, :]).then_inc(self.sg("mv").sem, 1)

    def act_rstd(self, a, b):
        if self.ln is None:
            return
        a.wait_ge(*self.sg("mv").at(b, NT))
        a.activation(self.lnv[:, :], self.mv[:, :, 1], ACT.Ln, bias=self.core.eps[:, 0:1]).then_inc(self.sg("lnv").sem, 1)
        a.wait_ge(*self.sg("lnv").at(b, 1))
        a.wait_ge(*self.sg("in").at(b, 0))
        a.activation(self.rstd[:, :], self.lnv[:, :], ACT.Exp, scale=-0.5).then_inc(self.sg("rstd").sem, 1)

    def dve_norm(self, v, b):
        if self.ln is None:
            return
        v.wait_ge(*self.sg("rstd").at(b, 1))
        v.wait_ge(*self.sg("turned").at(b, 0))
        for t in range(NT):
            v.tensor_scalar(self.x_in[:, t, :], self.src(b, t), self.mv[:, t, 0:1], self.rstd[:, t:t + 1],
                            ALU.subtract, ALU.mult).then_inc(self.sg("in").sem, 1)

    def pe_turn(self, pe, b, out):
        pe.wait_ge(*self.sg("in").at(b, self.sg("in").per))
        turn(pe, self.core, out, self.x_in).then_inc(self.sg("turned").sem, 1)

    def act_hi(self, a, b, src, used):
        a.wait_ge(*self.sg("turned").at(b, 1))
        if self.ln is None:
            a.wait_ge(*used.at(b, 0))
            a.activation(self.xh[:, :, :], src, ACT.Copy).then_inc(self.sg("hi").sem, 1)
            return
        a.wait_ge(*self.sg("lo").at(b, 0))
        for f in range(NF):
            a.activation(self.full[:, f, :], src[:, f, :], ACT.Identity, bias=self.core.col(self.ln[1], f),
                         scale=self.core.col(self.ln[0], f)).then_inc(self.sg("full").sem, 1)

    def dve_lo(self, v, b, src, used):
        if self.ln is None:
            v.wait_ge(*self.sg("hi").at(b, 1))
            v.wait_ge(*used.at(b, 0))
            v.tensor_tensor(self.xl[:, :, :], src, self.xh[:, :, :].bitcast(F32), ALU.subtract
                            ).then_inc(self.sg("lo").sem, 1)
            return
        v.wait_ge(*self.sg("full").at(b, NF))
        v.wait_ge(*used.at(b, 0))
        v.tensor_copy(self.xh[:, :, :], self.full[:, :, :]).then_inc(self.sg("hi").sem, 1)
        v.wait_ge(*self.sg("hi").at(b, 1))
        v.tensor_tensor(self.xl[:, :, :], self.full[:, :, :], self.xh[:, :, :].bitcast(F32), ALU.subtract
                        ).then_inc(self.sg("lo").sem, 1)


class Finish:

    def __init__(self, core, ctx, kind, rows, bias, g, state):
        nc = core.nc
        sb = lambda n, s, t=F32: ctx.enter_context(nc.sbuf_tensor(f"{core.phase}_fin_{n}", s, t))
        self.core, self.kind, self.rows, self.bias, self.g, self.state = core, kind, rows, bias, g, state
        self.y = sb("y", [P, NT, D])
        self.z = sb("z", [P, NT, D]) if kind != "pre" else None
        if kind != "pre":
            self.stats = sb("stats", [P, NT, 6])
            self.mv = sb("mv", [P, NT, 2])
            self.lnv = sb("lnv", [P, NT])
            self.rstd = sb("rstd", [P, NT])
        self.per = {"fin_read": 1, "fin_done": NT if kind == "post" else 1}
        if kind != "pre":
            self.per["fin_y" if kind == "post" else "fin_scaled"] = 1 if kind == "post" else NT
            self.per.update({"fin_stats": NT, "fin_aggr": 1, "fin_mv": NT, "fin_lnv": 1, "fin_rstd": 1,
                             "fin_norm": NT})

    def row(self, r):
        return self.rows[:, r:r + 1, :].broadcast_to([P, NT, D])

    def act_read(self, a, b, out, out_sig, out_n):
        s = self.core.s
        if self.kind != "inner":
            return
        a.wait_ge(*out_sig.at(b, out_n))
        a.wait_ge(*s("fin_norm").at(b, 0))
        a.activation(self.y[:, :, :], out, ACT.Copy).then_inc(s("fin_read").sem, 1)

    def dve_read(self, v, b, out, out_sig, out_n):
        s = self.core.s
        x = self.state[:, bass.ds(NT * b, NT), :]
        if self.kind == "inner":
            v.wait_ge(*s("fin_read").at(b, 1))
        else:
            v.wait_ge(*out_sig.at(b, out_n))
            v.wait_ge(*s("fin_done").at(b, 0))
            v.tensor_tensor(self.y[:, :, :], out, self.row(self.bias), ALU.add).then_inc(s("fin_read").sem, 1)
            v.wait_ge(*s("fin_read").at(b, 1))
        if self.kind == "pre":
            v.tensor_tensor(x, x, self.y[:, :, :], ALU.add).then_inc(s("fin_done").sem, 1)
            return
        if self.kind == "post":
            v.tensor_tensor(self.y[:, :, :], self.y[:, :, :], x, ALU.add).then_inc(s("fin_y").sem, 1)
            v.wait_ge(*s("fin_y").at(b, 1))
        for t in range(NT):
            v.bn_stats(self.stats[:, t, :], self.y[:, t, :]).then_inc(s("fin_stats").sem, 1)
        v.wait_ge(*s("fin_stats").at(b, NT))
        v.sem_inc(s("fin_aggr").sem, 1)
        for t in range(NT):
            v.bn_aggr(self.mv[:, t, :], self.stats[:, t, :]).then_inc(s("fin_mv").sem, 1)

    def act_rstd(self, a, b):
        s = self.core.s
        if self.kind == "pre":
            return
        a.wait_ge(*s("fin_mv").at(b, NT))
        a.activation(self.lnv[:, :], self.mv[:, :, 1], ACT.Ln, bias=self.core.eps[:, 0:1]).then_inc(s("fin_lnv").sem, 1)
        a.wait_ge(*s("fin_lnv").at(b, 1))
        a.activation(self.rstd[:, :], self.lnv[:, :], ACT.Exp, scale=-0.5).then_inc(s("fin_rstd").sem, 1)

    def dve_norm(self, v, b):
        s = self.core.s
        if self.kind == "pre":
            return
        v.wait_ge(*s("fin_mv").at(b, NT))
        for t in range(NT):
            v.scalar_tensor_tensor(self.z[:, t, :], self.y[:, t, :], self.mv[:, t, 0:1], self.rows[:, self.g, :],
                                   ALU.subtract, ALU.mult).then_inc(s("fin_norm").sem, 1)
        v.wait_ge(*s("fin_rstd").at(b, 1))
        v.wait_ge(*s("fin_norm").at(b, NT))
        for t in range(NT):
            out = self.state[:, NT * b + t, :] if self.kind == "post" else self.z[:, t, :]
            v.scalar_tensor_tensor(out, self.z[:, t, :], self.rstd[:, t:t + 1], self.rows[:, self.g + 1, :],
                                   ALU.mult, ALU.add
                                   ).then_inc(s("fin_done" if self.kind == "post" else "fin_scaled").sem, 1)
        if self.kind == "inner":
            x = self.state[:, bass.ds(NT * b, NT), :]
            v.wait_ge(*s("fin_scaled").at(b, NT))
            v.tensor_tensor(x, x, self.z[:, :, :], ALU.add).then_inc(s("fin_done").sem, 1)


def attention(core, name, q_src, kv_src, bq, bk, kind, g, mask, nxt):
    nc = core.nc
    with ExitStack() as ctx:
        core.phase = name
        sb = lambda n, s, t=F32: ctx.enter_context(nc.sbuf_tensor(f"{name}_{n}", s, t))
        wh, wl, rows = weights_of(core, name)
        w_at = lambda m: m * NF * D
        q = Source(core, ctx, "q", kind, **q_src)
        kv = Source(core, ctx, "kv", kind, **kv_src) if kv_src else q
        cross = kv is not q
        G8 = H // NF
        qh = [sb(f"qh{i}", [P, NF, S], F32R) for i in range(2)]
        ql = [sb(f"ql{i}", [P, NF, S], F32R) for i in range(2)]
        k2 = sb("k2", [P, NF, 2, S], F32R)
        kh, kl = k2[:, :, 0, :], k2[:, :, 1, :]
        kx = sb("kx", [P, NF, 2, G8, S], F32R)
        vx = [sb(f"vx{i}", [P, NT, H // 2, 2, 2 * DH]) for i in range(2)]
        e = sb("e", [P, 2, NT, 2, S])
        et = sb("et", [P, G8, NT, S])
        neg = sb("neg", [P, 2, NT, 2])
        den = sb("den", [P, 2, NT, H])
        rcp = sb("rcp", [P, NT, H])
        rcpx = sb("rcpx", [P, NT, H, DH])
        rt = sb("rt", [P, NF, S])
        on = sb("on", [P, NF, S])
        oh = sb("oh", [P, NF, S], F32R)
        ol = sb("ol", [P, NF, S], F32R)
        fin = Finish(core, ctx, kind, rows, 1, g, core.X)
        if mask in ("self", "keys"):
            mt = NT if mask == "self" else 1
            mi = sb("mi", [P, mt, S], I32)
            mb = [sb(f"mb{i}", [P, mt, S], BF16) for i in range(2)]
        U = H // 2
        keys_of = [P, S] if mask == "causal" else [S, S]
        NE_ = 2 * NT
        ETN = 2 if mask == "causal" else 1
        core.begin(**q.per, **(kv.per if cross else {}), **fin.per,
                   q_psum=1, qh=NF, ql=NF, k_psum=1, kh=NF, kl=NF, kx0=G8 * 16, kx1=G8 * 16, v_psum=1, vx=2,
                   scores=U, neg=(2 if mask == "causal" else 1) * U, exps=NE_ * U, et_psum=U,
                   et_v=ETN * U, et_a=ETN * U, pv=NF, rcp=1, rcpx=1, rt_psum=1, rt=1, on=1, oh=1, ol=1,
                   out_psum=1, mask_in=16 if mask in ("self", "keys") else 0, mask_b=1)
        s = core.s
        NEG = s("neg").per // U
        M = bank(core, 7)
        O = bank(core, 6)
        SC = [core.psum[:, 2 * i:2 * i + 2, :].rearrange("p t (h k) -> p t h k", h=2) for i in range(2)]
        ET = core.psum[:, 4:6, :].rearrange("p h (t q) -> p h t q", t=NT)
        kv_used = s("v_psum")
        kx_zero, vx_zero = s("kx_zero"), s("vx_zero")
        ready = core.s("w_split")
        ready_at = ready.base
        rows_at = core.s("rows_in").base

        with nc.Block() as block:
            @block.sync
            def _(sp):
                def kx_dma(b, ft):
                    for i in range(G8):
                        r = slice(DH * i, DH * (i + 1))
                        sp.dma_start(kx[r, ft, :, i, :].bitcast(F32), k2[r, ft, :, :].bitcast(F32)).then_inc(s(f"kx{ft}").sem, 16)

                def inputs(b):
                    q.load(sp, b)
                    if cross:
                        kv.load(sp, b)
                    if mask == "self" or mask == "keys":
                        sp.wait_ge(*s("mask_b").at(b, 0))
                        src = (core.d["mask_self"][:, bass.ds(NT * b, NT), :] if mask == "self" else
                               core.d["mask_keys"][bass.ds(b, 1), :].partition_broadcast(P))
                        sp.dma_start(mi[:, :, :], src).then_inc(s("mask_in").sem, 16)

                def body(b, par, first, last):
                    if not last:
                        inputs(b + 1)
                        nb = b + 1
                        sp.wait_ge(*s("kh").at(nb, NF))
                        sp.wait_ge(*s("kl").at(nb, NF))
                        sp.wait_ge(*s("scores").at(b, U // NF))
                        kx_dma(nb, 0)
                        sp.wait_ge(*s("scores").at(b, U))
                        kx_dma(nb, 1)
                inputs(0)
                sp.wait_ge(*s("kh").at(0, NF))
                sp.wait_ge(*s("kl").at(0, NF))
                sp.wait_ge(kx_zero.sem, kx_zero.base + 2)
                for ft in range(NF):
                    kx_dma(0, ft)
                for_sequences(sp, body)

            @block.gpsimd
            def _(pool):
                pool.memset(kx[:, 1, :, :, :].bitcast(F32), 0.0).then_inc(kx_zero.sem, 1)
                pool.memset(vx[0][:, :, :, :, :], 0.0).then_inc(vx_zero.sem, 1)
                pool.memset(vx[1][:, :, :, :, :], 0.0).then_inc(vx_zero.sem, 1)
                if nxt:
                    load_group(core, pool, nxt)

            @block.tensor
            def _(pe):
                def scores(b, par, u):
                    ft, pr = u // (U // NF), u % (U // NF)
                    if u == 0:
                        pe.wait_ge(*s("qh").at(b, NF))
                        pe.wait_ge(*s("ql").at(b, NF))
                        if mask in ("self", "keys"):
                            pe.wait_ge(*s("mask_b").at(b, 1))
                    if pr == 0:
                        pe.wait_ge(*s(f"kx{ft}").at(b, G8 * 16))
                    if u >= 2:
                        pe.wait_ge(*s("exps").at(b, NE_ * (u - 1)))
                    elif u == 1:
                        pe.wait_ge(*s("exps").at(b, 0))
                    elif not (isinstance(b, int) and b == 0):
                        pe.wait_ge(*s("exps").at(b - 1, NE_ * (U - 1)))
                    out = SC[u % 2]
                    for t in range(NT):
                        n = keys_of[t]
                        o = out[:, t, :, 0:n]
                        lh = qh[par][:, ft, t * P:(t + 1) * P]
                        ll = ql[par][:, ft, t * P:(t + 1) * P]
                        rh = kx[:, ft, 0, 2 * pr:2 * pr + 2, 0:n]
                        rl = kx[:, ft, 1, 2 * pr:2 * pr + 2, 0:n]
                        m = three_pass(pe, o, lh, ll, rh, rl, True, mask in (None, "causal"))
                        if mask == "causal":
                            tri = core.tri_bf[:, :].unsqueeze(1).broadcast_to([P, 2, P])
                            m = pe.matmul(out[:, t, :, n - P:n], core.ident_bf[:, :], tri, start=False, stop=True,
                                          skip_group_check=True)
                        elif mask:
                            mm = mb[par][:, t if mask == "self" else 0, :].unsqueeze(1).broadcast_to([P, 2, S])
                            m = pe.matmul(o, core.ident_bf[:, :], mm, start=False, stop=True)
                    m.then_inc(s("scores").sem, 1)

                def turn_e(b, u):
                    pe.wait_ge(*s("exps").at(b, NE_ * (u + 1)))
                    pe.wait_ge(*s("et_v").at(b, ETN * u))
                    pe.wait_ge(*s("et_a").at(b, ETN * u))
                    for h in range(2):
                        for k in range(NT):
                            for t in range(NT):
                                if k * P < keys_of[t]:
                                    m = pe.transpose(ET[:, h, k, t * P:(t + 1) * P],
                                                     e[:, u % 2, t, h, k * P:(k + 1) * P], core.ident[:, :])
                    m.then_inc(s("et_psum").sem, 1)

                def pv(b, par, ft):
                    pe.wait_ge(*s("et_v").at(b, ETN * (U // NF) * (ft + 1)))
                    pe.wait_ge(*s("et_a").at(b, ETN * (U // NF) * (ft + 1)))
                    pe.wait_ge(*s("vx").at(b, 2))
                    if ft == 0:
                        pe.wait_ge(*s("on").at(b, 0))
                    for hp in range(2):
                        for k in range(NT):
                            for g_ in range(G8 // 2):
                                q0 = P if (mask == "causal" and k == 1) else 0
                                lhs = vx[par][:, k, ft * (G8 // 2) + g_, hp, :]
                                m = pe.matmul(O[32 * g_:32 * g_ + 32, ft, q0:S], lhs, et[:, 2 * g_ + hp, k, q0:S],
                                              start=(hp == 0 and k == 0), stop=(hp == 1 and k == NT - 1),
                                              tile_position=(0, 32 * g_), skip_group_check=True)
                    m.then_inc(s("pv").sem, 1)

                def turn_rcp(b):
                    pe.wait_ge(*s("rcpx").at(b, 1))
                    for t in range(NT):
                        for f in range(NF):
                            m = pe.transpose(M[:, f, t * P:(t + 1) * P],
                                             rcpx[:, t, f * G8:(f + 1) * G8, :].rearrange("p h d -> p (h d)"),
                                             core.ident[:, :])
                    m.then_inc(s("rt_psum").sem, 1)

                def out_proj(b):
                    pe.wait_ge(*s("oh").at(b, 1))
                    pe.wait_ge(*s("ol").at(b, 1))
                    project_tokens(pe, M, wh, wl, w_at(3), oh, ol).then_inc(s("out_psum").sem, 1)

                def split_done(src, b):
                    pe.wait_ge(*src.sg("lo").at(b, 1))
                    pe.wait_ge(*src.sg("hi").at(b, src.sg("hi").per))

                def k_proj(b):
                    split_done(kv, b)
                    project_features(pe, M, wh, wl, w_at(1), D, kv.xh, kv.xl, range(NF)).then_inc(s("k_psum").sem, 1)

                def keys_taken(b):
                    pe.wait_ge(*s("kh").at(b, NF))
                    pe.wait_ge(*s("kl").at(b, NF))

                def q_proj(b):
                    if cross:
                        split_done(q, b)
                    else:
                        keys_taken(b)
                    project_features(pe, M, wh, wl, w_at(0), D, q.xh, q.xl, range(NF)).then_inc(s("q_psum").sem, 1)

                def v_proj(b):
                    pe.wait_ge(*s("qh").at(b, NF))
                    pe.wait_ge(*s("ql").at(b, NF))
                    project_tokens(pe, M, wh, wl, w_at(2), kv.xh, kv.xl).then_inc(s("v_psum").sem, 1)

                def body(b, par, first, last):
                    for u in range(U):
                        if u < U - 1:
                            scores(b, par, u + 1)
                        elif not last:
                            scores(b + 1, 1 - par, 0)
                        if u == 1 and not first:
                            pv(b - 1, 1 - par, 1)
                        if u == U // NF + 1:
                            pv(b, par, 0)
                        if u > 0:
                            turn_e(b, u - 1)
                        elif not first:
                            turn_e(b - 1, U - 1)
                        if u == 0 and not first:
                            pe.wait_ge(*s("vx").at(b, 2))
                            turn_rcp(b - 1)
                        if u == 1 and not last:
                            if first:
                                pe.wait_ge(*s("vx").at(b, 2))
                            else:
                                pe.wait_ge(*s("rt").at(b - 1, 1))
                            kv.pe_turn(pe, b + 1, M)
                        if u == 2 and not first:
                            if last:
                                pe.wait_ge(*s("rt").at(b - 1, 1))
                            else:
                                split_done(kv, b + 1)
                            out_proj(b - 1)
                        if not last:
                            if u == 3:
                                if not first:
                                    pe.wait_ge(*s("fin_read").at(b - 1, 1))
                                k_proj(b + 1)
                            if u == 4 and cross:
                                keys_taken(b + 1)
                                q.pe_turn(pe, b + 1, M)
                            if u == 5:
                                q_proj(b + 1)
                            if u == 6:
                                v_proj(b + 1)

                if ready_at:
                    pe.wait_ge(ready.sem, ready_at)
                kv.pe_turn(pe, 0, M)
                k_proj(0)
                if cross:
                    keys_taken(0)
                    q.pe_turn(pe, 0, M)
                q_proj(0)
                v_proj(0)
                scores(0, 0, 0)
                for_sequences(pe, body)
                turn_e(B - 1, U - 1)
                pv(B - 1, 1, 1)
                pe.wait_ge(*s("fin_read").at(B - 2, 1))
                turn_rcp(B - 1)
                pe.wait_ge(*s("rt").at(B - 1, 1))
                out_proj(B - 1)

            @block.scalar
            def _(a):
                def exps(b, par, u, t):
                    if t == 0:
                        a.wait_ge(*s("neg").at(b, NEG * (u + 1)))
                        if u >= 2:
                            a.wait_ge(*s("et_psum").at(b, u - 1))
                        elif u == 1:
                            a.wait_ge(*s("et_psum").at(b, 0))
                        elif not (isinstance(b, int) and b == 0):
                            a.wait_ge(*s("et_psum").at(b - 1, U - 1))
                    n = keys_of[t]
                    for h in range(2):
                        hd = 2 * u + h
                        a.activation(e[:, u % 2, t, h, 0:n], SC[u % 2][:, t, h, 0:n], ACT.Exp,
                                     bias=neg[:, u % 2, t, h:h + 1],
                                     accum_out=den[:, par, t, hd:hd + 1]).then_inc(s("exps").sem, 1)

                def copy_et(b, u):
                    a.wait_ge(*s("et_psum").at(b, u + 1))
                    if u == 0:
                        a.wait_ge(*s("pv").at(b, 0))
                    elif u == U // NF:
                        a.wait_ge(*s("pv").at(b, 1))
                    i = (2 * u) % G8 + 1
                    if mask == "causal":
                        a.activation(et[:, i, 0, :], ET[:, 1, 0, :], ACT.Copy).then_inc(s("et_a").sem, 1)
                        a.activation(et[:, i, 1, P:S], ET[:, 1, 1, P:S], ACT.Copy).then_inc(s("et_a").sem, 1)
                    else:
                        a.activation(et[:, i, :, :], ET[:, 1, :, :], ACT.Copy).then_inc(s("et_a").sem, 1)

                def copy_rt(b):
                    a.wait_ge(*s("rt_psum").at(b, 1))
                    a.wait_ge(*s("on").at(b, 0))
                    a.activation(rt[:, :, :], M, ACT.Copy).then_inc(s("rt").sem, 1)

                def hi_q(b, par):
                    a.wait_ge(*s("q_psum").at(b, 1))
                    for f in range(NF):
                        dst = qh[par][:, f, :]
                        a.activation(dst, M[:, f, :], ACT.Identity, bias=bq(f)).then_inc(s("qh").sem, 1)

                def hi_k(b):
                    a.wait_ge(*s("k_psum").at(b, 1))
                    a.wait_ge(*s("kx0").at(b, 0))
                    a.wait_ge(*s("kx1").at(b, 0))
                    for f in range(NF):
                        a.activation(kh[:, f, :], M[:, f, :], ACT.Identity, bias=bk(f)).then_inc(s("kh").sem, 1)

                def body(b, par, first, last):
                    for u in range(U):
                        exps(b, par, u, 0)
                        if u == 1 and not first:
                            copy_rt(b - 1)
                        if not last:
                            if u == 2:
                                kv.act_hi(a, b + 1, M, kv_used)
                            if u == 4:
                                hi_k(b + 1)
                            if u == 5 and cross:
                                q.act_hi(a, b + 1, M, s("q_psum"))
                            if u == 6:
                                hi_q(b + 1, 1 - par)
                        exps(b, par, u, 1)
                        if u > 0:
                            copy_et(b, u - 1)
                        elif not first:
                            copy_et(b - 1, U - 1)
                        if u == 0 and not last:
                            kv.act_rstd(a, b + 1)
                        if u == 2 and not last and cross:
                            q.act_rstd(a, b + 1)
                        if u == 3 and not first:
                            fin.act_rstd(a, b - 1)

                a.preload_act_table_set(EXP_LN)
                kv.act_rstd(a, 0)
                if cross:
                    q.act_rstd(a, 0)
                kv.act_hi(a, 0, M, kv_used)
                hi_k(0)
                if cross:
                    q.act_hi(a, 0, M, s("q_psum"))
                hi_q(0, 0)
                for_sequences(a, body)
                copy_et(B - 1, U - 1)
                copy_rt(B - 1)
                fin.act_rstd(a, B - 1)

            @block.vector
            def _(v):
                def maxes(b, u):
                    v.wait_ge(*s("scores").at(b, u + 1))
                    if mask == "causal":
                        for t in range(NT):
                            v.tensor_reduce(neg[:, u % 2, t, :], SC[u % 2][:, t, :, 0:keys_of[t]], AX.X, ALU.max,
                                            negate=True).then_inc(s("neg").sem, 1)
                    else:
                        v.tensor_reduce(neg[:, u % 2, :, :], SC[u % 2], AX.X, ALU.max,
                                        negate=True).then_inc(s("neg").sem, 1)

                def copy_et(b, u):
                    v.wait_ge(*s("et_psum").at(b, u + 1))
                    if u == 0:
                        v.wait_ge(*s("pv").at(b, 0))
                    elif u == U // NF:
                        v.wait_ge(*s("pv").at(b, 1))
                    i = (2 * u) % G8
                    if mask == "causal":
                        v.tensor_copy(et[:, i, 0, :], ET[:, 0, 0, :]).then_inc(s("et_v").sem, 1)
                        v.tensor_copy(et[:, i, 1, P:S], ET[:, 0, 1, P:S]).then_inc(s("et_v").sem, 1)
                    else:
                        v.tensor_copy(et[:, i, :, :], ET[:, 0, :, :]).then_inc(s("et_v").sem, 1)

                def recips(b, par):
                    v.wait_ge(*s("exps").at(b, NE_ * U))
                    v.wait_ge(*s("rcpx").at(b, 0))
                    v.reciprocal(rcp[:, :, :], den[:, par, :, :]).then_inc(s("rcp").sem, 1)
                    v.wait_ge(*s("rcp").at(b, 1))
                    v.wait_ge(*s("rt_psum").at(b, 0))
                    v.tensor_copy(rcpx[:, :, :, :].rearrange("p t h d -> p (t h) d"),
                                  rcp[:, :, :].rearrange("p t h -> p (t h)").unsqueeze(2).broadcast_to([P, NT * H, DH])
                                  ).then_inc(s("rcpx").sem, 1)

                def normalise(b):
                    v.wait_ge(*s("rt").at(b, 1))
                    v.wait_ge(*s("pv").at(b, NF))
                    v.wait_ge(*s("ol").at(b, 0))
                    v.tensor_tensor(on[:, :, :], O, rt[:, :, :], ALU.mult).then_inc(s("on").sem, 1)
                    v.wait_ge(*s("on").at(b, 1))
                    v.wait_ge(*s("out_psum").at(b, 0))
                    v.tensor_copy(oh[:, :, :], on[:, :, :]).then_inc(s("oh").sem, 1)
                    v.wait_ge(*s("oh").at(b, 1))
                    v.tensor_tensor(ol[:, :, :], on[:, :, :], oh[:, :, :].bitcast(F32), ALU.subtract).then_inc(s("ol").sem, 1)

                def lo_q(b, par):
                    v.wait_ge(*s("qh").at(b, NF))
                    for f in range(NF):
                        v.scalar_tensor_tensor(ql[par][:, f, :], M[:, f, :], bq(f), qh[par][:, f, :].bitcast(F32),
                                               ALU.add, ALU.subtract).then_inc(s("ql").sem, 1)

                def lo_k(b):
                    v.wait_ge(*s("kh").at(b, NF))
                    v.wait_ge(*s("kx0").at(b, 0))
                    v.wait_ge(*s("kx1").at(b, 0))
                    for f in range(NF):
                        v.scalar_tensor_tensor(kl[:, f, :], M[:, f, :], bk(f), kh[:, f, :].bitcast(F32),
                                               ALU.add, ALU.subtract).then_inc(s("kl").sem, 1)

                def spread_v(b, par):
                    v.wait_ge(*s("v_psum").at(b, 1))
                    src = M.rearrange("p t (g x d) -> p t g x d", x=2, d=DH)
                    bv = rows[:, 0, :].rearrange("p (g x d) -> p g x d", x=2, d=DH)
                    for x in range(2):
                        v.tensor_tensor(vx[par][:, :, :, x, x * DH:(x + 1) * DH], src[:, :, :, x, :],
                                        bv[:, :, x, :].unsqueeze(1).broadcast_to([P, NT, H // 2, DH]), ALU.add
                                        ).then_inc(s("vx").sem, 1)

                def convert_mask(b, par):
                    if mask in ("self", "keys"):
                        v.wait_ge(*s("mask_in").at(b, 16))
                        v.tensor_scalar(mb[par][:, :, :], mi[:, :, :], 0.0, MASKED, ALU.is_equal, ALU.mult
                                        ).then_inc(s("mask_b").sem, 1)

                def body(b, par, first, last):
                    for u in range(U):
                        if u == 0 and not first:
                            recips(b - 1, 1 - par)
                        if u == 3 and not first:
                            fin.dve_read(v, b - 1, M, s("out_psum"), 1)
                        if u == 7 and not last:
                            spread_v(b + 1, 1 - par)
                        if not last:
                            if u == 2:
                                kv.dve_lo(v, b + 1, M, kv_used)
                            if u == 4:
                                lo_k(b + 1)
                            if u == 5 and cross:
                                q.dve_lo(v, b + 1, M, s("q_psum"))
                            if u == 6:
                                lo_q(b + 1, 1 - par)
                        if u < U - 1:
                            maxes(b, u + 1)
                        elif not last:
                            maxes(b + 1, 0)
                        if u > 0:
                            copy_et(b, u - 1)
                        elif not first:
                            copy_et(b - 1, U - 1)
                        if not last:
                            if u == 0:
                                kv.dve_stats(v, b + 1)
                                kv.dve_norm(v, b + 1)
                            if u == 2 and cross:
                                q.dve_stats(v, b + 1)
                            if u == 3 and cross:
                                q.dve_norm(v, b + 1)
                            if u == 3:
                                convert_mask(b + 1, 1 - par)
                        if not first:
                            if u == 1:
                                normalise(b - 1)
                            if u == 4:
                                fin.dve_norm(v, b - 1)

                v.memset(kx[:, 0, :, :, :].bitcast(F32), 0.0).then_inc(kx_zero.sem, 1)
                kv.dve_stats(v, 0)
                if cross:
                    q.dve_stats(v, 0)
                kv.dve_norm(v, 0)
                if cross:
                    q.dve_norm(v, 0)
                kv.dve_lo(v, 0, M, kv_used)
                lo_k(0)
                if cross:
                    q.dve_lo(v, 0, M, s("q_psum"))
                convert_mask(0, 0)
                lo_q(0, 0)
                v.wait_ge(vx_zero.sem, vx_zero.base + 2)
                if rows_at:
                    v.wait_ge(s("rows_in").sem, rows_at)
                spread_v(0, 0)
                maxes(0, 0)
                for_sequences(v, body)
                recips(B - 1, 1)
                copy_et(B - 1, U - 1)
                normalise(B - 1)
                fin.dve_read(v, B - 1, M, s("out_psum"), 1)
                fin.dve_norm(v, B - 1)

        kx_zero.base += 2
        vx_zero.base += 2
        core.end()


def hidden_bank(core, j):
    return core.psum[:, j, :].rearrange("p (a n) -> p a n", a=2)


def feed_forward(core, name, src, hidden, b1, kind, bias, g, state, nxt):
    nc = core.nc
    with ExitStack() as ctx:
        core.phase = name
        sb = lambda n, s, t=F32: ctx.enter_context(nc.sbuf_tensor(f"{name}_{n}", s, t))
        wh, wl, rows = weights_of(core, name)
        q = Source(core, ctx, "q", kind, **src)
        fin = Finish(core, ctx, kind, rows, bias, g, state)
        HT = hidden // P
        NB = HT // 2
        relu = sb("relu", [P, HT, S]) if b1 else None
        hh = [sb(f"hid_hi{i}", [P, HT, S], F32R) for i in range(2)]
        hl = [sb(f"hid_lo{i}", [P, HT, S], F32R) for i in range(2)]
        core.begin(**q.per, **fin.per, hid_psum=NB, relu=HT if b1 else 0, hid_hi=NB, hid_lo=NB, out_psum=1)
        s = core.s
        M, O = bank(core, 7), bank(core, 6)
        ready_at, rows_at = core.s("w_split").base, core.s("rows_in").base

        with nc.Block() as block:
            @block.gpsimd
            def _(pool):
                if nxt:
                    load_group(core, pool, nxt)

            @block.tensor
            def _(pe):
                def turn_q(b):
                    pe.wait_ge(*q.sg("lo").at(b, 0))
                    q.pe_turn(pe, b, M)

                def hidden_of(b):
                    pe.wait_ge(*q.sg("lo").at(b, 1))
                    pe.wait_ge(*q.sg("hi").at(b, q.sg("hi").per))
                    for j in range(NB):
                        if b1:
                            pe.wait_ge(*s("relu").at(b, 0))
                        else:
                            pe.wait_ge(*s("hid_lo").at(b, 0))
                        project_features(pe, hidden_bank(core, j), wh, wl, 0, hidden, q.xh, q.xl,
                                         (2 * j, 2 * j + 1)).then_inc(s("hid_psum").sem, 1)

                def out_of(b, par):
                    pe.wait_ge(*s("hid_hi").at(b, NB))
                    pe.wait_ge(*s("hid_lo").at(b, NB))
                    pe.wait_ge(*s("fin_read").at(b, 0))
                    project_tokens(pe, O, wh, wl, NF * hidden, hh[par], hl[par], HT).then_inc(s("out_psum").sem, 1)

                def body(b, par, first, ahead):
                    if ahead:
                        hidden_of(b + 1)
                    if ahead == 2:
                        turn_q(b + 2)
                    out_of(b, par)

                pe.wait_ge(s("w_split").sem, ready_at)
                q.pe_turn(pe, 0, M)
                hidden_of(0)
                turn_q(1)
                for_sequences_ahead(pe, body)

            @block.scalar
            def _(a):
                def relus(b, par):
                    if b1:
                        a.wait_ge(*s("hid_lo").at(b, 0))
                    elif not (isinstance(b, int) and b < 2):
                        a.wait_ge(*s("out_psum").at(b - 1, 0))
                    for j in range(NB):
                        a.wait_ge(*s("hid_psum").at(b, j + 1))
                        if b1:
                            for f in (2 * j, 2 * j + 1):
                                a.activation(relu[:, f, :], hidden_bank(core, j)[:, f % 2, :], ACT.Relu,
                                             bias=core.col(b1, f)).then_inc(s("relu").sem, 1)
                        else:
                            a.activation(hh[par][:, 2 * j:2 * j + 2, :], hidden_bank(core, j), ACT.Relu
                                         ).then_inc(s("hid_hi").sem, 1)

                def body(b, par, first, ahead):
                    if ahead == 2:
                        q.act_rstd(a, b + 2)
                    if not first:
                        fin.act_read(a, b - 1, O, s("out_psum"), 1)
                        fin.act_rstd(a, b - 1)
                    if ahead:
                        relus(b + 1, 1 - par)
                    if ahead == 2:
                        q.act_hi(a, b + 2, M, s("hid_psum"))

                a.preload_act_table_set(EXP_LN)
                q.act_rstd(a, 0)
                q.act_hi(a, 0, M, s("hid_psum"))
                q.act_rstd(a, 1)
                relus(0, 0)
                q.act_hi(a, 1, M, s("hid_psum"))
                for_sequences_ahead(a, body)
                fin.act_read(a, B - 1, O, s("out_psum"), 1)
                fin.act_rstd(a, B - 1)

            @block.vector
            def _(v):
                def splits(b, par, tiles):
                    if b1 and not (isinstance(b, int) and b < 2):
                        v.wait_ge(*s("out_psum").at(b - 1, 0))
                    for j in tiles:
                        t = slice(2 * j, 2 * j + 2)
                        if b1:
                            v.wait_ge(*s("relu").at(b, 2 * (j + 1)))
                            v.tensor_copy(hh[par][:, t, :], relu[:, t, :]).then_inc(s("hid_hi").sem, 1)
                            v.wait_ge(*s("hid_hi").at(b, j + 1))
                            v.tensor_tensor(hl[par][:, t, :], relu[:, t, :], hh[par][:, t, :].bitcast(F32),
                                            ALU.subtract).then_inc(s("hid_lo").sem, 1)
                        else:
                            v.wait_ge(*s("hid_hi").at(b, j + 1))
                            v.scalar_tensor_tensor(hl[par][:, t, :], hidden_bank(core, j), 0.0,
                                                   hh[par][:, t, :].bitcast(F32), ALU.max, ALU.subtract
                                                   ).then_inc(s("hid_lo").sem, 1)

                def body(b, par, first, ahead):
                    if ahead == 2:
                        q.dve_stats(v, b + 2)
                    if not first:
                        fin.dve_read(v, b - 1, O, s("out_psum"), 1)
                    if ahead:
                        splits(b + 1, 1 - par, range(NB // 2))
                    if ahead == 2:
                        q.dve_norm(v, b + 2)
                    if ahead:
                        splits(b + 1, 1 - par, range(NB // 2, NB))
                    if not first:
                        fin.dve_norm(v, b - 1)
                    if ahead == 2:
                        q.dve_lo(v, b + 2, M, s("hid_psum"))

                q.dve_stats(v, 0)
                q.dve_norm(v, 0)
                q.dve_lo(v, 0, M, s("hid_psum"))
                q.dve_stats(v, 1)
                q.dve_norm(v, 1)
                if rows_at:
                    v.wait_ge(s("rows_in").sem, rows_at)
                splits(0, 0, range(NB))
                q.dve_lo(v, 1, M, s("hid_psum"))
                for_sequences_ahead(v, body)
                fin.dve_read(v, B - 1, O, s("out_psum"), 1)
                fin.dve_norm(v, B - 1)
        core.end()


LH = 8
LD = D // LH
LB = P + P // LD


def linear_attention(core, name, q_src, kv_src, g, state, nxt):
    nc = core.nc
    with ExitStack() as ctx:
        core.phase = name
        sb = lambda n, s, t=F32: ctx.enter_context(nc.sbuf_tensor(f"{name}_{n}", s, t))
        wh, wl, rows = weights_of(core, name)
        w_at = lambda m: m * NF * D
        q = Source(core, ctx, "q", "inner", **q_src)
        kv = Source(core, ctx, "kv", "inner", **kv_src) if kv_src else q
        cross = kv is not q
        fin = Finish(core, ctx, "inner", rows, None, g, state)
        ex = sb("ex", [P, NF, S])
        rl = sb("rl", [P, NF, S])
        exk = sb("exk", [P, NT, D])
        rlk = sb("rlk", [P, NT, D])
        qe = [sb(f"qe{i}", [P, NF, S]) for i in range(2)]
        ke = sb("ke", [P, NT, D])
        vo = sb("vo", [P, NT, NF, LB])
        bd = sb("bd", [P, NF, LB])
        z = sb("z", [P, NT, NF, LB - P])
        zr = sb("zr", [P, NT, NF, LB - P])
        ms = sb("ms", [P, NT, D])
        mh = sb("mh", [P, NF, S], F32R)
        ml = sb("ml", [P, NF, S], F32R)
        core.begin(**q.per, **(kv.per if cross else {}), **fin.per, q_psum=1, q_ex=1, q_rl=1, qe=1,
                   k_psum=1, k_ex=1, k_rl=1, ke=1, v_psum=1, vo=1, kv_psum=1, bd=1, msg_psum=1, z=1, zr=1,
                   ms=NT, mt_psum=1, mh=1, ml=1, out_psum=1)
        s = core.s
        M, QB, KB, VB, TM = (bank(core, i) for i in (7, 0, 1, 2, 6))
        KV = core.psum[:, 3, 0:NF * LB].rearrange("p (f c) -> p f c", f=NF)
        MS = core.psum[:, 4:6, 0:NF * LB].rearrange("p t (f c) -> p t f c", f=NF)
        ready_at, rows_at = s("w_split").base, s("rows_in").base
        ones = s("ones")

        with nc.Block() as block:
            @block.gpsimd
            def _(pool):
                if nxt:
                    load_group(core, pool, nxt)

            @block.tensor
            def _(pe):
                def free(src, b):
                    pe.wait_ge(*src.sg("lo").at(b, 1))
                    pe.wait_ge(*src.sg("hi").at(b, 1))

                def q_proj(b):
                    free(q, b)
                    pe.wait_ge(*s("qe").at(b, 0))
                    project_features(pe, QB, wh, wl, w_at(0), D, q.xh, q.xl, range(NF)).then_inc(s("q_psum").sem, 1)

                def k_proj(b):
                    free(kv, b)
                    pe.wait_ge(*s("ke").at(b, 0))
                    project_tokens(pe, KB, wh, wl, w_at(1), kv.xh, kv.xl).then_inc(s("k_psum").sem, 1)

                def v_proj(b):
                    pe.wait_ge(*s("vo").at(b, 0))
                    project_tokens(pe, VB, wh, wl, w_at(2), kv.xh, kv.xl).then_inc(s("v_psum").sem, 1)

                def kv_product(b):
                    pe.wait_ge(*s("ke").at(b, 1))
                    pe.wait_ge(*s("vo").at(b, 1))
                    pe.wait_ge(*s("bd").at(b, 0))
                    for f in range(NF):
                        for t in range(NT):
                            m = pe.matmul(KV[:, f, :], ke[:, t, f * P:(f + 1) * P], vo[:, t, f, :],
                                          start=(t == 0), stop=(t == NT - 1))
                    m.then_inc(s("kv_psum").sem, 1)

                def message(b, par):
                    pe.wait_ge(*s("bd").at(b, 1))
                    pe.wait_ge(*s("qe").at(b, 1))
                    pe.wait_ge(*s("ms").at(b, 0))
                    for t in range(NT):
                        for f in range(NF):
                            m = pe.matmul(MS[:, t, f, :], qe[par][:, f, t * P:(t + 1) * P], bd[:, f, :],
                                          start=True, stop=True)
                    m.then_inc(s("msg_psum").sem, 1)

                def turn_message(b):
                    pe.wait_ge(*s("ms").at(b, NT))
                    pe.wait_ge(*s("fin_read").at(b, 0))
                    turn(pe, core, TM, ms).then_inc(s("mt_psum").sem, 1)

                def out_proj(b):
                    pe.wait_ge(*s("ml").at(b, 1))
                    project_tokens(pe, TM, wh, wl, w_at(3), mh, ml).then_inc(s("out_psum").sem, 1)

                def body(b, par, first, ahead):
                    kv_product(b)
                    if ahead:
                        q_proj(b + 1)
                    if ahead == 2 and cross:
                        free(kv, b + 1)
                        q.pe_turn(pe, b + 2, M)
                    message(b, par)
                    if ahead:
                        k_proj(b + 1)
                    turn_message(b)
                    if ahead:
                        v_proj(b + 1)
                    if ahead == 2:
                        free(q, b + 2 if cross else b + 1)
                        kv.pe_turn(pe, b + 2, M)
                    out_proj(b)

                pe.wait_ge(s("w_split").sem, ready_at)
                q.pe_turn(pe, 0, M)
                if cross:
                    free(q, 0)
                    kv.pe_turn(pe, 0, M)
                q_proj(0)
                if cross:
                    free(kv, 0)
                    q.pe_turn(pe, 1, M)
                k_proj(0)
                v_proj(0)
                free(q, 1 if cross else 0)
                kv.pe_turn(pe, 1, M)
                for_sequences_ahead(pe, body)

            @block.scalar
            def _(a):
                def used(src):
                    return s("v_psum") if src is kv else s("q_psum")

                def phi_parts(b, src, psum, ex_, rl_, n):
                    a.wait_ge(*s(f"{n}_psum").at(b, 1))
                    a.wait_ge(*s(f"{n}e").at(b, 0))
                    a.activation(ex_[:, :, :], psum, ACT.Exp).then_inc(s(f"{n}_ex").sem, 1)
                    a.activation(rl_[:, :, :], psum, ACT.Relu).then_inc(s(f"{n}_rl").sem, 1)

                def values(b):
                    a.wait_ge(*s("v_psum").at(b, 1))
                    a.wait_ge(*s("kv_psum").at(b, 0))
                    a.activation(vo[:, :, :, 0:P], VB.rearrange("p t (f c) -> p t f c", f=NF), ACT.Copy
                                 ).then_inc(s("vo").sem, 1)

                def message_hi(b):
                    a.wait_ge(*s("mt_psum").at(b, 1))
                    a.wait_ge(*s("out_psum").at(b, 0))
                    a.activation(mh[:, :, :], TM, ACT.Copy).then_inc(s("mh").sem, 1)

                def body(b, par, first, ahead):
                    if not first:
                        fin.act_read(a, b - 1, TM, s("out_psum"), 1)
                    if ahead:
                        phi_parts(b + 1, q, QB, ex, rl, "q")
                    if ahead == 2 and cross:
                        q.act_hi(a, b + 2, M, used(q))
                    if not first:
                        fin.act_rstd(a, b - 1)
                    if ahead:
                        phi_parts(b + 1, kv, KB, exk, rlk, "k")
                    message_hi(b)
                    if ahead:
                        values(b + 1)
                    if ahead == 2:
                        kv.act_hi(a, b + 2, M, used(kv))

                a.preload_act_table_set(EXP_LN)
                q.act_hi(a, 0, M, used(q))
                if cross:
                    kv.act_hi(a, 0, M, used(kv))
                phi_parts(0, q, QB, ex, rl, "q")
                if cross:
                    q.act_hi(a, 1, M, used(q))
                phi_parts(0, kv, KB, exk, rlk, "k")
                values(0)
                kv.act_hi(a, 1, M, used(kv))
                for_sequences_ahead(a, body)
                fin.act_read(a, B - 1, TM, s("out_psum"), 1)
                fin.act_rstd(a, B - 1)

            @block.vector
            def _(v):
                def used(src):
                    return s("v_psum") if src is kv else s("q_psum")

                def phi(b, out, ex_, rl_, n):
                    v.wait_ge(*s(f"{n}_rl").at(b, 1))
                    v.wait_ge(*s(f"{n}_ex").at(b, 1))
                    v.scalar_tensor_tensor(out[:, :, :], ex_[:, :, :], 1.0, rl_[:, :, :], ALU.min, ALU.add
                                           ).then_inc(s(f"{n}e").sem, 1)

                def phi_k(b):
                    v.wait_ge(*s("kv_psum").at(b, 0))
                    phi(b, ke, exk, rlk, "k")

                def block_diagonal(b):
                    v.wait_ge(*s("kv_psum").at(b, 1))
                    v.wait_ge(*s("msg_psum").at(b, 0))
                    v.tensor_tensor(bd[:, :, :], KV, core.blocks[:, :].unsqueeze(1).broadcast_to([P, NF, LB]), ALU.mult
                                    ).then_inc(s("bd").sem, 1)

                def message(b):
                    v.wait_ge(*s("msg_psum").at(b, 1))
                    v.wait_ge(*s("zr").at(b, 0))
                    v.tensor_scalar(z[:, :, :, :], MS[:, :, :, P:LB], 1e-6, None, ALU.add).then_inc(s("z").sem, 1)
                    v.wait_ge(*s("z").at(b, 1))
                    v.wait_ge(*s("ms").at(b, 0))
                    v.reciprocal(zr[:, :, :, :], z[:, :, :, :]).then_inc(s("zr").sem, 1)
                    v.wait_ge(*s("zr").at(b, 1))
                    v.wait_ge(*s("mt_psum").at(b, 0))
                    for t in range(NT):
                        v.tensor_tensor(ms[:, t, :].rearrange("p (f j d) -> p f j d", f=NF, d=LD),
                                        MS[:, t, :, 0:P].rearrange("p f (j d) -> p f j d", d=LD),
                                        zr[:, t, :, :].unsqueeze(3).broadcast_to([P, NF, P // LD, LD]), ALU.mult
                                        ).then_inc(s("ms").sem, 1)

                def message_lo(b):
                    v.wait_ge(*s("mh").at(b, 1))
                    v.tensor_tensor(ml[:, :, :], TM, mh[:, :, :].bitcast(F32), ALU.subtract).then_inc(s("ml").sem, 1)

                def body(b, par, first, ahead):
                    block_diagonal(b)
                    if not first:
                        fin.dve_read(v, b - 1, TM, s("out_psum"), 1)
                    if ahead == 2:
                        q.dve_stats(v, b + 2)
                    message(b)
                    if ahead == 2 and cross:
                        q.dve_lo(v, b + 2, M, used(q))
                        kv.dve_stats(v, b + 2)
                    if ahead:
                        phi(b + 1, qe[1 - par], ex, rl, "q")
                    message_lo(b)
                    if ahead:
                        phi_k(b + 1)
                    if not first:
                        fin.dve_norm(v, b - 1)
                    if ahead == 2:
                        kv.dve_lo(v, b + 2, M, used(kv))

                v.memset(vo[:, :, :, P:LB], 1.0).then_inc(ones.sem, 1)
                if rows_at:
                    v.wait_ge(s("rows_in").sem, rows_at)
                q.dve_stats(v, 0)
                if cross:
                    kv.dve_stats(v, 0)
                q.dve_lo(v, 0, M, used(q))
                if cross:
                    kv.dve_lo(v, 0, M, used(kv))
                q.dve_stats(v, 1)
                if cross:
                    kv.dve_stats(v, 1)
                phi(0, qe[0], ex, rl, "q")
                if cross:
                    q.dve_lo(v, 1, M, used(q))
                phi_k(0)
                kv.dve_lo(v, 1, M, used(kv))
                for_sequences_ahead(v, body)
                fin.dve_read(v, B - 1, TM, s("out_psum"), 1)
                fin.dve_norm(v, B - 1)
        ones.base += 1
        core.end()


def load_expert(core, pool, e, par):
    s, d = core.s, core.d
    n = GSIZE["E0"] // CHUNK
    col0 = GOFF["E0"] + e * GSIZE["E0"]
    wh, wl = core.wh[par], core.wl[par]

    def bring(c):
        pool.wait_ge(*s("xw_split").at(e, max(0, c - STAGES + 1)))
        pool.dma_start(core.stage[:, c % STAGES, :], d["weights"][:, bass.ds(col0 + c * CHUNK, CHUNK)]
                       ).then_inc(s(f"xw_raw{c % STAGES}").sem, 16)

    pool.dma_start(core.rows[par][:, 0:1, :],
                   d["rows"][bass.ds(ROFF["E0"] + e, 1), :].partition_broadcast(P)).then_inc(s("xw_row").sem, 16)
    for c in range(STAGES - 1):
        bring(c)
    for c in range(n):
        if c + STAGES - 1 < n:
            bring(c + STAGES - 1)
        pool.wait_ge(*s(f"xw_raw{c % STAGES}").at(e, 16 * (c // STAGES + 1)))
        st = core.stage[:, c % STAGES, :]
        a, z = c * CHUNK, (c + 1) * CHUNK
        pool.sem_inc(s("xw_seen").sem, 1)
        pool.tensor_copy(wh[:, a:z], st).then_inc(s("xw_hi").sem, 1)
        pool.wait_ge(*s("xw_hi").at(e, c + 1))
        pool.tensor_tensor(wl[:, a:z], st, wh[:, a:z].bitcast(F32), ALU.subtract).then_inc(s("xw_split").sem, 1)
    pool.wait_ge(*s("xw_row").at(e, 16))


def gates(core, ctx, nxt_unused=None):
    nc = core.nc
    sb = lambda n, s, t=F32: ctx.enter_context(nc.sbuf_tensor(f"moe_{n}", s, t))
    xah = sb("xa_hi", [P, NF, B * S], F32R)
    xal = sb("xa_lo", [P, NF, B * S], F32R)
    gate = sb("gate", [P, B * NT, NE])
    with ExitStack() as inner:
        sb = lambda n, s, t=F32: inner.enter_context(nc.sbuf_tensor(f"moe_{n}", s, t))
        q = Source(core, inner, "q", "pre", ln=("L2_xattn_moe_ln_g", "L2_xattn_moe_ln_b"), state=core.X)
        rh = sb("router_hi", [P, NF, NE], F32R)
        rl = sb("router_lo", [P, NF, NE], F32R)
        T = B * NT
        lg = sb("lg", [P, T, NE])
        top = sb("top", [P, T, 8])
        idx = sb("idx", [P, T, 8], U32)
        idf = sb("idf", [P, T, 8])
        dif = sb("dif", [P, T, 1])
        e2 = sb("e2", [P, T, 1])
        dn = sb("dn", [P, T, 1])
        g1 = sb("g1", [P, T, 1])
        g2 = sb("g2", [P, T, 1])
        o1 = sb("o1", [P, T, NE])
        o2 = sb("o2", [P, T, NE])
        core.begin(**q.per, lg_psum=1, lg=1, xa_h=1, xa_l=1)
        s = core.s
        M, L = bank(core, 7), bank(core, 6)
        one = s("gate_step")
        base = one.base

        with nc.Block() as block:
            @block.gpsimd
            def _(pool):
                load_expert(core, pool, 0, 0)

            @block.tensor
            def _(pe):
                def body(b, par, first, last):
                    if not first:
                        pe.wait_ge(*q.sg("lo").at(b, 0))
                    q.pe_turn(pe, b, M)
                    pe.wait_ge(*q.sg("lo").at(b, 1))
                    pe.wait_ge(*s("lg").at(b, 0))
                    for t in range(NT):
                        for k in range(NF):
                            m = three_pass(pe, L[:, t, 0:NE], q.xh[:, k, t * P:(t + 1) * P],
                                           q.xl[:, k, t * P:(t + 1) * P], rh[:, k, :], rl[:, k, :],
                                           k == 0, k == NF - 1)
                    m.then_inc(s("lg_psum").sem, 1)
                pe.wait_ge(one.sem, base + 2)
                for_sequences(pe, body)

            @block.scalar
            def _(a):
                def body(b, par, first, last):
                    q.act_rstd(a, b)
                    q.act_hi(a, b, M, None)
                    cols = bass.ds(b * S, S)
                    a.wait_ge(*q.sg("hi").at(b, 1))
                    a.wait_ge(*q.sg("lo").at(b, 1))
                    a.sem_inc(s("split_seen").sem, 1)
                    a.activation(xah[:, :, cols], q.xh[:, :, :].bitcast(F32), ACT.Copy).then_inc(s("xa_h").sem, 1)
                    a.activation(xal[:, :, cols], q.xl[:, :, :].bitcast(F32), ACT.Copy).then_inc(s("xa_l").sem, 1)
                a.preload_act_table_set(EXP_LN)
                for_sequences(a, body)
                a.wait_ge(one.sem, base + 3)
                a.activation(e2[:, :, :], dif[:, :, :], ACT.Exp).then_inc(s("gate_exp").sem, 1)

            @block.vector
            def _(v):
                def body(b, par, first, last):
                    q.dve_stats(v, b)
                    q.dve_norm(v, b)
                    v.wait_ge(*s("xa_h").at(b, 0))
                    v.wait_ge(*s("xa_l").at(b, 0))
                    q.dve_lo(v, b, M, s("lg_psum"))
                    v.wait_ge(*s("lg_psum").at(b, 1))
                    v.tensor_tensor(lg[:, bass.ds(NT * b, NT), :], L[:, :, 0:NE],
                                    core.router_b[:, :].unsqueeze(1).broadcast_to([P, NT, NE]), ALU.add
                                    ).then_inc(s("lg").sem, 1)
                n = [base]

                def step(ins):
                    n[0] += 1
                    ins.then_inc(one.sem, 1)
                    v.wait_ge(one.sem, n[0])

                step(v.tensor_copy(rh[:, :, :], core.router_w[:, :, :]))
                step(v.tensor_tensor(rl[:, :, :], core.router_w[:, :, :], rh[:, :, :].bitcast(F32), ALU.subtract))
                for_sequences(v, body)
                v.wait_ge(*s("lg").at(B - 1, 1))
                for t in range(T):
                    v.max(top[:, t, :], lg[:, t, :]).then_inc(s("top").sem, 1)
                v.wait_ge(s("top").sem, s("top").base + T)
                for t in range(T):
                    v.max_index(idx[:, t, :], top[:, t, :], lg[:, t, :]).then_inc(s("top").sem, 1)
                step(v.tensor_tensor(dif[:, :, :], top[:, :, 1:2], top[:, :, 0:1], ALU.subtract))
                v.wait_ge(s("top").sem, s("top").base + 2 * T)
                step(v.tensor_copy(idf[:, :, :], idx[:, :, :]))
                v.wait_ge(s("gate_exp").sem, s("gate_exp").base + 1)
                step(v.tensor_scalar(dn[:, :, :], e2[:, :, :], 1.0, None, ALU.add))
                step(v.reciprocal(g1[:, :, :], dn[:, :, :]))
                step(v.tensor_tensor(g2[:, :, :], e2[:, :, :], g1[:, :, :], ALU.mult))
                ids = core.iota[:, :].unsqueeze(1).broadcast_to([P, T, NE])
                for o, g, j in ((o1, g1, 0), (o2, g2, 1)):
                    step(v.tensor_tensor(o[:, :, :], ids, idf[:, :, j:j + 1].broadcast_to([P, T, NE]), ALU.is_equal))
                    step(v.tensor_tensor(o[:, :, :], o[:, :, :], g[:, :, :].broadcast_to([P, T, NE]), ALU.mult))
                step(v.tensor_tensor(gate[:, :, :], o1[:, :, :], o2[:, :, :], ALU.add))
        one.base += 11
        s("top").base += 2 * T
        s("gate_exp").base += 1
        core.end()
    return xah, xal, gate


def experts(core, nxt):
    nc = core.nc
    s = core.s
    core.phase = "moe"
    with ExitStack() as ctx:
        for n, k in dict(xw_split=GSIZE["E0"] // CHUNK, xw_hi=GSIZE["E0"] // CHUNK, xw_row=16, b1e=1).items():
            s(n).begin(k)
        for i in range(STAGES):
            s(f"xw_raw{i}").begin(16 * GSIZE["E0"] // CHUNK // STAGES)
        xah, xal, gate = gates(core, ctx)
        sb = lambda n, s, t=F32: ctx.enter_context(nc.sbuf_tensor(f"moe_{n}", s, t))
        HT = FE // P
        NB = HT // 2
        act = sb("gelu", [P, HT, S])
        hh = [sb(f"hid_hi{i}", [P, HT, S], F32R) for i in range(2)]
        hl = [sb(f"hid_lo{i}", [P, HT, S], F32R) for i in range(2)]
        y = sb("y", [P, NT, D])
        b1e = sb("b1e", [P, HT])
        core.begin(hid_psum=NB, gelu=HT, hid_hi=NB, hid_lo=NB, out_psum=1, y=1, mixed=NT)
        O = bank(core, 6)

        with nc.Block() as block:
            @block.gpsimd
            def _(pool):
                def body(e, par, first, last):
                    if last:
                        pool.wait_ge(*s("mixed").at(B * (NE - 1), 0))
                        pool.wait_ge(*s("xw_split").at(NE - 1, GSIZE["E0"] // CHUNK))
                        load_group(core, pool, nxt)
                    else:
                        if not first:
                            pool.wait_ge(*s("mixed").at(B * e, 0))
                        load_expert(core, pool, e + 1, 1 - par)
                for_sequences(pool, body)

            @block.tensor
            def _(pe):
                def expert(e, ep, first_e, last_e):
                    wh, wl = core.wh[ep], core.wl[ep]

                    def hidden_of(b):
                        n = B * e + b
                        pe.wait_ge(*s("gelu").at(n, 0))
                        for j in range(NB):
                            cols = bass.ds(b * S, S)
                            o = hidden_bank(core, j)
                            for i, f in enumerate((2 * j, 2 * j + 1)):
                                for k in range(NF):
                                    a = k * FE + f * P
                                    m = three_pass(pe, o[:, i, :], wh[:, a:a + P], wl[:, a:a + P],
                                                   xah[:, k, cols], xal[:, k, cols], k == 0, k == NF - 1)
                            m.then_inc(s("hid_psum").sem, 1)

                    def body(b, par, first, last):
                        if not last:
                            hidden_of(b + 1)
                        n = B * e + b
                        pe.wait_ge(*s("hid_lo").at(n, NB))
                        pe.wait_ge(*s("y").at(n, 0))
                        project_tokens(pe, O, wh, wl, NF * FE, hh[par], hl[par], HT).then_inc(s("out_psum").sem, 1)

                    pe.wait_ge(*s("xw_split").at(e, GSIZE["E0"] // CHUNK))
                    hidden_of(0)
                    for_sequences(pe, body)
                for_sequences(pe, expert)

            @block.scalar
            def _(a):
                def expert(e, ep, first_e, last_e):
                    a.wait_ge(*s("gelu").at(B * e, 0))
                    a.sem_inc(s("bias_free").sem, 1)
                    a.activation(b1e[:, :], core.cols[:, bass.ds(COFF["experts"] + HT * e, HT)], ACT.Copy
                                 ).then_inc(s("b1e").sem, 1)
                    a.wait_ge(*s("b1e").at(e, 1))

                    def body(b, par, first, last):
                        n = B * e + b
                        a.wait_ge(*s("hid_lo").at(n, 0))
                        for j in range(NB):
                            a.wait_ge(*s("hid_psum").at(n, j + 1))
                            for f in (2 * j, 2 * j + 1):
                                a.activation(act[:, f, :], hidden_bank(core, j)[:, f % 2, :], ACT.Gelu,
                                             bias=b1e[:, f:f + 1]
                                             ).then_inc(s("gelu").sem, 1)
                    for_sequences(a, body)
                a.preload_act_table_set("gelu_and_others")
                for_sequences(a, expert)

            @block.vector
            def _(v):
                def expert(e, ep, first_e, last_e):
                    def splits(b, par):
                        n = B * e + b
                        for j in range(NB):
                            t = slice(2 * j, 2 * j + 2)
                            v.wait_ge(*s("gelu").at(n, 2 * (j + 1)))
                            v.tensor_copy(hh[par][:, t, :], act[:, t, :]).then_inc(s("hid_hi").sem, 1)
                            v.wait_ge(*s("hid_hi").at(n, j + 1))
                            v.tensor_tensor(hl[par][:, t, :], act[:, t, :], hh[par][:, t, :].bitcast(F32),
                                            ALU.subtract).then_inc(s("hid_lo").sem, 1)

                    def body(b, par, first, last):
                        n = B * e + b
                        if not last:
                            splits(b + 1, 1 - par)
                        v.wait_ge(*s("out_psum").at(n, 1))
                        v.wait_ge(*s("mixed").at(n, 0))
                        v.tensor_tensor(y[:, :, :], O, core.rows[ep][:, 0:1, :].broadcast_to([P, NT, D]), ALU.add
                                        ).then_inc(s("y").sem, 1)
                        v.wait_ge(*s("y").at(n, 1))
                        for t in range(NT):
                            x = core.X[:, NT * b + t, :]
                            v.scalar_tensor_tensor(x, y[:, t, :], gate[:, NT * b + t, bass.ds(e, 1)], x,
                                                   ALU.mult, ALU.add).then_inc(s("mixed").sem, 1)

                    v.wait_ge(*s("xw_split").at(e, GSIZE["E0"] // CHUNK))
                    v.wait_ge(*s("xw_row").at(e, 16))
                    splits(0, 0)
                    for_sequences(v, body)
                for_sequences(v, expert)
        for n in core.begun:
            s(n).end(B * NE)
        for n in ["xw_split", "xw_hi", "xw_row", "b1e"] + [f"xw_raw{i}" for i in range(STAGES)]:
            s(n).end(NE)


def program(nc, d):
    with ExitStack() as ctx:
        core = Core(nc, ctx, d)
        s = core.s
        sb = lambda n, sh, t=F32: ctx.enter_context(nc.sbuf_tensor(n, sh, t))
        core.eps = sb("eps", [P, 1])
        core.blocks = sb("blocks", [P, LB])
        core.router_w = sb("router_w", [P, NF, NE])
        core.router_b = sb("router_b", [P, NE])
        core.iota = sb("iota", [P, NE])
        core.raw_sems = [s(f"w_raw{i}") for i in range(STAGES)]

        with nc.Block() as block:
            @block.sync
            def _(sp):
                for dst, src in ((core.X[:, :, :], d["x"]), (core.cols[:, :], d["cols"]), (core.ident[:, :], d["ident"]),
                                 (core.tri[:, :], d["tri"]), (core.blocks[:, :], d["blocks"]),
                                 (core.router_w[:, :, :], d["router_w"]),
                                 (core.router_b[:, :], d["router_b"].partition_broadcast(P)),
                                 (core.iota[:, :], d["iota"].partition_broadcast(P))):
                    sp.dma_start(dst, src).then_inc(s("first_loads").sem, 16)
                sp.wait_ge(s("first_loads").sem, 8 * 16)

            @block.gpsimd
            def _(pool):
                load_group(core, pool, "L0s")

            @block.vector
            def _(v):
                v.memset(core.eps[:, :], EPS).then_inc(s("set_up").sem, 1)
                v.wait_ge(s("first_loads").sem, 8 * 16)
                v.tensor_copy(core.ident_bf[:, :], core.ident[:, :]).then_inc(s("set_up").sem, 1)
                v.tensor_copy(core.tri_bf[:, :], core.tri[:, :]).then_inc(s("set_up").sem, 1)
                for i, n in enumerate(BQS):
                    v.tensor_scalar(core.bq4[:, i, :], core.cols[:, COFF[n]:COFF[n] + NF], DH ** -0.5, None, ALU.mult
                                    ).then_inc(s("set_up").sem, 1)

        bq = lambda i: (lambda f: core.bq4[:, i, f:f + 1])
        bk = lambda n: (lambda f: core.col(n, f))
        X = core.X
        attention(core, "L0s", dict(state=X), None, bq(0), bk("L0_xattn_sa_bk"), "post", 2, "self", "L0c")
        attention(core, "L0c", dict(state=X), dict(dram=d["ctx"]), bq(1), bk("L0_xattn_ca_bk"), "post", 2, "keys", "L0f")
        feed_forward(core, "L0f", dict(state=X), 1024, "L0_xattn_ffn_b1", "post", 0, 1, X, "L1e")
        with ExitStack() as l1:
            C = l1.enter_context(nc.sbuf_tensor("C", [P, B * NT, D], F32))
            with nc.Block() as block:
                @block.sync
                def _(sp):
                    sp.dma_start(C[:, :, :], d["ctx"]).then_inc(s("ctx_in").sem, 16)

                @block.vector
                def _(v):
                    v.wait_ge(s("ctx_in").sem, 16)
                    v.tensor_tensor(C[:, :, :], C[:, :, :], C[:, :, :], ALU.add).then_inc(s("set_up").sem, 1)
            linear_attention(core, "L1e", dict(state=C), None, 0, C, "L1ef")
            feed_forward(core, "L1ef", dict(state=C), 512, None, "inner", None, 0, C, "L1s")
            linear_attention(core, "L1s", dict(state=X), None, 0, X, "L1c")
            linear_attention(core, "L1c", dict(state=X), dict(state=C), 0, X, "L1df")
            feed_forward(core, "L1df", dict(state=X), 512, None, "inner", None, 0, X, "L2s")
        ln = lambda n: (n + "_g", n + "_b")
        attention(core, "L2s", dict(state=X, ln=ln("L2_xattn_sa_ln")), None, bq(2), bk("@L2_xattn_sa_in_b:1"),
                  "pre", 0, None, "L2c")
        attention(core, "L2c", dict(state=X, ln=ln("L2_xattn_ca_q_ln")),
                  dict(dram=d["ctx"], ln=ln("L2_xattn_ca_kv_ln")), bq(3), bk("@L2_xattn_ca_in_b:1"),
                  "pre", 0, None, None)
        experts(core, "L3s")
        attention(core, "L3s", dict(state=X, ln=ln("L3_xattn_ln1")), None, bq(4), bk("L3_xattn_mmha_wk_b"),
                  "pre", 0, "causal", "L3c")
        attention(core, "L3c", dict(state=X, ln=ln("L3_xattn_ln2")), dict(dram=d["ctx"]), bq(5),
                  bk("L3_xattn_mha_wk_b"), "pre", 0, None, "L3f")
        feed_forward(core, "L3f", dict(state=X, ln=ln("L3_xattn_ln3")), 1024, "L3_xattn_ffn_b1", "pre", 0, 0, X, None)
        with nc.Block() as block:
            @block.sync
            def _(sp):
                sp.dma_start(d["out"], X[:, :, :]).then_inc(s("stored").sem, 16)
                sp.wait_ge(s("stored").sem, 16)


def token_tiles(a):
    return np.ascontiguousarray(a.reshape(B * NT, P, a.shape[-1]).transpose(1, 0, 2))


def operand(w):
    i, o = w.shape
    return w.reshape(i // P, P, o).transpose(1, 0, 2).reshape(P, -1)


def kernel(**inputs):
    import concourse.bacc as bacc
    from concourse.bass_utils import run_bass_kernel_spmd as launch

    a = {n: np.asarray(v) for n, v in inputs.items()}

    def vec(n):
        if n[0] == "@":
            n, j = n[1:].split(":")
            return a[n][int(j) * D:(int(j) + 1) * D]
        if n[0] == "#":
            n, j = n[1:].split(":")
            return a[n][int(j)]
        return a[n]

    w = []
    for x in ("sa", "ca"):
        w += [operand(a[f"L0_xattn_{x}_w{m}"].T) for m in "qkvo"]
    w += [operand(a["L0_xattn_ffn_w1"].T), operand(a["L0_xattn_ffn_w2"].T)]
    w += [operand(a[f"L1_xattn_e_w{m}"]) for m in "qkvm12"]
    for j in "01":
        w += [operand(a[f"L1_xattn_d_w{m}{j}"]) for m in "qkvm"]
    w += [operand(a["L1_xattn_d_w1"]), operand(a["L1_xattn_d_w2"])]
    for x in ("sa", "ca"):
        w += [operand(a[f"L2_xattn_{x}_in_w"][m * D:(m + 1) * D].T) for m in range(3)]
        w += [operand(a[f"L2_xattn_{x}_out_w"].T)]
    for e in range(NE):
        w += [operand(a["L2_xattn_e_fc1_w"][e].T), operand(a["L2_xattn_e_fc2_w"][e].T)]
    for x in ("mmha", "mha"):
        w += [operand(a[f"L3_xattn_{x}_w{m}"]) for m in "qkvo"]
    w += [operand(a["L3_xattn_ffn_w1"]), operand(a["L3_xattn_ffn_w2"])]

    cols = [vec(n).reshape(NF, P).T for n in COLS]
    cols += [a["L0_xattn_ffn_b1"].reshape(-1, P).T, a["L3_xattn_ffn_b1"].reshape(-1, P).T]
    cols += [a["L2_xattn_e_fc1_b"].reshape(-1, P).T]
    data = {
        "x": token_tiles(a["x"]), "ctx": token_tiles(a["ctx_1024"]),
        "mask_self": token_tiles(a["mask_Bx1xSxS2_if1"][:, 0]),
        "mask_keys": np.ascontiguousarray(a["mask_Bx1x1xS2_if1"].reshape(B, S)),
        "weights": np.ascontiguousarray(np.concatenate(w, axis=1)),
        "rows": np.stack([vec(n) for r in ROWS.values() for n in r]),
        "cols": np.ascontiguousarray(np.concatenate(cols, axis=1)),
        "router_w": np.ascontiguousarray(a["L2_xattn_router_w"].T.reshape(NF, P, NE).transpose(1, 0, 2)),
        "router_b": a["L2_xattn_router_b"],
        "ident": np.eye(P, dtype=np.float32),
        "tri": np.triu(np.full((P, P), MASKED, np.float32), 1),
        "blocks": np.ascontiguousarray(np.concatenate(
            [np.kron(np.eye(P // LD), np.ones((LD, LD))), np.kron(np.eye(P // LD), np.ones((LD, 1)))], axis=1
        ).astype(np.float32)),
        "iota": np.arange(NE, dtype=np.float32),
    }
    nc = bacc.Bacc("TRN2", target_bir_lowering=False, num_devices=1)
    d = {n: nc.dram_tensor(f"in_{n}", v.shape, mybir.dt.from_np(v.dtype), kind="ExternalInput").ap()
         for n, v in data.items()}
    d["out"] = nc.dram_tensor("out_0", (P, B * NT, D), F32, kind="ExternalOutput").ap()
    program(nc, d)
    r = launch(nc, [{f"in_{n}": v for n, v in data.items()}], core_ids=[0])
    got = r.results[0]["out_0"]
    return np.ascontiguousarray(got.transpose(1, 0, 2)).reshape(B, S, D)
```

```python
from contextlib import ExitStack

import numpy as np

import concourse.bass as bass
from concourse import mybir

F32 = mybir.dt.float32
F32R = mybir.dt.float32r
BF16 = mybir.dt.bfloat16
I32 = mybir.dt.int32
U32 = mybir.dt.uint32
ALU = mybir.AluOpType
ACT = mybir.ActivationFunctionType
AX = mybir.AxisListType

P = 128
B = 8
S = 256
D = 256
NT = S // P
NF = D // P
H = 16
DH = D // H
NE = 8
FE = 1024
EPS = 1e-5
EXP_LN = "natural_log_exp_and_others"
MASKED = -float(2 ** 100)
CHUNK = 512
STAGES = 4


class Signal:

    def __init__(self, nc, ctx, name):
        self.sem = ctx.enter_context(nc.semaphore(name))
        self.base = 0
        self.per = 0

    def begin(self, per):
        self.per = per

    def end(self, n=B):
        self.base += self.per * n
        self.per = 0

    def at(self, b, k):
        return self.sem, b * self.per + (self.base + k)


def for_sequences(eng, body):
    body(0, 0, True, False)
    with eng.Fori(0, (B - 2) // 2) as i:
        body(2 * i + 1, 1, False, False)
        body(2 * i + 2, 0, False, False)
    body(B - 1, 1, False, True)


def for_sequences_ahead(eng, body):
    body(0, 0, True, 2)
    with eng.Fori(0, (B - 4) // 2) as i:
        body(2 * i + 1, 1, False, 2)
        body(2 * i + 2, 0, False, 2)
    for b in range(B - 3, B):
        body(b, b % 2, False, min(2, B - 1 - b))


GROUPS = [("L0s", 4 * NF * D), ("L0c", 4 * NF * D), ("L0f", 2 * 4 * NF * D),
          ("L1e", 4 * NF * D), ("L1ef", 2 * 2 * NF * D), ("L1s", 4 * NF * D), ("L1c", 4 * NF * D),
          ("L1df", 2 * 2 * NF * D), ("L2s", 4 * NF * D), ("L2c", 4 * NF * D)] + \
         [(f"E{e}", 2 * 4 * NF * D) for e in range(NE)] + \
         [("L3s", 4 * NF * D), ("L3c", 4 * NF * D), ("L3f", 2 * 4 * NF * D)]
GOFF = {}
_o = 0
for _n, _c in GROUPS:
    GOFF[_n] = _o
    _o += _c
WCOLS = _o
GSIZE = dict(GROUPS)
GINDEX = {n: i for i, (n, _) in enumerate(GROUPS)}

ROWS = {"L0s": ["L0_xattn_sa_bv", "L0_xattn_sa_bo", "L0_xattn_ln1_g", "L0_xattn_ln1_b"],
        "L0c": ["L0_xattn_ca_bv", "L0_xattn_ca_bo", "L0_xattn_ln2_g", "L0_xattn_ln2_b"],
        "L0f": ["L0_xattn_ffn_b2", "L0_xattn_ln3_g", "L0_xattn_ln3_b"],
        "L1e": ["L1_xattn_e_g1", "L1_xattn_e_b1"], "L1ef": ["L1_xattn_e_g2", "L1_xattn_e_b2"],
        "L1s": ["L1_xattn_d_g0", "L1_xattn_d_b0"], "L1c": ["L1_xattn_d_g1", "L1_xattn_d_b1"],
        "L1df": ["L1_xattn_d_g2", "L1_xattn_d_b2"],
        "L2s": ["@L2_xattn_sa_in_b:2", "L2_xattn_sa_out_b"],
        "L2c": ["@L2_xattn_ca_in_b:2", "L2_xattn_ca_out_b"],
        "E0": ["#L2_xattn_e_fc2_b:%d" % e for e in range(NE)],
        "L3s": ["L3_xattn_mmha_wv_b", "L3_xattn_mmha_wo_b"],
        "L3c": ["L3_xattn_mha_wv_b", "L3_xattn_mha_wo_b"],
        "L3f": ["L3_xattn_ffn_b2"]}
ROFF = {}
_o = 0
for _n, _r in ROWS.items():
    ROFF[_n] = _o
    _o += len(_r)
NROWS = _o
MAXROWS = 4

COLS = ["L0_xattn_sa_bq", "L0_xattn_sa_bk", "L0_xattn_ca_bq", "L0_xattn_ca_bk",
        "@L2_xattn_sa_in_b:0", "@L2_xattn_sa_in_b:1", "@L2_xattn_ca_in_b:0", "@L2_xattn_ca_in_b:1",
        "L3_xattn_mmha_wq_b", "L3_xattn_mmha_wk_b", "L3_xattn_mha_wq_b", "L3_xattn_mha_wk_b",
        "L2_xattn_sa_ln_g", "L2_xattn_sa_ln_b", "L2_xattn_ca_q_ln_g", "L2_xattn_ca_q_ln_b",
        "L2_xattn_ca_kv_ln_g", "L2_xattn_ca_kv_ln_b", "L2_xattn_moe_ln_g", "L2_xattn_moe_ln_b",
        "L3_xattn_ln1_g", "L3_xattn_ln1_b", "L3_xattn_ln2_g", "L3_xattn_ln2_b",
        "L3_xattn_ln3_g", "L3_xattn_ln3_b"]
COFF = {}
_o = 0
for _n in COLS:
    COFF[_n] = _o
    _o += NF
for _n in ("L0_xattn_ffn_b1", "L3_xattn_ffn_b1"):
    COFF[_n] = _o
    _o += 8
COFF["experts"] = _o
_o += NE * FE // P
NCOLS = _o
BQS = ["L0_xattn_sa_bq", "L0_xattn_ca_bq", "@L2_xattn_sa_in_b:0", "@L2_xattn_ca_in_b:0",
       "L3_xattn_mmha_wq_b", "L3_xattn_mha_wq_b"]


class Core:

    def __init__(self, nc, ctx, d):
        self.nc, self.d = nc, d
        sb = lambda n, s, t=F32: ctx.enter_context(nc.sbuf_tensor(n, s, t))
        self.X = sb("X", [P, B * NT, D])
        self.wh = [sb(f"w_hi{i}", [P, 4096], F32R) for i in range(2)]
        self.wl = [sb(f"w_lo{i}", [P, 4096], F32R) for i in range(2)]
        self.stage = sb("w_stage", [P, STAGES, CHUNK])
        self.rows = [sb(f"rows{i}", [P, MAXROWS, D]) for i in range(2)]
        self.cols = sb("cols", [P, NCOLS])
        self.bq4 = sb("bq4", [P, len(BQS), NF])
        self.ident = sb("ident", [P, P])
        self.ident_bf = sb("ident_bf", [P, P], BF16)
        self.tri = sb("tri", [P, P])
        self.tri_bf = sb("tri_bf", [P, P], BF16)
        self.psum = ctx.enter_context(nc.psum_tensor("psum", [P, 8, 512], F32))
        self.k_dram = nc.dram_tensor("k_rows", (D, 2, S), F32, kind="Internal").ap()
        self.sig = {}
        self.ctx = ctx
        self.begun = []
        self.phase = ""

    def s(self, name):
        if name not in self.sig:
            self.sig[name] = Signal(self.nc, self.ctx, name)
        return self.sig[name]

    def begin(self, **per):
        for n, k in per.items():
            self.s(n).begin(k)
        self.begun = list(per)
        return [self.s(n) for n in per]

    def end(self):
        for n in self.begun:
            self.s(n).end()

    def col(self, name, j):
        c = COFF[name] + j
        return self.cols[:, c:c + 1]


def load_group(core, pool, name):
    nc, d = core.nc, core.d
    g = GINDEX[name]
    par = g % 2
    n = GSIZE[name] // CHUNK
    raw, hi_done, split = core.s("w_raw"), core.s("w_hi_done"), core.s("w_split")
    wh, wl = core.wh[par], core.wl[par]
    if name in ROWS and name != "E0":
        nr = len(ROWS[name])
        src = d["rows"][ROFF[name]:ROFF[name] + nr, :].partition_broadcast(P)
        pool.dma_start(core.rows[par][:, 0:nr, :], src).then_inc(core.s("rows_in").sem, 16)

    def bring(c):
        if split.base + c - STAGES + 1 > 0:
            pool.wait_ge(split.sem, split.base + c - STAGES + 1)
        pool.dma_start(core.stage[:, c % STAGES, :],
                       d["weights"][:, GOFF[name] + c * CHUNK:GOFF[name] + (c + 1) * CHUNK]
                       ).then_inc(core.raw_sems[c % STAGES].sem, 16)

    for c in range(min(STAGES - 1, n)):
        bring(c)
    for c in range(n):
        if c + STAGES - 1 < n:
            bring(c + STAGES - 1)
        slot = core.raw_sems[c % STAGES]
        slot.base += 16
        pool.wait_ge(slot.sem, slot.base)
        st = core.stage[:, c % STAGES, :]
        a, z = c * CHUNK, (c + 1) * CHUNK
        if name in ("L0s", "L0c", "L2s", "L2c", "L3s", "L3c") and c == 0:
            sc = core.s("w_scaled")
            pool.tensor_scalar(st, st, DH ** -0.5, None, ALU.mult).then_inc(sc.sem, 1)
            sc.base += 1
            pool.wait_ge(sc.sem, sc.base)
        pool.tensor_copy(wh[:, a:z], st).then_inc(hi_done.sem, 1)
        hi_done.base += 1
        pool.wait_ge(hi_done.sem, hi_done.base)
        pool.tensor_tensor(wl[:, a:z], st, wh[:, a:z].bitcast(F32), ALU.subtract).then_inc(split.sem, 1)
    split.base += n
    if name in ROWS and name != "E0":
        rin = core.s("rows_in")
        rin.base += 16
        pool.wait_ge(rin.sem, rin.base)


def bring_first(core, sp, name):
    d = core.d
    sp.dma_start(core.rows[0][:, 0:len(ROWS[name]), :], d["rows"][0:len(ROWS[name]), :].partition_broadcast(P)
                 ).then_inc(core.s("rows_first").sem, 16)
    for c in range(STAGES):
        sp.dma_start(core.stage[:, c, :], d["weights"][:, c * CHUNK:(c + 1) * CHUNK]
                     ).then_inc(core.s(f"w_first{c}").sem, 16)


def split_first(core, v, name):
    scaled, hi_done, split = core.s("w_scaled"), core.s("w_hi_done"), core.s("w_split")
    assert GINDEX[name] == 0 and GSIZE[name] == STAGES * CHUNK
    wh, wl = core.wh[0], core.wl[0]
    for c in range(STAGES):
        v.wait_ge(core.s(f"w_first{c}").sem, 16)
        st = core.stage[:, c, :]
        a, z = c * CHUNK, (c + 1) * CHUNK
        if c == 0:
            v.tensor_scalar(st, st, DH ** -0.5, None, ALU.mult).then_inc(scaled.sem, 1)
            v.wait_ge(scaled.sem, 1)
        v.tensor_copy(wh[:, a:z], st).then_inc(hi_done.sem, 1)
        v.wait_ge(hi_done.sem, c + 1)
        v.tensor_tensor(wl[:, a:z], st, wh[:, a:z].bitcast(F32), ALU.subtract).then_inc(split.sem, 1)
    v.wait_ge(core.s("rows_first").sem, 16)
    scaled.base, hi_done.base, split.base = 1, STAGES, STAGES


def weights_of(core, name):
    par = GINDEX[name] % 2
    return core.wh[par], core.wl[par], core.rows[par]


def three_pass(pe, out, lh, ll, rh, rl, first, last):
    pe.matmul(out, lh, rh, start=first, stop=False)
    pe.matmul(out, lh, rl, start=False, stop=False)
    return pe.matmul(out, ll, rh, start=False, stop=last)


def project_features(pe, out, wh, wl, off, width, xh, xl, tiles, n=S):
    for j, f in enumerate(tiles):
        for k in range(NF):
            a = off + k * width + f * P
            m = three_pass(pe, out[:, j, 0:n], wh[:, a:a + P], wl[:, a:a + P], xh[:, k, :], xl[:, k, :],
                           k == 0, k == NF - 1)
    return m


def project_tokens(pe, out, wh, wl, off, xh, xl, nk=NF):
    for t in range(NT):
        for k in range(nk):
            a = off + k * D
            m = three_pass(pe, out[:, t, :], xh[:, k, t * P:(t + 1) * P], xl[:, k, t * P:(t + 1) * P],
                           wh[:, a:a + D], wl[:, a:a + D], k == 0, k == nk - 1)
    return m


def turn(pe, core, out, x):
    for t in range(NT):
        for f in range(NF):
            m = pe.transpose(out[:, f, t * P:(t + 1) * P], x[:, t, f * P:(f + 1) * P], core.ident[:, :])
    return m


def bank(core, i):
    return core.psum[:, i, :].rearrange("p (a n) -> p a n", a=2)


class Source:

    def __init__(self, core, ctx, tag, kind, ln=None, state=None, dram=None, buffered=False):
        nc = core.nc
        sb = lambda n, s, t=F32: ctx.enter_context(nc.sbuf_tensor(f"{core.phase}_{tag}_{n}", s, t))
        self.core, self.tag, self.ln, self.state, self.dram = core, tag, ln, state, dram
        self.x_in = sb("in", [P, NT, D])
        self.raw = sb("raw", [P, NT, D]) if dram is not None and ln else None
        self.xh = sb("hi", [P, NF, S], F32R)
        self.xl = sb("lo", [P, NF, S], F32R)
        self.buffered = buffered or ln is not None
        if self.buffered:
            self.full = sb("full", [P, NF, S])
        if ln:
            self.stats = sb("stats", [P, NT, 6])
            self.mv = sb("mv", [P, NT, 2])
            self.lnv = sb("lnv", [P, NT])
            self.rstd = sb("rstd", [P, NT])
        per = {f"{tag}_in": NT if ln else 1, f"{tag}_turned": 1, f"{tag}_hi": 1, f"{tag}_lo": 1}
        if self.buffered:
            per[f"{tag}_full"] = NF if ln else 1
        if dram is not None:
            per[f"{tag}_load" if ln else f"{tag}_in"] = 16
        if ln:
            per.update({f"{tag}_stats": NT, f"{tag}_mv": NT, f"{tag}_aggr": 1, f"{tag}_lnv": 1, f"{tag}_rstd": 1})
        self.per = per

    def sg(self, n):
        return self.core.s(f"{self.tag}_{n}")

    def load(self, sp, b):
        if self.dram is None:
            return
        if self.ln:
            sp.wait_ge(*self.sg("in").at(b, 0))
            sp.dma_start(self.raw[:, :, :], self.dram[:, bass.ds(NT * b, NT), :]).then_inc(self.sg("load").sem, 16)
        else:
            sp.wait_ge(*self.sg("turned").at(b, 0))
            sp.dma_start(self.x_in[:, :, :], self.dram[:, bass.ds(NT * b, NT), :]).then_inc(self.sg("in").sem, 16)

    def src(self, b, t=None):
        if self.raw is not None:
            return self.raw[:, :, :] if t is None else self.raw[:, t, :]
        return self.state[:, bass.ds(NT * b, NT), :] if t is None else self.state[:, NT * b + t, :]

    def dve_stats(self, v, b):
        if self.ln is None:
            if self.dram is None:
                v.wait_ge(*self.sg("turned").at(b, 0))
                v.tensor_copy(self.x_in[:, :, :], self.src(b)).then_inc(self.sg("in").sem, 1)
            return
        if self.raw is not None:
            v.wait_ge(*self.sg("load").at(b, 16))
        for t in range(NT):
            v.bn_stats(self.stats[:, t, :], self.src(b, t)).then_inc(self.sg("stats").sem, 1)
        v.wait_ge(*self.sg("stats").at(b, NT))
        v.wait_ge(*self.sg("rstd").at(b, 0))
        v.sem_inc(self.sg("aggr").sem, 1)
        for t in range(NT):
            v.bn_aggr(self.mv[:, t, :], self.stats[:, t, :]).then_inc(self.sg("mv").sem, 1)

    def act_rstd(self, a, b):
        if self.ln is None:
            return
        a.wait_ge(*self.sg("mv").at(b, NT))
        a.activation(self.lnv[:, :], self.mv[:, :, 1], ACT.Ln, bias=self.core.eps[:, 0:1]).then_inc(self.sg("lnv").sem, 1)
        a.wait_ge(*self.sg("lnv").at(b, 1))
        a.wait_ge(*self.sg("in").at(b, 0))
        a.activation(self.rstd[:, :], self.lnv[:, :], ACT.Exp, scale=-0.5).then_inc(self.sg("rstd").sem, 1)

    def dve_norm(self, v, b):
        if self.ln is None:
            return
        v.wait_ge(*self.sg("rstd").at(b, 1))
        v.wait_ge(*self.sg("turned").at(b, 0))
        for t in range(NT):
            v.tensor_scalar(self.x_in[:, t, :], self.src(b, t), self.mv[:, t, 0:1], self.rstd[:, t:t + 1],
                            ALU.subtract, ALU.mult).then_inc(self.sg("in").sem, 1)

    def pe_turn(self, pe, b, out):
        pe.wait_ge(*self.sg("in").at(b, self.sg("in").per))
        turn(pe, self.core, out, self.x_in).then_inc(self.sg("turned").sem, 1)

    def act_hi(self, a, b, src, used):
        a.wait_ge(*self.sg("turned").at(b, 1))
        if not self.buffered:
            a.wait_ge(*used.at(b, 0))
            a.activation(self.xh[:, :, :], src, ACT.Copy).then_inc(self.sg("hi").sem, 1)
            return
        a.wait_ge(*self.sg("lo").at(b, 0))
        if self.ln is None:
            a.activation(self.full[:, :, :], src, ACT.Copy).then_inc(self.sg("full").sem, 1)
            return
        for f in range(NF):
            a.activation(self.full[:, f, :], src[:, f, :], ACT.Identity, bias=self.core.col(self.ln[1], f),
                         scale=self.core.col(self.ln[0], f)).then_inc(self.sg("full").sem, 1)

    def dve_lo(self, v, b, src, used):
        if not self.buffered:
            v.wait_ge(*self.sg("hi").at(b, 1))
            v.wait_ge(*used.at(b, 0))
            v.tensor_tensor(self.xl[:, :, :], src, self.xh[:, :, :].bitcast(F32), ALU.subtract
                            ).then_inc(self.sg("lo").sem, 1)
            return
        v.wait_ge(*self.sg("full").at(b, self.sg("full").per))
        v.wait_ge(*used.at(b, 0))
        v.tensor_copy(self.xh[:, :, :], self.full[:, :, :]).then_inc(self.sg("hi").sem, 1)
        v.wait_ge(*self.sg("hi").at(b, 1))
        v.tensor_tensor(self.xl[:, :, :], self.full[:, :, :], self.xh[:, :, :].bitcast(F32), ALU.subtract
                        ).then_inc(self.sg("lo").sem, 1)


class Finish:

    def __init__(self, core, ctx, kind, rows, bias, g, state):
        nc = core.nc
        sb = lambda n, s, t=F32: ctx.enter_context(nc.sbuf_tensor(f"{core.phase}_fin_{n}", s, t))
        self.core, self.kind, self.rows, self.bias, self.g, self.state = core, kind, rows, bias, g, state
        self.y = sb("y", [P, NT, D])
        self.z = sb("z", [P, NT, D]) if kind != "pre" else None
        if kind != "pre":
            self.stats = sb("stats", [P, NT, 6])
            self.mv = sb("mv", [P, NT, 2])
            self.lnv = sb("lnv", [P, NT])
            self.rstd = sb("rstd", [P, NT])
        self.per = {"fin_read": 1, "fin_done": NT if kind == "post" else 1}
        if kind != "pre":
            self.per["fin_y" if kind == "post" else "fin_scaled"] = 1 if kind == "post" else NT
            self.per.update({"fin_stats": NT, "fin_aggr": 1, "fin_mv": NT, "fin_lnv": 1, "fin_rstd": 1,
                             "fin_norm": NT})

    def row(self, r):
        return self.rows[:, r:r + 1, :].broadcast_to([P, NT, D])

    def act_read(self, a, b, out, out_sig, out_n):
        s = self.core.s
        if self.kind != "inner":
            return
        a.wait_ge(*out_sig.at(b, out_n))
        a.wait_ge(*s("fin_norm").at(b, 0))
        a.activation(self.y[:, :, :], out, ACT.Copy).then_inc(s("fin_read").sem, 1)

    def dve_read(self, v, b, out, out_sig, out_n):
        self.dve_take(v, b, out, out_sig, out_n)
        self.dve_add(v, b)

    def dve_take(self, v, b, out, out_sig, out_n):
        s = self.core.s
        if self.kind == "inner":
            v.wait_ge(*s("fin_read").at(b, 1))
        else:
            v.wait_ge(*out_sig.at(b, out_n))
            v.wait_ge(*s("fin_done").at(b, 0))
            v.tensor_tensor(self.y[:, :, :], out, self.row(self.bias), ALU.add).then_inc(s("fin_read").sem, 1)
            v.wait_ge(*s("fin_read").at(b, 1))

    def dve_add(self, v, b):
        s = self.core.s
        x = self.state[:, bass.ds(NT * b, NT), :]
        if self.kind == "pre":
            v.tensor_tensor(x, x, self.y[:, :, :], ALU.add).then_inc(s("fin_done").sem, 1)
            return
        if self.kind == "post":
            v.tensor_tensor(self.y[:, :, :], self.y[:, :, :], x, ALU.add).then_inc(s("fin_y").sem, 1)
            v.wait_ge(*s("fin_y").at(b, 1))
        for t in range(NT):
            v.bn_stats(self.stats[:, t, :], self.y[:, t, :]).then_inc(s("fin_stats").sem, 1)
        v.wait_ge(*s("fin_stats").at(b, NT))
        v.sem_inc(s("fin_aggr").sem, 1)
        for t in range(NT):
            v.bn_aggr(self.mv[:, t, :], self.stats[:, t, :]).then_inc(s("fin_mv").sem, 1)

    def act_rstd(self, a, b):
        s = self.core.s
        if self.kind == "pre":
            return
        a.wait_ge(*s("fin_mv").at(b, NT))
        a.activation(self.lnv[:, :], self.mv[:, :, 1], ACT.Ln, bias=self.core.eps[:, 0:1]).then_inc(s("fin_lnv").sem, 1)
        a.wait_ge(*s("fin_lnv").at(b, 1))
        a.activation(self.rstd[:, :], self.lnv[:, :], ACT.Exp, scale=-0.5).then_inc(s("fin_rstd").sem, 1)

    def dve_norm(self, v, b):
        s = self.core.s
        if self.kind == "pre":
            return
        v.wait_ge(*s("fin_mv").at(b, NT))
        if self.kind == "inner":
            v.wait_ge(*s("fin_done").at(b, 0))
        for t in range(NT):
            v.scalar_tensor_tensor(self.z[:, t, :], self.y[:, t, :], self.mv[:, t, 0:1], self.rows[:, self.g, :],
                                   ALU.subtract, ALU.mult).then_inc(s("fin_norm").sem, 1)
        v.wait_ge(*s("fin_rstd").at(b, 1))
        v.wait_ge(*s("fin_norm").at(b, NT))
        for t in range(NT):
            out = self.state[:, NT * b + t, :] if self.kind == "post" else self.z[:, t, :]
            v.scalar_tensor_tensor(out, self.z[:, t, :], self.rstd[:, t:t + 1], self.rows[:, self.g + 1, :],
                                   ALU.mult, ALU.add
                                   ).then_inc(s("fin_done" if self.kind == "post" else "fin_scaled").sem, 1)

    def pool_add(self, pool):
        s = self.core.s

        def body(b, par, first, last):
            x = self.state[:, bass.ds(NT * b, NT), :]
            pool.wait_ge(*s("fin_scaled").at(b, NT))
            pool.tensor_tensor(x, x, self.z[:, :, :], ALU.add).then_inc(s("fin_done").sem, 1)
        if self.kind == "inner":
            for_sequences(pool, body)


def attention(core, name, q_src, kv_src, bq, bk, kind, g, mask, nxt):
    nc = core.nc
    with ExitStack() as ctx:
        core.phase = name
        sb = lambda n, s, t=F32: ctx.enter_context(nc.sbuf_tensor(f"{name}_{n}", s, t))
        wh, wl, rows = weights_of(core, name)
        w_at = lambda m: m * NF * D
        q = Source(core, ctx, "q", kind, buffered=True, **q_src)
        kv = Source(core, ctx, "kv", kind, buffered=True, **kv_src) if kv_src else q
        cross = kv is not q
        G8 = H // NF
        U = H // 2
        W = 2 * DH
        q2 = sb("q2", [P, NF, 2, S], F32R)
        k2 = sb("k2", [P, NF, 2, S], F32R)
        qx = [w[:, GSIZE[name]:GSIZE[name] + U * S].rearrange("p (u s) -> p u s", u=U) for w in (wh, wl)]
        kx = [sb(f"kx{i}", [P, U, 2, S], F32R) for i in range(2)]
        vx = [sb(f"vx{i}", [P, NT, H // 2, 2, 2 * DH]) for i in range(2)]
        e = sb("e", [P, 2, NT, 2, S])
        et = sb("et", [P, G8, NT, S])
        neg = sb("neg", [P, 2, NT, 2])
        den = sb("den", [P, 2, NT, H])
        rcp = sb("rcp", [P, NT, H])
        rcpx = sb("rcpx", [P, NT, H, DH])
        rt = sb("rt", [P, NF, S])
        on = sb("on", [P, NF, S])
        oh = sb("oh", [P, NF, S], F32R)
        ol = sb("ol", [P, NF, S], F32R)
        fin = Finish(core, ctx, kind, rows, 1, g, core.X)
        if mask in ("self", "keys"):
            mt = NT if mask == "self" else 1
            mi = sb("mi", [P, mt, S], I32)
            mb = [sb(f"mb{i}", [P, mt, S], BF16 if mask == "self" else F32R) for i in range(2)]
        keys_of = [P, S] if mask == "causal" else [S, S]
        NE_ = 2 * NT
        ETN = 2 if mask == "causal" else 1
        core.begin(**q.per, **(kv.per if cross else {}), **fin.per,
                   q_psum=1, qh=NF, ql=NF, k_psum=1, kh=NF, kl=NF, k_stored=16,
                   kx=(6 + 2 * (mask == "keys")) * 16, **{f"qx{g_}": 3 * 16 for g_ in range(U // NF)}, v_psum=1, vx=2,
                   scores=NT * U, neg=NT * U, exps=NE_ * U, et_psum=2 * U,
                   et_v=ETN * U, et_a=ETN * U, pv=NF, rcp=1, rcpx=1, rt_psum=1, rt=1, on=1, oh=1, ol=1,
                   out_psum=1, mask_in=16 if mask in ("self", "keys") else 0, mask_b=1 if mask in ("self", "keys") else 0)
        s = core.s
        MROW, KX_SET = 3 * W, 4
        M = bank(core, 7)
        O = bank(core, 6)
        SC = [core.psum[:, 2 * i:2 * i + 2, :].rearrange("p t (h k) -> p t h k", h=2) for i in range(2)]
        ET = core.psum[:, 4:6, :].rearrange("p h (t q) -> p h t q", t=NT)
        kv_used = s("v_psum")
        kx_set, vx_zero = s("kx_set"), s("vx_zero")
        ready = core.s("w_split")
        ready_at = ready.base
        rows_at = core.s("rows_in").base

        with nc.Block() as block:
            @block.sync
            def _(sp):
                PARTS = ((0, 0, 0), (1, 0, 1), (2, 1, 0))

                def spread_keys(b, par):
                    sp.wait_ge(*s("kh").at(b, NF))
                    sp.wait_ge(*s("kl").at(b, NF))
                    sp.dma_start(core.k_dram[:, :, :].rearrange("(f p) h s -> p f (h s)", f=NF),
                                 k2[:, :, :, :].rearrange("p f h s -> p f (h s)").bitcast(F32)
                                 ).then_inc(s("k_stored").sem, 16)
                    sp.wait_ge(*s("k_stored").at(b, 16))
                    for i in range(2):
                        for j, _, half in PARTS:
                            src = core.k_dram[:, half, :].rearrange("(u i x) s -> i x u s", i=2, x=DH)[i]
                            sp.dma_start(kx[par][W * j + DH * i:W * j + DH * (i + 1), :, i, :].bitcast(F32), src
                                         ).then_inc(s("kx").sem, 16)
                    if mask == "keys":
                        sp.wait_ge(*s("mask_b").at(b, 1))
                        for i in range(2):
                            sp.dma_start(kx[par][MROW:MROW + 1, :, i, :].bitcast(F32),
                                         mb[par][MROW:MROW + 1, :, :].bitcast(F32).broadcast_to([1, U, S])
                                         ).then_inc(s("kx").sem, 16)

                def spread_queries(b, par):
                    sp.wait_ge(*s("qh").at(b, NF))
                    sp.wait_ge(*s("ql").at(b, NF))
                    for g_ in range(U // NF):
                        for j, half, _ in PARTS:
                            sp.dma_start(qx[par][W * j:W * (j + 1), g_:U:U // NF, :].bitcast(F32),
                                         q2[W * g_:W * (g_ + 1), :, half, :].bitcast(F32)
                                         ).then_inc(s(f"qx{g_}").sem, 16)

                def masks(b):
                    if mask in ("self", "keys"):
                        sp.wait_ge(*s("mask_b").at(b, 0))
                        if mask == "self":
                            sp.dma_start(mi[:, :, :], core.d["mask_self"][:, bass.ds(NT * b, NT), :]
                                         ).then_inc(s("mask_in").sem, 16)
                        else:
                            sp.dma_start(mi[MROW:MROW + 1, 0, :], core.d["mask_keys"][bass.ds(b, 1), :]
                                         ).then_inc(s("mask_in").sem, 16)

                def body(b, par, first, ahead):
                    if ahead:
                        masks(b + 1)
                        if ahead == 2:
                            kv.load(sp, b + 2)
                            if cross:
                                q.load(sp, b + 2)
                        spread_keys(b + 1, 1 - par)
                        spread_queries(b + 1, 1 - par)
                kv.load(sp, 0)
                if cross:
                    q.load(sp, 0)
                masks(0)
                kv.load(sp, 1)
                if cross:
                    q.load(sp, 1)
                sp.wait_ge(kx_set.sem, kx_set.base + KX_SET)
                spread_keys(0, 0)
                spread_queries(0, 0)
                for_sequences_ahead(sp, body)

            @block.gpsimd
            def _(pool):
                for i in range(2):
                    pool.memset(kx[i][:, :, :, :].bitcast(F32), 0.0).then_inc(kx_set.sem, 1)
                pool.memset(vx[0][:, :, :, :, :], 0.0).then_inc(vx_zero.sem, 1)
                pool.memset(vx[1][:, :, :, :, :], 0.0).then_inc(vx_zero.sem, 1)
                if nxt:
                    load_group(core, pool, nxt)

            @block.tensor
            def _(pe):
                def scores(b, par, u):
                    if u < U // NF:
                        pe.wait_ge(*s(f"qx{u}").at(b, 3 * 16))
                    if u == 0:
                        pe.wait_ge(*s("kx").at(b, s("kx").per))
                        if mask == "self":
                            pe.wait_ge(*s("mask_b").at(b, 1))
                    for t in range(NT):
                        if u >= 2:
                            pe.wait_ge(*s("exps").at(b, NE_ * (u - 2) + 2 * (t + 1)))
                        elif not (isinstance(b, int) and b == 0):
                            pe.wait_ge(*s("exps").at(b - 1, NE_ * (U + u - 2) + 2 * (t + 1)))
                        n = keys_of[t]
                        o = SC[u % 2][:, t, :, 0:n]
                        m = pe.matmul(o, qx[par][:, u, t * P:(t + 1) * P], kx[par][:, u, :, 0:n], start=True,
                                      stop=mask != "self")
                        if mask == "causal":
                            tri = core.tri_bf[:, :].unsqueeze(1).broadcast_to([P, 2, P])
                            m = pe.matmul(SC[u % 2][:, t, :, n - P:n], core.ident_bf[:, :], tri, start=False, stop=True,
                                          skip_group_check=True)
                        elif mask == "self":
                            mm = mb[par][:, t, :].unsqueeze(1).broadcast_to([P, 2, S])
                            m = pe.matmul(o, core.ident_bf[:, :], mm, start=False, stop=True)
                        m.then_inc(s("scores").sem, 1)

                def turn_e(b, u):
                    pe.wait_ge(*s("exps").at(b, NE_ * (u + 1)))
                    for h in range(2):
                        pe.wait_ge(*s(("et_v", "et_a")[h]).at(b, ETN * u))
                        for k in range(NT):
                            for t in range(NT):
                                if k * P < keys_of[t]:
                                    m = pe.transpose(ET[:, h, k, t * P:(t + 1) * P],
                                                     e[:, u % 2, t, h, k * P:(k + 1) * P], core.ident[:, :])
                        m.then_inc(s("et_psum").sem, 1)

                def pv(b, par, ft):
                    pe.wait_ge(*s("et_v").at(b, ETN * (U // NF) * (ft + 1)))
                    pe.wait_ge(*s("et_a").at(b, ETN * (U // NF) * (ft + 1)))
                    pe.wait_ge(*s("vx").at(b, 2))
                    if ft == 0:
                        pe.wait_ge(*s("on").at(b, 0))
                    for hp in range(2):
                        for k in range(NT):
                            for g_ in range(G8 // 2):
                                q0 = P if (mask == "causal" and k == 1) else 0
                                lhs = vx[par][:, k, ft * (G8 // 2) + g_, hp, :]
                                m = pe.matmul(O[32 * g_:32 * g_ + 32, ft, q0:S], lhs, et[:, 2 * g_ + hp, k, q0:S],
                                              start=(hp == 0 and k == 0), stop=(hp == 1 and k == NT - 1),
                                              tile_position=(0, 32 * g_), skip_group_check=True)
                    m.then_inc(s("pv").sem, 1)

                def turn_rcp(b):
                    pe.wait_ge(*s("rcpx").at(b, 1))
                    for t in range(NT):
                        for f in range(NF):
                            m = pe.transpose(M[:, f, t * P:(t + 1) * P],
                                             rcpx[:, t, f * G8:(f + 1) * G8, :].rearrange("p h d -> p (h d)"),
                                             core.ident[:, :])
                    m.then_inc(s("rt_psum").sem, 1)

                def out_proj(b):
                    pe.wait_ge(*s("oh").at(b, 1))
                    pe.wait_ge(*s("ol").at(b, 1))
                    project_tokens(pe, M, wh, wl, w_at(3), oh, ol).then_inc(s("out_psum").sem, 1)

                def split_done(src, b):
                    pe.wait_ge(*src.sg("lo").at(b, 1))
                    pe.wait_ge(*src.sg("hi").at(b, src.sg("hi").per))

                def k_proj(b):
                    split_done(kv, b)
                    project_features(pe, M, wh, wl, w_at(1), D, kv.xh, kv.xl, range(NF)).then_inc(s("k_psum").sem, 1)

                def keys_taken(b):
                    pe.wait_ge(*s("kh").at(b, NF))
                    pe.wait_ge(*s("kl").at(b, NF))

                def q_proj(b):
                    split_done(q, b)
                    project_features(pe, M, wh, wl, w_at(0), D, q.xh, q.xl, range(NF)).then_inc(s("q_psum").sem, 1)

                def queries_taken(b):
                    pe.wait_ge(*s("qh").at(b, NF))
                    pe.wait_ge(*s("ql").at(b, NF))

                def v_proj(b):
                    project_tokens(pe, M, wh, wl, w_at(2), kv.xh, kv.xl).then_inc(s("v_psum").sem, 1)

                def source_read(src, b):
                    pe.wait_ge(*src.sg("full").at(b, src.sg("full").per))

                def step(b, u, first, ahead):
                    if u == 0 and ahead and cross:
                        source_read(kv, b + 1)
                        q.pe_turn(pe, b + 1, M)
                    if u == 1 and not first:
                        if ahead:
                            source_read(q, b + 1)
                        else:
                            pe.wait_ge(*s("vx").at(b, 2))
                        turn_rcp(b - 1)
                    if ahead:
                        if u == 2:
                            if first:
                                source_read(q, b + 1)
                            else:
                                pe.wait_ge(*s("rt").at(b - 1, 1))
                            k_proj(b + 1)
                        if u == 3:
                            keys_taken(b + 1)
                            q_proj(b + 1)
                    if u == 5 and not first:
                        if ahead:
                            queries_taken(b + 1)
                        else:
                            pe.wait_ge(*s("rt").at(b - 1, 1))
                        out_proj(b - 1)
                    if u == 6 and ahead:
                        if first:
                            queries_taken(b + 1)
                        else:
                            pe.wait_ge(*s("fin_read").at(b - 1, 1))
                        v_proj(b + 1)
                    if u == 7 and ahead == 2:
                        pe.wait_ge(*s("vx").at(b + 1, 2))
                        kv.pe_turn(pe, b + 2, M)

                def body(b, par, first, ahead):
                    for u in range(U):
                        if u < U - 1:
                            scores(b, par, u + 1)
                        elif ahead:
                            scores(b + 1, 1 - par, 0)
                        step(b, u, first, ahead)
                        if u == 1 and not first:
                            pv(b - 1, 1 - par, 1)
                        if u == U // NF + 1:
                            pv(b, par, 0)
                        if u > 0:
                            turn_e(b, u - 1)
                        elif not first:
                            turn_e(b - 1, U - 1)

                if ready_at:
                    pe.wait_ge(ready.sem, ready_at)
                kv.pe_turn(pe, 0, M)
                k_proj(0)
                keys_taken(0)
                if cross:
                    q.pe_turn(pe, 0, M)
                q_proj(0)
                queries_taken(0)
                v_proj(0)
                scores(0, 0, 0)
                pe.wait_ge(*s("vx").at(0, 2))
                kv.pe_turn(pe, 1, M)
                for_sequences_ahead(pe, body)
                turn_e(B - 1, U - 1)
                pv(B - 1, 1, 1)
                pe.wait_ge(*s("fin_read").at(B - 2, 1))
                turn_rcp(B - 1)
                pe.wait_ge(*s("rt").at(B - 1, 1))
                out_proj(B - 1)

            @block.scalar
            def _(a):
                def exps(b, par, u, t):
                    a.wait_ge(*s("neg").at(b, NT * u + t + 1))
                    if t == 0:
                        if u >= 2:
                            a.wait_ge(*s("et_psum").at(b, 2 * (u - 1)))
                        elif u == 1:
                            a.wait_ge(*s("et_psum").at(b, 0))
                        elif not (isinstance(b, int) and b == 0):
                            a.wait_ge(*s("et_psum").at(b - 1, 2 * (U - 1)))
                    n = keys_of[t]
                    for h in range(2):
                        hd = 2 * u + h
                        a.activation(e[:, u % 2, t, h, 0:n], SC[u % 2][:, t, h, 0:n], ACT.Exp,
                                     bias=neg[:, u % 2, t, h:h + 1],
                                     accum_out=den[:, par, t, hd:hd + 1]).then_inc(s("exps").sem, 1)

                def copy_et(b, u):
                    a.wait_ge(*s("et_psum").at(b, 2 * u + 2))
                    if u == 0:
                        a.wait_ge(*s("pv").at(b, 0))
                    elif u == U // NF:
                        a.wait_ge(*s("pv").at(b, 1))
                    i = (2 * u) % G8 + 1
                    if mask == "causal":
                        a.activation(et[:, i, 0, :], ET[:, 1, 0, :], ACT.Copy).then_inc(s("et_a").sem, 1)
                        a.activation(et[:, i, 1, P:S], ET[:, 1, 1, P:S], ACT.Copy).then_inc(s("et_a").sem, 1)
                    else:
                        a.activation(et[:, i, :, :], ET[:, 1, :, :], ACT.Copy).then_inc(s("et_a").sem, 1)

                def copy_rt(b):
                    a.wait_ge(*s("rt_psum").at(b, 1))
                    a.wait_ge(*s("on").at(b, 0))
                    a.activation(rt[:, :, :], M, ACT.Copy).then_inc(s("rt").sem, 1)

                def hi_q(b):
                    a.wait_ge(*s("q_psum").at(b, 1))
                    for g_ in range(U // NF):
                        a.wait_ge(*s(f"qx{g_}").at(b, 0))
                    for f in range(NF):
                        dst = q2[:, f, 0, :]
                        a.activation(dst, M[:, f, :], ACT.Identity, bias=bq(f)).then_inc(s("qh").sem, 1)

                def hi_k(b):
                    a.wait_ge(*s("k_psum").at(b, 1))
                    a.wait_ge(*s("kx").at(b, 0))
                    for f in range(NF):
                        a.activation(k2[:, f, 0, :], M[:, f, :], ACT.Identity, bias=bk(f)).then_inc(s("kh").sem, 1)

                def body(b, par, first, ahead):
                    for u in range(U):
                        if u == 2 and not first:
                            copy_rt(b - 1)
                        if ahead:
                            if u == 0:
                                kv.act_hi(a, b + 1, M, kv_used)
                            if u == 1 and cross:
                                q.act_hi(a, b + 1, M, s("q_psum"))
                            if u == 3:
                                hi_k(b + 1)
                            if u == 4:
                                hi_q(b + 1)
                        exps(b, par, u, 0)
                        if u > 1:
                            copy_et(b, u - 2)
                        elif not first:
                            copy_et(b - 1, U + u - 2)
                        exps(b, par, u, 1)
                        if ahead == 2:
                            if u == 4:
                                kv.act_rstd(a, b + 2)
                            if u == 5 and cross:
                                q.act_rstd(a, b + 2)
                        if u == 7 and not first:
                            fin.act_rstd(a, b - 1)

                a.preload_act_table_set(EXP_LN)
                kv.act_rstd(a, 0)
                if cross:
                    q.act_rstd(a, 0)
                kv.act_hi(a, 0, M, kv_used)
                hi_k(0)
                if cross:
                    q.act_hi(a, 0, M, s("q_psum"))
                hi_q(0)
                kv.act_rstd(a, 1)
                if cross:
                    q.act_rstd(a, 1)
                for_sequences_ahead(a, body)
                copy_et(B - 1, U - 2)
                copy_et(B - 1, U - 1)
                copy_rt(B - 1)
                fin.act_rstd(a, B - 1)

            @block.vector
            def _(v):
                def maxes(b, u):
                    for t in range(NT):
                        v.wait_ge(*s("scores").at(b, NT * u + t + 1))
                        v.tensor_reduce(neg[:, u % 2, t, :], SC[u % 2][:, t, :, 0:keys_of[t]], AX.X, ALU.max,
                                        negate=True).then_inc(s("neg").sem, 1)

                def copy_et(b, u):
                    v.wait_ge(*s("et_psum").at(b, 2 * u + 1))
                    if u == 0:
                        v.wait_ge(*s("pv").at(b, 0))
                    elif u == U // NF:
                        v.wait_ge(*s("pv").at(b, 1))
                    i = (2 * u) % G8
                    if mask == "causal":
                        v.tensor_copy(et[:, i, 0, :], ET[:, 0, 0, :]).then_inc(s("et_v").sem, 1)
                        v.tensor_copy(et[:, i, 1, P:S], ET[:, 0, 1, P:S]).then_inc(s("et_v").sem, 1)
                    else:
                        v.tensor_copy(et[:, i, :, :], ET[:, 0, :, :]).then_inc(s("et_v").sem, 1)

                def recips(b, par):
                    v.wait_ge(*s("exps").at(b, NE_ * U))
                    v.wait_ge(*s("rcpx").at(b, 0))
                    v.reciprocal(rcp[:, :, :], den[:, par, :, :]).then_inc(s("rcp").sem, 1)
                    v.wait_ge(*s("rcp").at(b, 1))
                    v.wait_ge(*s("rt_psum").at(b, 0))
                    v.tensor_copy(rcpx[:, :, :, :].rearrange("p t h d -> p (t h) d"),
                                  rcp[:, :, :].rearrange("p t h -> p (t h)").unsqueeze(2).broadcast_to([P, NT * H, DH])
                                  ).then_inc(s("rcpx").sem, 1)

                def normalise(b):
                    v.wait_ge(*s("rt").at(b, 1))
                    v.wait_ge(*s("pv").at(b, NF))
                    v.wait_ge(*s("ol").at(b, 0))
                    v.tensor_tensor(on[:, :, :], O, rt[:, :, :], ALU.mult).then_inc(s("on").sem, 1)

                def split_out(b):
                    v.wait_ge(*s("on").at(b, 1))
                    v.wait_ge(*s("out_psum").at(b, 0))
                    v.tensor_copy(oh[:, :, :], on[:, :, :]).then_inc(s("oh").sem, 1)
                    v.wait_ge(*s("oh").at(b, 1))
                    v.tensor_tensor(ol[:, :, :], on[:, :, :], oh[:, :, :].bitcast(F32), ALU.subtract).then_inc(s("ol").sem, 1)

                def lo_q(b):
                    v.wait_ge(*s("qh").at(b, NF))
                    for g_ in range(U // NF):
                        v.wait_ge(*s(f"qx{g_}").at(b, 0))
                    for f in range(NF):
                        v.scalar_tensor_tensor(q2[:, f, 1, :], M[:, f, :], bq(f), q2[:, f, 0, :].bitcast(F32),
                                               ALU.add, ALU.subtract).then_inc(s("ql").sem, 1)

                def lo_k(b):
                    v.wait_ge(*s("kh").at(b, NF))
                    v.wait_ge(*s("kx").at(b, 0))
                    for f in range(NF):
                        v.scalar_tensor_tensor(k2[:, f, 1, :], M[:, f, :], bk(f), k2[:, f, 0, :].bitcast(F32),
                                               ALU.add, ALU.subtract).then_inc(s("kl").sem, 1)

                def spread_v(b, par):
                    v.wait_ge(*s("v_psum").at(b, 1))
                    src = M.rearrange("p t (g x d) -> p t g x d", x=2, d=DH)
                    bv = rows[:, 0, :].rearrange("p (g x d) -> p g x d", x=2, d=DH)
                    for x in range(2):
                        v.tensor_tensor(vx[par][:, :, :, x, x * DH:(x + 1) * DH], src[:, :, :, x, :],
                                        bv[:, :, x, :].unsqueeze(1).broadcast_to([P, NT, H // 2, DH]), ALU.add
                                        ).then_inc(s("vx").sem, 1)

                def convert_mask(b, par):
                    if mask in ("self", "keys"):
                        v.wait_ge(*s("mask_in").at(b, 16))
                        at = slice(0, P) if mask == "self" else slice(MROW, MROW + 1)
                        v.tensor_scalar(mb[par][at, :, :], mi[at, :, :], 0.0, MASKED, ALU.is_equal, ALU.mult
                                        ).then_inc(s("mask_b").sem, 1)

                def body(b, par, first, ahead):
                    for u in range(U):
                        if u < U - 1:
                            maxes(b, u + 1)
                        elif ahead:
                            maxes(b + 1, 0)
                        if not first:
                            if u == 0:
                                recips(b - 1, 1 - par)
                            if u == 2:
                                normalise(b - 1)
                            if u == 3:
                                split_out(b - 1)
                            if u == 5:
                                fin.dve_take(v, b - 1, M, s("out_psum"), 1)
                            if u == 6:
                                fin.dve_add(v, b - 1)
                            if u == 7:
                                fin.dve_norm(v, b - 1)
                        if u == 1 and ahead:
                            convert_mask(b + 1, 1 - par)
                        if u == 6 and ahead:
                            spread_v(b + 1, 1 - par)
                        if ahead == 2:
                            if u == 3:
                                kv.dve_stats(v, b + 2)
                            if u == 4 and cross:
                                q.dve_stats(v, b + 2)
                            if u == 5:
                                kv.dve_norm(v, b + 2)
                            if u == 7 and cross:
                                q.dve_norm(v, b + 2)
                        if u > 0:
                            copy_et(b, u - 1)
                        elif not first:
                            copy_et(b - 1, U - 1)
                        if ahead:
                            if u == 0:
                                kv.dve_lo(v, b + 1, M, kv_used)
                            if u == 1 and cross:
                                q.dve_lo(v, b + 1, M, s("q_psum"))
                            if u == 2:
                                lo_k(b + 1)
                            if u == 3:
                                lo_q(b + 1)

                def fixed_rows(x):
                    v.memset(x[MROW:P, :, :].bitcast(F32), 1.0 if mask == "keys" else 0.0).then_inc(kx_set.sem, 1)

                kv.dve_stats(v, 0)
                if cross:
                    q.dve_stats(v, 0)
                kv.dve_norm(v, 0)
                fixed_rows(qx[0])
                kv.dve_lo(v, 0, M, kv_used)
                fixed_rows(qx[1])
                if cross:
                    q.dve_norm(v, 0)
                lo_k(0)
                if cross:
                    q.dve_lo(v, 0, M, s("q_psum"))
                kv.dve_stats(v, 1)
                convert_mask(0, 0)
                lo_q(0)
                kv.dve_norm(v, 1)
                v.wait_ge(s("x_rest").sem, 16)
                v.wait_ge(vx_zero.sem, vx_zero.base + 2)
                if rows_at:
                    v.wait_ge(s("rows_in").sem, rows_at)
                spread_v(0, 0)
                if cross:
                    q.dve_stats(v, 1)
                maxes(0, 0)
                if cross:
                    q.dve_norm(v, 1)
                for_sequences_ahead(v, body)
                recips(B - 1, 1)
                copy_et(B - 1, U - 1)
                normalise(B - 1)
                split_out(B - 1)
                fin.dve_read(v, B - 1, M, s("out_psum"), 1)
                fin.dve_norm(v, B - 1)

        kx_set.base += KX_SET
        vx_zero.base += 2
        core.end()


def hidden_bank(core, j):
    return core.psum[:, j, :].rearrange("p (a n) -> p a n", a=2)


def feed_forward(core, name, src, hidden, b1, kind, bias, g, state, nxt, out=None):
    nc = core.nc
    with ExitStack() as ctx:
        core.phase = name
        sb = lambda n, s, t=F32: ctx.enter_context(nc.sbuf_tensor(f"{name}_{n}", s, t))
        wh, wl, rows = weights_of(core, name)
        q = Source(core, ctx, "q", kind, **src)
        fin = Finish(core, ctx, kind, rows, bias, g, state)
        HT = hidden // P
        NB = HT // 2
        relu = sb("relu", [P, HT, S]) if b1 else None
        hh = [sb(f"hid_hi{i}", [P, HT, S], F32R) for i in range(2)]
        hl = [sb(f"hid_lo{i}", [P, HT, S], F32R) for i in range(2)]
        core.begin(**q.per, **fin.per, hid_psum=NB, relu=HT if b1 else 0, hid_hi=NB, hid_lo=NB, out_psum=1)
        s = core.s
        M, O = bank(core, 7), bank(core, 6)
        ready_at, rows_at = core.s("w_split").base, core.s("rows_in").base

        with nc.Block() as block:
            if out is not None:
                @block.sync
                def _(sp):
                    def body(b, par, first, last):
                        sp.wait_ge(*s("fin_done").at(b, s("fin_done").per))
                        sp.dma_start(out[:, bass.ds(NT * b, NT), :], state[:, bass.ds(NT * b, NT), :]
                                     ).then_inc(s("stored").sem, 16)
                    for_sequences(sp, body)
                    sp.wait_ge(s("stored").sem, 16 * B)

            @block.gpsimd
            def _(pool):
                if nxt:
                    load_group(core, pool, nxt)
                fin.pool_add(pool)

            @block.tensor
            def _(pe):
                def turn_q(b):
                    pe.wait_ge(*q.sg("lo").at(b, 0))
                    q.pe_turn(pe, b, M)

                def hidden_of(b):
                    pe.wait_ge(*q.sg("lo").at(b, 1))
                    pe.wait_ge(*q.sg("hi").at(b, q.sg("hi").per))
                    for j in range(NB):
                        if b1:
                            pe.wait_ge(*s("relu").at(b, 0))
                        else:
                            pe.wait_ge(*s("hid_lo").at(b, 0))
                        project_features(pe, hidden_bank(core, j), wh, wl, 0, hidden, q.xh, q.xl,
                                         (2 * j, 2 * j + 1)).then_inc(s("hid_psum").sem, 1)

                def out_of(b, par):
                    pe.wait_ge(*s("hid_hi").at(b, NB))
                    pe.wait_ge(*s("hid_lo").at(b, NB))
                    pe.wait_ge(*s("fin_read").at(b, 0))
                    project_tokens(pe, O, wh, wl, NF * hidden, hh[par], hl[par], HT).then_inc(s("out_psum").sem, 1)

                def body(b, par, first, ahead):
                    if ahead:
                        hidden_of(b + 1)
                    if ahead == 2:
                        turn_q(b + 2)
                    out_of(b, par)

                pe.wait_ge(s("w_split").sem, ready_at)
                q.pe_turn(pe, 0, M)
                hidden_of(0)
                turn_q(1)
                for_sequences_ahead(pe, body)

            @block.scalar
            def _(a):
                def relus(b, par):
                    if b1:
                        a.wait_ge(*s("hid_lo").at(b, 0))
                    elif not (isinstance(b, int) and b < 2):
                        a.wait_ge(*s("out_psum").at(b - 1, 0))
                    for j in range(NB):
                        a.wait_ge(*s("hid_psum").at(b, j + 1))
                        if b1:
                            for f in (2 * j, 2 * j + 1):
                                a.activation(relu[:, f, :], hidden_bank(core, j)[:, f % 2, :], ACT.Relu,
                                             bias=core.col(b1, f)).then_inc(s("relu").sem, 1)
                        else:
                            a.activation(hh[par][:, 2 * j:2 * j + 2, :], hidden_bank(core, j), ACT.Relu
                                         ).then_inc(s("hid_hi").sem, 1)

                def body(b, par, first, ahead):
                    if ahead == 2:
                        q.act_rstd(a, b + 2)
                    if not first:
                        fin.act_read(a, b - 1, O, s("out_psum"), 1)
                        fin.act_rstd(a, b - 1)
                    if ahead:
                        relus(b + 1, 1 - par)
                    if ahead == 2:
                        q.act_hi(a, b + 2, M, s("hid_psum"))

                a.preload_act_table_set(EXP_LN)
                q.act_rstd(a, 0)
                q.act_hi(a, 0, M, s("hid_psum"))
                q.act_rstd(a, 1)
                relus(0, 0)
                q.act_hi(a, 1, M, s("hid_psum"))
                for_sequences_ahead(a, body)
                fin.act_read(a, B - 1, O, s("out_psum"), 1)
                fin.act_rstd(a, B - 1)

            @block.vector
            def _(v):
                def splits(b, par, tiles):
                    if b1 and not (isinstance(b, int) and b < 2):
                        v.wait_ge(*s("out_psum").at(b - 1, 0))
                    for j in tiles:
                        t = slice(2 * j, 2 * j + 2)
                        if b1:
                            v.wait_ge(*s("relu").at(b, 2 * (j + 1)))
                            v.tensor_copy(hh[par][:, t, :], relu[:, t, :]).then_inc(s("hid_hi").sem, 1)
                            v.wait_ge(*s("hid_hi").at(b, j + 1))
                            v.tensor_tensor(hl[par][:, t, :], relu[:, t, :], hh[par][:, t, :].bitcast(F32),
                                            ALU.subtract).then_inc(s("hid_lo").sem, 1)
                        else:
                            v.wait_ge(*s("hid_hi").at(b, j + 1))
                            v.scalar_tensor_tensor(hl[par][:, t, :], hidden_bank(core, j), 0.0,
                                                   hh[par][:, t, :].bitcast(F32), ALU.max, ALU.subtract
                                                   ).then_inc(s("hid_lo").sem, 1)

                def body(b, par, first, ahead):
                    if ahead == 2:
                        q.dve_stats(v, b + 2)
                    if not first:
                        fin.dve_read(v, b - 1, O, s("out_psum"), 1)
                    if ahead:
                        splits(b + 1, 1 - par, range(NB // 2))
                    if ahead == 2:
                        q.dve_norm(v, b + 2)
                    if ahead:
                        splits(b + 1, 1 - par, range(NB // 2, NB))
                    if ahead == 2:
                        q.dve_lo(v, b + 2, M, s("hid_psum"))
                    if not first:
                        fin.dve_norm(v, b - 1)

                q.dve_stats(v, 0)
                q.dve_norm(v, 0)
                q.dve_lo(v, 0, M, s("hid_psum"))
                q.dve_stats(v, 1)
                q.dve_norm(v, 1)
                if rows_at:
                    v.wait_ge(s("rows_in").sem, rows_at)
                splits(0, 0, range(NB))
                q.dve_lo(v, 1, M, s("hid_psum"))
                for_sequences_ahead(v, body)
                fin.dve_read(v, B - 1, O, s("out_psum"), 1)
                fin.dve_norm(v, B - 1)
        core.end()


LH = 8
LD = D // LH
LB = P + P // LD


def linear_attention(core, name, q_src, kv_src, g, state, nxt):
    nc = core.nc
    with ExitStack() as ctx:
        core.phase = name
        sb = lambda n, s, t=F32: ctx.enter_context(nc.sbuf_tensor(f"{name}_{n}", s, t))
        wh, wl, rows = weights_of(core, name)
        w_at = lambda m: m * NF * D
        q = Source(core, ctx, "q", "inner", **q_src)
        kv = Source(core, ctx, "kv", "inner", **kv_src) if kv_src else q
        cross = kv is not q
        fin = Finish(core, ctx, "inner", rows, None, g, state)
        ex = sb("ex", [P, NF, S])
        rl = sb("rl", [P, NF, S])
        exk = sb("exk", [P, NT, D])
        rlk = sb("rlk", [P, NT, D])
        qe = [sb(f"qe{i}", [P, NF, S]) for i in range(2)]
        ke = sb("ke", [P, NT, D])
        vo = sb("vo", [P, NT, NF, LB])
        bd = sb("bd", [P, NF, LB])
        z = sb("z", [P, NT, NF, LB - P])
        zr = sb("zr", [P, NT, NF, LB - P])
        ms = sb("ms", [P, NT, D])
        mh = sb("mh", [P, NF, S], F32R)
        ml = sb("ml", [P, NF, S], F32R)
        core.begin(**q.per, **(kv.per if cross else {}), **fin.per, q_psum=1, q_ex=1, q_rl=1, qe=1,
                   k_psum=1, k_ex=1, k_rl=1, ke=1, v_psum=1, vo=1, kv_psum=1, bd=1, msg_psum=1, z=1, zr=1,
                   ms=NT, mt_psum=1, mh=1, ml=1, out_psum=1)
        s = core.s
        M, QB, KB, VB, TM = (bank(core, i) for i in (7, 0, 1, 2, 6))
        KV = core.psum[:, 3, 0:NF * LB].rearrange("p (f c) -> p f c", f=NF)
        MS = core.psum[:, 4:6, 0:NF * LB].rearrange("p t (f c) -> p t f c", f=NF)
        ready_at, rows_at = s("w_split").base, s("rows_in").base
        ones = s("ones")

        with nc.Block() as block:
            @block.gpsimd
            def _(pool):
                if nxt:
                    load_group(core, pool, nxt)
                fin.pool_add(pool)

            @block.tensor
            def _(pe):
                def free(src, b):
                    pe.wait_ge(*src.sg("lo").at(b, 1))
                    pe.wait_ge(*src.sg("hi").at(b, 1))

                def q_proj(b):
                    free(q, b)
                    pe.wait_ge(*s("qe").at(b, 0))
                    project_features(pe, QB, wh, wl, w_at(0), D, q.xh, q.xl, range(NF)).then_inc(s("q_psum").sem, 1)

                def k_proj(b):
                    free(kv, b)
                    pe.wait_ge(*s("ke").at(b, 0))
                    project_tokens(pe, KB, wh, wl, w_at(1), kv.xh, kv.xl).then_inc(s("k_psum").sem, 1)

                def v_proj(b):
                    pe.wait_ge(*s("vo").at(b, 0))
                    project_tokens(pe, VB, wh, wl, w_at(2), kv.xh, kv.xl).then_inc(s("v_psum").sem, 1)

                def kv_product(b):
                    pe.wait_ge(*s("ke").at(b, 1))
                    pe.wait_ge(*s("vo").at(b, 1))
                    pe.wait_ge(*s("bd").at(b, 0))
                    for f in range(NF):
                        for t in range(NT):
                            m = pe.matmul(KV[:, f, :], ke[:, t, f * P:(f + 1) * P], vo[:, t, f, :],
                                          start=(t == 0), stop=(t == NT - 1))
                    m.then_inc(s("kv_psum").sem, 1)

                def message(b, par):
                    pe.wait_ge(*s("bd").at(b, 1))
                    pe.wait_ge(*s("qe").at(b, 1))
                    pe.wait_ge(*s("ms").at(b, 0))
                    for t in range(NT):
                        for f in range(NF):
                            m = pe.matmul(MS[:, t, f, :], qe[par][:, f, t * P:(t + 1) * P], bd[:, f, :],
                                          start=True, stop=True)
                    m.then_inc(s("msg_psum").sem, 1)

                def turn_message(b):
                    pe.wait_ge(*s("ms").at(b, NT))
                    pe.wait_ge(*s("fin_read").at(b, 0))
                    turn(pe, core, TM, ms).then_inc(s("mt_psum").sem, 1)

                def out_proj(b):
                    pe.wait_ge(*s("ml").at(b, 1))
                    project_tokens(pe, TM, wh, wl, w_at(3), mh, ml).then_inc(s("out_psum").sem, 1)

                def body(b, par, first, ahead):
                    kv_product(b)
                    if ahead:
                        q_proj(b + 1)
                    if ahead == 2 and cross:
                        free(kv, b + 1)
                        q.pe_turn(pe, b + 2, M)
                    message(b, par)
                    if ahead:
                        k_proj(b + 1)
                    turn_message(b)
                    if ahead:
                        v_proj(b + 1)
                    if ahead == 2:
                        free(q, b + 2 if cross else b + 1)
                        kv.pe_turn(pe, b + 2, M)
                    out_proj(b)

                pe.wait_ge(s("w_split").sem, ready_at)
                q.pe_turn(pe, 0, M)
                if cross:
                    free(q, 0)
                    kv.pe_turn(pe, 0, M)
                q_proj(0)
                if cross:
                    free(kv, 0)
                    q.pe_turn(pe, 1, M)
                k_proj(0)
                v_proj(0)
                free(q, 1 if cross else 0)
                kv.pe_turn(pe, 1, M)
                for_sequences_ahead(pe, body)

            @block.scalar
            def _(a):
                def used(src):
                    return s("v_psum") if src is kv else s("q_psum")

                def phi_parts(b, src, psum, ex_, rl_, n):
                    a.wait_ge(*s(f"{n}_psum").at(b, 1))
                    a.wait_ge(*s(f"{n}e").at(b, 0))
                    a.activation(ex_[:, :, :], psum, ACT.Exp).then_inc(s(f"{n}_ex").sem, 1)
                    a.activation(rl_[:, :, :], psum, ACT.Relu).then_inc(s(f"{n}_rl").sem, 1)

                def values(b):
                    a.wait_ge(*s("v_psum").at(b, 1))
                    a.wait_ge(*s("kv_psum").at(b, 0))
                    a.activation(vo[:, :, :, 0:P], VB.rearrange("p t (f c) -> p t f c", f=NF), ACT.Copy
                                 ).then_inc(s("vo").sem, 1)

                def message_hi(b):
                    a.wait_ge(*s("mt_psum").at(b, 1))
                    a.wait_ge(*s("out_psum").at(b, 0))
                    a.activation(mh[:, :, :], TM, ACT.Copy).then_inc(s("mh").sem, 1)

                def body(b, par, first, ahead):
                    if not first:
                        fin.act_read(a, b - 1, TM, s("out_psum"), 1)
                    if ahead:
                        phi_parts(b + 1, q, QB, ex, rl, "q")
                    if ahead == 2 and cross:
                        q.act_hi(a, b + 2, M, used(q))
                    if not first:
                        fin.act_rstd(a, b - 1)
                    if ahead:
                        phi_parts(b + 1, kv, KB, exk, rlk, "k")
                    message_hi(b)
                    if ahead:
                        values(b + 1)
                    if ahead == 2:
                        kv.act_hi(a, b + 2, M, used(kv))

                a.preload_act_table_set(EXP_LN)
                q.act_hi(a, 0, M, used(q))
                if cross:
                    kv.act_hi(a, 0, M, used(kv))
                phi_parts(0, q, QB, ex, rl, "q")
                if cross:
                    q.act_hi(a, 1, M, used(q))
                phi_parts(0, kv, KB, exk, rlk, "k")
                values(0)
                kv.act_hi(a, 1, M, used(kv))
                for_sequences_ahead(a, body)
                fin.act_read(a, B - 1, TM, s("out_psum"), 1)
                fin.act_rstd(a, B - 1)

            @block.vector
            def _(v):
                def used(src):
                    return s("v_psum") if src is kv else s("q_psum")

                def phi(b, out, ex_, rl_, n):
                    v.wait_ge(*s(f"{n}_rl").at(b, 1))
                    v.wait_ge(*s(f"{n}_ex").at(b, 1))
                    v.scalar_tensor_tensor(out[:, :, :], ex_[:, :, :], 1.0, rl_[:, :, :], ALU.min, ALU.add
                                           ).then_inc(s(f"{n}e").sem, 1)

                def phi_k(b):
                    v.wait_ge(*s("kv_psum").at(b, 0))
                    phi(b, ke, exk, rlk, "k")

                def block_diagonal(b):
                    v.wait_ge(*s("kv_psum").at(b, 1))
                    v.wait_ge(*s("msg_psum").at(b, 0))
                    v.tensor_tensor(bd[:, :, :], KV, core.blocks[:, :].unsqueeze(1).broadcast_to([P, NF, LB]), ALU.mult
                                    ).then_inc(s("bd").sem, 1)

                def message(b):
                    v.wait_ge(*s("msg_psum").at(b, 1))
                    v.wait_ge(*s("zr").at(b, 0))
                    v.tensor_scalar(z[:, :, :, :], MS[:, :, :, P:LB], 1e-6, None, ALU.add).then_inc(s("z").sem, 1)
                    v.wait_ge(*s("z").at(b, 1))
                    v.wait_ge(*s("ms").at(b, 0))
                    v.reciprocal(zr[:, :, :, :], z[:, :, :, :]).then_inc(s("zr").sem, 1)
                    v.wait_ge(*s("zr").at(b, 1))
                    v.wait_ge(*s("mt_psum").at(b, 0))
                    for t in range(NT):
                        v.tensor_tensor(ms[:, t, :].rearrange("p (f j d) -> p f j d", f=NF, d=LD),
                                        MS[:, t, :, 0:P].rearrange("p f (j d) -> p f j d", d=LD),
                                        zr[:, t, :, :].unsqueeze(3).broadcast_to([P, NF, P // LD, LD]), ALU.mult
                                        ).then_inc(s("ms").sem, 1)

                def message_lo(b):
                    v.wait_ge(*s("mh").at(b, 1))
                    v.tensor_tensor(ml[:, :, :], TM, mh[:, :, :].bitcast(F32), ALU.subtract).then_inc(s("ml").sem, 1)

                def body(b, par, first, ahead):
                    block_diagonal(b)
                    if not first:
                        fin.dve_read(v, b - 1, TM, s("out_psum"), 1)
                    if ahead == 2:
                        q.dve_stats(v, b + 2)
                    message(b)
                    if ahead == 2 and cross:
                        q.dve_lo(v, b + 2, M, used(q))
                        kv.dve_stats(v, b + 2)
                    if ahead:
                        phi(b + 1, qe[1 - par], ex, rl, "q")
                    message_lo(b)
                    if ahead:
                        phi_k(b + 1)
                    if ahead == 2:
                        kv.dve_lo(v, b + 2, M, used(kv))
                    if not first:
                        fin.dve_norm(v, b - 1)

                v.memset(vo[:, :, :, P:LB], 1.0).then_inc(ones.sem, 1)
                if rows_at:
                    v.wait_ge(s("rows_in").sem, rows_at)
                q.dve_stats(v, 0)
                if cross:
                    kv.dve_stats(v, 0)
                q.dve_lo(v, 0, M, used(q))
                if cross:
                    kv.dve_lo(v, 0, M, used(kv))
                q.dve_stats(v, 1)
                if cross:
                    kv.dve_stats(v, 1)
                phi(0, qe[0], ex, rl, "q")
                if cross:
                    q.dve_lo(v, 1, M, used(q))
                phi_k(0)
                kv.dve_lo(v, 1, M, used(kv))
                for_sequences_ahead(v, body)
                fin.dve_read(v, B - 1, TM, s("out_psum"), 1)
                fin.dve_norm(v, B - 1)
        ones.base += 1
        core.end()


def load_expert(core, pool, e, par):
    s, d = core.s, core.d
    n = GSIZE["E0"] // CHUNK
    col0 = GOFF["E0"] + e * GSIZE["E0"]
    wh, wl = core.wh[par], core.wl[par]

    def bring(c):
        pool.wait_ge(*s("xw_split").at(e, max(0, c - STAGES + 1)))
        pool.dma_start(core.stage[:, c % STAGES, :], d["weights"][:, bass.ds(col0 + c * CHUNK, CHUNK)]
                       ).then_inc(s(f"xw_raw{c % STAGES}").sem, 16)

    pool.dma_start(core.rows[par][:, 0:1, :],
                   d["rows"][bass.ds(ROFF["E0"] + e, 1), :].partition_broadcast(P)).then_inc(s("xw_row").sem, 16)
    for c in range(STAGES - 1):
        bring(c)
    for c in range(n):
        if c + STAGES - 1 < n:
            bring(c + STAGES - 1)
        pool.wait_ge(*s(f"xw_raw{c % STAGES}").at(e, 16 * (c // STAGES + 1)))
        st = core.stage[:, c % STAGES, :]
        a, z = c * CHUNK, (c + 1) * CHUNK
        pool.sem_inc(s("xw_seen").sem, 1)
        pool.tensor_copy(wh[:, a:z], st).then_inc(s("xw_hi").sem, 1)
        pool.wait_ge(*s("xw_hi").at(e, c + 1))
        pool.tensor_tensor(wl[:, a:z], st, wh[:, a:z].bitcast(F32), ALU.subtract).then_inc(s("xw_split").sem, 1)
    pool.wait_ge(*s("xw_row").at(e, 16))


def gates(core, ctx):
    nc = core.nc
    sb = lambda n, s, t=F32: ctx.enter_context(nc.sbuf_tensor(f"moe_{n}", s, t))
    xah = sb("xa_hi", [P, NF, B * S], F32R)
    xal = sb("xa_lo", [P, NF, B * S], F32R)
    gate = sb("gate", [P, B * NT, NE])
    with ExitStack() as inner:
        sb = lambda n, s, t=F32: inner.enter_context(nc.sbuf_tensor(f"moe_{n}", s, t))
        q = Source(core, inner, "q", "pre", ln=("L2_xattn_moe_ln_g", "L2_xattn_moe_ln_b"), state=core.X)
        rh = sb("router_hi", [P, NF, NE], F32R)
        rl = sb("router_lo", [P, NF, NE], F32R)
        T = B * NT
        lg = sb("lg", [P, T, NE])
        top = sb("top", [P, T, 8])
        idx = sb("idx", [P, T, 8], U32)
        idf = sb("idf", [P, T, 8])
        dif = sb("dif", [P, T, 1])
        e2 = sb("e2", [P, T, 1])
        dn = sb("dn", [P, T, 1])
        g1 = sb("g1", [P, T, 1])
        g2 = sb("g2", [P, T, 1])
        o1 = sb("o1", [P, T, NE])
        o2 = sb("o2", [P, T, NE])
        core.begin(**q.per, lg_psum=1, lg=1, xa_h=1, xa_l=1)
        s = core.s
        M, L = bank(core, 7), bank(core, 6)
        one = s("gate_step")
        base = one.base

        with nc.Block() as block:
            @block.gpsimd
            def _(pool):
                load_expert(core, pool, 0, 0)

            @block.tensor
            def _(pe):
                def body(b, par, first, last):
                    pe.wait_ge(*q.sg("lo").at(b, 1))
                    if not last:
                        q.pe_turn(pe, b + 1, M)
                    pe.wait_ge(*s("lg").at(b, 0))
                    for t in range(NT):
                        for k in range(NF):
                            m = three_pass(pe, L[:, t, 0:NE], q.xh[:, k, t * P:(t + 1) * P],
                                           q.xl[:, k, t * P:(t + 1) * P], rh[:, k, :], rl[:, k, :],
                                           k == 0, k == NF - 1)
                    m.then_inc(s("lg_psum").sem, 1)
                pe.wait_ge(one.sem, base + 2)
                q.pe_turn(pe, 0, M)
                for_sequences(pe, body)

            @block.scalar
            def _(a):
                def body(b, par, first, last):
                    q.act_hi(a, b, M, None)
                    if not last:
                        q.act_rstd(a, b + 1)
                    cols = bass.ds(b * S, S)
                    a.wait_ge(*q.sg("hi").at(b, 1))
                    a.wait_ge(*q.sg("lo").at(b, 1))
                    a.sem_inc(s("split_seen").sem, 1)
                    a.activation(xah[:, :, cols], q.xh[:, :, :].bitcast(F32), ACT.Copy).then_inc(s("xa_h").sem, 1)
                    a.activation(xal[:, :, cols], q.xl[:, :, :].bitcast(F32), ACT.Copy).then_inc(s("xa_l").sem, 1)
                a.preload_act_table_set(EXP_LN)
                q.act_rstd(a, 0)
                for_sequences(a, body)
                a.wait_ge(one.sem, base + 3)
                a.activation(e2[:, :, :], dif[:, :, :], ACT.Exp).then_inc(s("gate_exp").sem, 1)

            @block.vector
            def _(v):
                def logits(b):
                    v.wait_ge(*s("lg_psum").at(b, 1))
                    v.tensor_tensor(lg[:, bass.ds(NT * b, NT), :], L[:, :, 0:NE],
                                    core.router_b[:, :].unsqueeze(1).broadcast_to([P, NT, NE]), ALU.add
                                    ).then_inc(s("lg").sem, 1)

                def body(b, par, first, last):
                    v.wait_ge(*s("xa_h").at(b, 0))
                    v.wait_ge(*s("xa_l").at(b, 0))
                    q.dve_lo(v, b, M, s("lg_psum"))
                    if not last:
                        q.dve_stats(v, b + 1)
                    if not first:
                        logits(b - 1)
                    if not last:
                        q.dve_norm(v, b + 1)
                n = [base]

                def step(ins):
                    n[0] += 1
                    ins.then_inc(one.sem, 1)
                    v.wait_ge(one.sem, n[0])

                step(v.tensor_copy(rh[:, :, :], core.router_w[:, :, :]))
                step(v.tensor_tensor(rl[:, :, :], core.router_w[:, :, :], rh[:, :, :].bitcast(F32), ALU.subtract))
                q.dve_stats(v, 0)
                q.dve_norm(v, 0)
                for_sequences(v, body)
                logits(B - 1)
                v.wait_ge(*s("lg").at(B - 1, 1))
                for t in range(T):
                    v.max(top[:, t, :], lg[:, t, :]).then_inc(s("top").sem, 1)
                v.wait_ge(s("top").sem, s("top").base + T)
                for t in range(T):
                    v.max_index(idx[:, t, :], top[:, t, :], lg[:, t, :]).then_inc(s("top").sem, 1)
                step(v.tensor_tensor(dif[:, :, :], top[:, :, 1:2], top[:, :, 0:1], ALU.subtract))
                v.wait_ge(s("top").sem, s("top").base + 2 * T)
                step(v.tensor_copy(idf[:, :, :], idx[:, :, :]))
                v.wait_ge(s("gate_exp").sem, s("gate_exp").base + 1)
                step(v.tensor_scalar(dn[:, :, :], e2[:, :, :], 1.0, None, ALU.add))
                step(v.reciprocal(g1[:, :, :], dn[:, :, :]))
                step(v.tensor_tensor(g2[:, :, :], e2[:, :, :], g1[:, :, :], ALU.mult))
                ids = core.iota[:, :].unsqueeze(1).broadcast_to([P, T, NE])
                for o, g, j in ((o1, g1, 0), (o2, g2, 1)):
                    step(v.tensor_tensor(o[:, :, :], ids, idf[:, :, j:j + 1].broadcast_to([P, T, NE]), ALU.is_equal))
                    step(v.tensor_tensor(o[:, :, :], o[:, :, :], g[:, :, :].broadcast_to([P, T, NE]), ALU.mult))
                step(v.tensor_tensor(gate[:, :, :], o1[:, :, :], o2[:, :, :], ALU.add))
        one.base += 11
        s("top").base += 2 * T
        s("gate_exp").base += 1
        core.end()
    return xah, xal, gate


def experts(core, nxt):
    nc = core.nc
    s = core.s
    core.phase = "moe"
    with ExitStack() as ctx:
        for n, k in dict(xw_split=GSIZE["E0"] // CHUNK, xw_hi=GSIZE["E0"] // CHUNK, xw_row=16, b1e=1).items():
            s(n).begin(k)
        for i in range(STAGES):
            s(f"xw_raw{i}").begin(16 * GSIZE["E0"] // CHUNK // STAGES)
        xah, xal, gate = gates(core, ctx)
        sb = lambda n, s, t=F32: ctx.enter_context(nc.sbuf_tensor(f"moe_{n}", s, t))
        HT = FE // P
        NB = HT // 2
        act = sb("gelu", [P, HT, S])
        hh = [sb(f"hid_hi{i}", [P, HT, S], F32R) for i in range(2)]
        hl = [sb(f"hid_lo{i}", [P, HT, S], F32R) for i in range(2)]
        y = sb("y", [P, NT, D])
        b1e = sb("b1e", [P, HT])
        core.begin(hid_psum=NB, gelu=HT, hid_hi=NB, hid_lo=NB, out_psum=1, y=1, mixed=NT)
        O = bank(core, 6)

        with nc.Block() as block:
            @block.gpsimd
            def _(pool):
                def body(e, par, first, last):
                    if last:
                        pool.wait_ge(*s("mixed").at(B * (NE - 1), 0))
                        pool.wait_ge(*s("xw_split").at(NE - 1, GSIZE["E0"] // CHUNK))
                        load_group(core, pool, nxt)
                    else:
                        if not first:
                            pool.wait_ge(*s("mixed").at(B * e, 0))
                        load_expert(core, pool, e + 1, 1 - par)
                for_sequences(pool, body)

            @block.tensor
            def _(pe):
                def expert(e, ep, first_e, last_e):
                    def hidden_of(n, b, ep):
                        wh, wl = core.wh[ep], core.wl[ep]
                        pe.wait_ge(*s("gelu").at(n, 0))
                        for j in range(NB):
                            cols = bass.ds(b * S, S)
                            o = hidden_bank(core, j)
                            for i, f in enumerate((2 * j, 2 * j + 1)):
                                for k in range(NF):
                                    a = k * FE + f * P
                                    m = three_pass(pe, o[:, i, :], wh[:, a:a + P], wl[:, a:a + P],
                                                   xah[:, k, cols], xal[:, k, cols], k == 0, k == NF - 1)
                            m.then_inc(s("hid_psum").sem, 1)

                    def body(b, par, first, last):
                        n = B * e + b
                        if not last:
                            hidden_of(n + 1, b + 1, ep)
                        elif not last_e:
                            pe.wait_ge(*s("xw_split").at(e + 1, GSIZE["E0"] // CHUNK))
                            hidden_of(n + 1, 0, 1 - ep)
                        pe.wait_ge(*s("hid_lo").at(n, NB))
                        pe.wait_ge(*s("y").at(n, 0))
                        project_tokens(pe, O, core.wh[ep], core.wl[ep], NF * FE, hh[par], hl[par], HT
                                       ).then_inc(s("out_psum").sem, 1)

                    if first_e:
                        pe.wait_ge(*s("xw_split").at(0, GSIZE["E0"] // CHUNK))
                        hidden_of(0, 0, 0)
                    for_sequences(pe, body)
                for_sequences(pe, expert)

            @block.scalar
            def _(a):
                def expert(e, ep, first_e, last_e):
                    a.wait_ge(*s("gelu").at(B * e, 0))
                    a.sem_inc(s("bias_free").sem, 1)
                    a.activation(b1e[:, :], core.cols[:, bass.ds(COFF["experts"] + HT * e, HT)], ACT.Copy
                                 ).then_inc(s("b1e").sem, 1)
                    a.wait_ge(*s("b1e").at(e, 1))

                    def body(b, par, first, last):
                        n = B * e + b
                        a.wait_ge(*s("hid_lo").at(n, 0))
                        for j in range(NB):
                            a.wait_ge(*s("hid_psum").at(n, j + 1))
                            for f in (2 * j, 2 * j + 1):
                                a.activation(act[:, f, :], hidden_bank(core, j)[:, f % 2, :], ACT.Gelu,
                                             bias=b1e[:, f:f + 1]
                                             ).then_inc(s("gelu").sem, 1)
                    for_sequences(a, body)
                a.preload_act_table_set("gelu_and_others")
                for_sequences(a, expert)

            @block.vector
            def _(v):
                def expert(e, ep, first_e, last_e):
                    def splits(n, par):
                        for j in range(NB):
                            t = slice(2 * j, 2 * j + 2)
                            v.wait_ge(*s("gelu").at(n, 2 * (j + 1)))
                            v.tensor_copy(hh[par][:, t, :], act[:, t, :]).then_inc(s("hid_hi").sem, 1)
                            v.wait_ge(*s("hid_hi").at(n, j + 1))
                            v.tensor_tensor(hl[par][:, t, :], act[:, t, :], hh[par][:, t, :].bitcast(F32),
                                            ALU.subtract).then_inc(s("hid_lo").sem, 1)

                    def body(b, par, first, last):
                        n = B * e + b
                        if not (last and last_e):
                            splits(n + 1, 1 - par)
                        v.wait_ge(*s("out_psum").at(n, 1))
                        v.wait_ge(*s("mixed").at(n, 0))
                        v.tensor_tensor(y[:, :, :], O, core.rows[ep][:, 0:1, :].broadcast_to([P, NT, D]), ALU.add
                                        ).then_inc(s("y").sem, 1)
                        v.wait_ge(*s("y").at(n, 1))
                        for t in range(NT):
                            x = core.X[:, NT * b + t, :]
                            v.scalar_tensor_tensor(x, y[:, t, :], gate[:, NT * b + t, bass.ds(e, 1)], x,
                                                   ALU.mult, ALU.add).then_inc(s("mixed").sem, 1)

                    v.wait_ge(*s("xw_split").at(e, GSIZE["E0"] // CHUNK))
                    v.wait_ge(*s("xw_row").at(e, 16))
                    if first_e:
                        splits(0, 0)
                    for_sequences(v, body)
                for_sequences(v, expert)
        for n in core.begun:
            s(n).end(B * NE)
        for n in ["xw_split", "xw_hi", "xw_row", "b1e"] + [f"xw_raw{i}" for i in range(STAGES)]:
            s(n).end(NE)


def program(nc, d):
    with ExitStack() as ctx:
        core = Core(nc, ctx, d)
        s = core.s
        sb = lambda n, sh, t=F32: ctx.enter_context(nc.sbuf_tensor(n, sh, t))
        core.eps = sb("eps", [P, 1])
        core.blocks = sb("blocks", [P, LB])
        core.router_w = sb("router_w", [P, NF, NE])
        core.router_b = sb("router_b", [P, NE])
        core.iota = sb("iota", [P, NE])
        core.raw_sems = [s(f"w_raw{i}") for i in range(STAGES)]

        with nc.Block() as block:
            @block.sync
            def _(sp):
                n = 2 * NT
                for dst, src in ((core.X[:, 0:n, :], d["x"][:, 0:n, :]), (core.cols[:, :], d["cols"]), (core.ident[:, :], d["ident"]),
                                 (core.tri[:, :], d["tri"]), (core.blocks[:, :], d["blocks"]),
                                 (core.router_w[:, :, :], d["router_w"]),
                                 (core.router_b[:, :], d["router_b"].partition_broadcast(P)),
                                 (core.iota[:, :], d["iota"].partition_broadcast(P))):
                    sp.dma_start(dst, src).then_inc(s("first_loads").sem, 16)
                bring_first(core, sp, "L0s")
                sp.wait_ge(s("first_loads").sem, 8 * 16)
                sp.dma_start(core.X[:, n:, :], d["x"][:, n:, :]).then_inc(s("x_rest").sem, 16)

            @block.vector
            def _(v):
                v.memset(core.eps[:, :], EPS).then_inc(s("set_up").sem, 1)
                v.wait_ge(s("first_loads").sem, 8 * 16)
                v.tensor_copy(core.ident_bf[:, :], core.ident[:, :]).then_inc(s("set_up").sem, 1)
                v.tensor_copy(core.tri_bf[:, :], core.tri[:, :]).then_inc(s("set_up").sem, 1)
                for i, n in enumerate(BQS):
                    v.tensor_scalar(core.bq4[:, i, :], core.cols[:, COFF[n]:COFF[n] + NF], DH ** -0.5, None, ALU.mult
                                    ).then_inc(s("set_up").sem, 1)
                split_first(core, v, "L0s")

        bq = lambda i: (lambda f: core.bq4[:, i, f:f + 1])
        bk = lambda n: (lambda f: core.col(n, f))
        X = core.X
        attention(core, "L0s", dict(state=X), None, bq(0), bk("L0_xattn_sa_bk"), "post", 2, "self", "L0c")
        attention(core, "L0c", dict(state=X), dict(dram=d["ctx"]), bq(1), bk("L0_xattn_ca_bk"), "post", 2, "keys", "L0f")
        feed_forward(core, "L0f", dict(state=X), 1024, "L0_xattn_ffn_b1", "post", 0, 1, X, "L1e")
        with ExitStack() as l1:
            C = l1.enter_context(nc.sbuf_tensor("C", [P, B * NT, D], F32))
            with nc.Block() as block:
                @block.sync
                def _(sp):
                    sp.dma_start(C[:, :, :], d["ctx"]).then_inc(s("ctx_in").sem, 16)

                @block.vector
                def _(v):
                    v.wait_ge(s("ctx_in").sem, 16)
                    v.tensor_tensor(C[:, :, :], C[:, :, :], C[:, :, :], ALU.add).then_inc(s("set_up").sem, 1)
            linear_attention(core, "L1e", dict(state=C), None, 0, C, "L1ef")
            feed_forward(core, "L1ef", dict(state=C), 512, None, "inner", None, 0, C, "L1s")
            linear_attention(core, "L1s", dict(state=X), None, 0, X, "L1c")
            linear_attention(core, "L1c", dict(state=X), dict(state=C), 0, X, "L1df")
            feed_forward(core, "L1df", dict(state=X), 512, None, "inner", None, 0, X, "L2s")
        ln = lambda n: (n + "_g", n + "_b")
        attention(core, "L2s", dict(state=X, ln=ln("L2_xattn_sa_ln")), None, bq(2), bk("@L2_xattn_sa_in_b:1"),
                  "pre", 0, None, "L2c")
        attention(core, "L2c", dict(state=X, ln=ln("L2_xattn_ca_q_ln")),
                  dict(dram=d["ctx"], ln=ln("L2_xattn_ca_kv_ln")), bq(3), bk("@L2_xattn_ca_in_b:1"),
                  "pre", 0, None, None)
        experts(core, "L3s")
        attention(core, "L3s", dict(state=X, ln=ln("L3_xattn_ln1")), None, bq(4), bk("L3_xattn_mmha_wk_b"),
                  "pre", 0, "causal", "L3c")
        attention(core, "L3c", dict(state=X, ln=ln("L3_xattn_ln2")), dict(dram=d["ctx"]), bq(5),
                  bk("L3_xattn_mha_wk_b"), "pre", 0, None, "L3f")
        feed_forward(core, "L3f", dict(state=X, ln=ln("L3_xattn_ln3")), 1024, "L3_xattn_ffn_b1", "pre", 0, 0, X, None,
                     out=d["out"])


def token_tiles(a):
    return np.ascontiguousarray(a.reshape(B * NT, P, a.shape[-1]).transpose(1, 0, 2))


def operand(w):
    i, o = w.shape
    return w.reshape(i // P, P, o).transpose(1, 0, 2).reshape(P, -1)


def kernel(**inputs):
    import concourse.bacc as bacc
    from concourse.bass_utils import run_bass_kernel_spmd as launch

    a = {n: np.asarray(v) for n, v in inputs.items()}

    def vec(n):
        if n[0] == "@":
            n, j = n[1:].split(":")
            return a[n][int(j) * D:(int(j) + 1) * D]
        if n[0] == "#":
            n, j = n[1:].split(":")
            return a[n][int(j)]
        return a[n]

    w = []
    for x in ("sa", "ca"):
        w += [operand(a[f"L0_xattn_{x}_w{m}"].T) for m in "qkvo"]
    w += [operand(a["L0_xattn_ffn_w1"].T), operand(a["L0_xattn_ffn_w2"].T)]
    w += [operand(a[f"L1_xattn_e_w{m}"]) for m in "qkvm12"]
    for j in "01":
        w += [operand(a[f"L1_xattn_d_w{m}{j}"]) for m in "qkvm"]
    w += [operand(a["L1_xattn_d_w1"]), operand(a["L1_xattn_d_w2"])]
    for x in ("sa", "ca"):
        w += [operand(a[f"L2_xattn_{x}_in_w"][m * D:(m + 1) * D].T) for m in range(3)]
        w += [operand(a[f"L2_xattn_{x}_out_w"].T)]
    for e in range(NE):
        w += [operand(a["L2_xattn_e_fc1_w"][e].T), operand(a["L2_xattn_e_fc2_w"][e].T)]
    for x in ("mmha", "mha"):
        w += [operand(a[f"L3_xattn_{x}_w{m}"]) for m in "qkvo"]
    w += [operand(a["L3_xattn_ffn_w1"]), operand(a["L3_xattn_ffn_w2"])]

    cols = [vec(n).reshape(NF, P).T for n in COLS]
    cols += [a["L0_xattn_ffn_b1"].reshape(-1, P).T, a["L3_xattn_ffn_b1"].reshape(-1, P).T]
    cols += [a["L2_xattn_e_fc1_b"].reshape(-1, P).T]
    data = {
        "x": token_tiles(a["x"]), "ctx": token_tiles(a["ctx_1024"]),
        "mask_self": token_tiles(a["mask_Bx1xSxS2_if1"][:, 0]),
        "mask_keys": np.ascontiguousarray(a["mask_Bx1x1xS2_if1"].reshape(B, S)),
        "weights": np.ascontiguousarray(np.concatenate(w, axis=1)),
        "rows": np.stack([vec(n) for r in ROWS.values() for n in r]),
        "cols": np.ascontiguousarray(np.concatenate(cols, axis=1)),
        "router_w": np.ascontiguousarray(a["L2_xattn_router_w"].T.reshape(NF, P, NE).transpose(1, 0, 2)),
        "router_b": a["L2_xattn_router_b"],
        "ident": np.eye(P, dtype=np.float32),
        "tri": np.triu(np.full((P, P), MASKED, np.float32), 1),
        "blocks": np.ascontiguousarray(np.concatenate(
            [np.kron(np.eye(P // LD), np.ones((LD, LD))), np.kron(np.eye(P // LD), np.ones((LD, 1)))], axis=1
        ).astype(np.float32)),
        "iota": np.arange(NE, dtype=np.float32),
    }
    nc = bacc.Bacc("TRN2", target_bir_lowering=False, num_devices=1)
    d = {n: nc.dram_tensor(f"in_{n}", v.shape, mybir.dt.from_np(v.dtype), kind="ExternalInput").ap()
         for n, v in data.items()}
    d["out"] = nc.dram_tensor("out_0", (P, B * NT, D), F32, kind="ExternalOutput").ap()
    program(nc, d)
    r = launch(nc, [{f"in_{n}": v for n, v in data.items()}], core_ids=[0])
    got = r.results[0]["out_0"]
    return np.ascontiguousarray(got.transpose(1, 0, 2)).reshape(B, S, D)
```
